# Optimizing a Trainium2 kernel written in Bass

```python
import numpy as np
import jax
import jax.numpy as jnp

def _softmax(x, axis=-1):
    return jax.nn.softmax(x, axis=axis)

def _gelu(x):
    return jax.nn.gelu(x, approximate=True)

def _silu(x):
    return jax.nn.silu(x)

def _sigmoid(x):
    return jax.nn.sigmoid(x)

def _layernorm(x, axis=-1, eps=1e-05):
    m = jnp.mean(x, axis=axis, keepdims=True)
    v = jnp.var(x, axis=axis, keepdims=True)
    return (x - m) / jnp.sqrt(v + eps)

def _scatter_add(tgt, idx, src, axis=0):
    return tgt.at[idx].add(src)

def _segment_sum(src, seg, n):
    return jax.ops.segment_sum(src, seg, n)
kernel_name = 'mk_adj_resnorm_d2_adj_r2_568d5d'

def setup_inputs(seed: int=0):
    np.random.seed(seed)
    _w = jnp.asarray

    def _rec_inputs():
        import jax
        import jax.numpy as jnp
        _gk = jax.random.key(seed)
        x = -0.0005207 + 1.001 * jax.random.normal(jax.random.fold_in(_gk, 1), (4096, 128), jnp.float32)
        _w = (1.0 + jnp.arange(4096, dtype=jnp.float32)) ** (-0.5)
        _w = _w / _w.mean()
        _pij = jnp.clip(0.000976562 * _w[:, None] * _w[None, :], 0.0, 1.0)
        _a = jax.random.uniform(jax.random.fold_in(_gk, 2), (4096, 4096)) < _pij
        _a = jnp.logical_or(_a, jnp.eye(4096, dtype=bool))
        _af = _a.astype(jnp.float32)
        _af = _af * jax.random.uniform(jax.random.fold_in(_gk, 3), (4096, 4096), jnp.float32, 0.05, 1)
        adj = _af
        return (x, adj)
    x, adj = _rec_inputs()

    def _L0_gnn_setup():
        import jax, jax.numpy as jnp
        import numpy as np
        N = 4096
        D = 128
        L = 3

        def _cxin_conv(x, a, eps, W, b):
            ax = a @ x
            h = ax + (1.0 + eps[0]) * ax
            for i in range(L):
                h = jax.nn.relu(h @ W[i].T + b[i])
            return h
        key = jax.random.key(seed)
        ks = jax.random.split(key, 8)
        s = 1.0 / np.sqrt(D)
        return {'x1': jax.random.normal(ks[0], (N, D), jnp.float32), 'x2': jax.random.normal(ks[1], (N, D), jnp.float32), 'G1': jax.random.uniform(ks[2], (N, N), jnp.float32), 'G2': jax.random.uniform(ks[3], (N, N), jnp.float32), 'eps1': jnp.zeros((1,), jnp.float32), 'eps2': jnp.zeros((1,), jnp.float32), 'W1': jax.random.normal(ks[4], (L, D, D), jnp.float32) * s, 'b1': jnp.zeros((L, D), jnp.float32), 'W2': jax.random.normal(ks[5], (L, D, D), jnp.float32) * s, 'b2': jnp.zeros((L, D), jnp.float32), 'Wm': jax.random.normal(ks[6], (D, 2 * D), jnp.float32) * (1.0 / np.sqrt(2 * D)), 'bm': jnp.zeros((D,), jnp.float32)}
    _L0_gnn_all = _L0_gnn_setup()
    _L0_gnn_in = {k: v for k, v in _L0_gnn_all.items() if k in ('x2', 'eps1', 'eps2', 'W1', 'b1', 'W2', 'b2', 'Wm', 'bm')}
    del _L0_gnn_all

    def _L1_gnn_setup():
        import jax, jax.numpy as jnp
        import numpy as np
        N, H, HEADS = (2048, 128, 3)
        ALPHA = 0.2
        NEG_INF = -9000000000000000.0

        def _sign_adj(key, n, density):
            k1, k2 = jax.random.split(key)
            mask = jax.random.uniform(k1, (n, n)) < density
            sign = jnp.where(jax.random.uniform(k2, (n, n)) < 0.5, -1.0, 1.0)
            adj = jnp.where(mask, sign, 0.0).astype(jnp.float32)
            idx = jnp.arange(n)
            return adj.at[idx, idx].set(1.0)

        def _gru_cell(x, hstate, Wih, Whh, bih, bhh):
            gi = x @ Wih.T + bih
            gh = hstate @ Whh.T + bhh
            ir, iz, inn = jnp.split(gi, 3, axis=1)
            hr, hz, hn = jnp.split(gh, 3, axis=1)
            r = jax.nn.sigmoid(ir + hr)
            z = jax.nn.sigmoid(iz + hz)
            n = jnp.tanh(inn + r * hn)
            return (1.0 - z) * n + z * hstate

        def _gat_head(h, node_adj, edge_adj, W, a):
            hW = h @ W
            hp = (node_adj > 0).astype(hW.dtype) @ hW
            hm = (node_adj < 0).astype(hW.dtype) @ hW
            e_plus = jax.nn.leaky_relu(jnp.concatenate([hp, hm], axis=1) @ a, ALPHA)[:, 0]
            e_minus = jax.nn.leaky_relu(jnp.concatenate([hm, hp], axis=1) @ a, ALPHA)[:, 0]
            att = jnp.where(edge_adj > 0, e_plus[None, :], NEG_INF)
            att = jnp.where(edge_adj < 0, e_minus[None, :], att)
            att = jax.nn.softmax(att, axis=1)
            return att * edge_adj @ hW
        key = jax.random.key(seed)
        ks = jax.random.split(key, 16)
        std = 0.01
        gain = 1.414
        return {'h': jax.random.normal(ks[0], (N, H), jnp.float32), 'node_adj': _sign_adj(ks[1], N, 0.005), 'edge_adj': _sign_adj(ks[2], N, 0.005), 'gat_W': jax.random.normal(ks[3], (HEADS, H, H), jnp.float32) * (gain / np.sqrt(H, dtype=np.float32)), 'gat_a': jax.random.normal(ks[4], (HEADS, 2 * H, 1), jnp.float32) * 0.1, 'edge_Wih': jax.random.normal(ks[5], (3 * H, H), jnp.float32) * std, 'edge_Whh': jax.random.normal(ks[6], (3 * H, H), jnp.float32) * std, 'edge_bih': jnp.zeros((3 * H,), jnp.float32), 'edge_bhh': jnp.zeros((3 * H,), jnp.float32), 'node_Wih': jax.random.normal(ks[7], (3 * H, H), jnp.float32) * std, 'node_Whh': jax.random.normal(ks[8], (3 * H, H), jnp.float32) * std, 'node_bih': jnp.zeros((3 * H,), jnp.float32), 'node_bhh': jnp.zeros((3 * H,), jnp.float32)}
    _L1_gnn_all = _L1_gnn_setup()
    _L1_gnn_in = {k: v for k, v in _L1_gnn_all.items() if k in ('gat_W', 'gat_a', 'edge_Wih', 'edge_Whh', 'edge_bih', 'edge_bhh', 'node_Wih', 'node_Whh', 'node_bih', 'node_bhh')}
    del _L1_gnn_all
    return {'x': x, 'adj': adj, 'L0_gnn_x2': _L0_gnn_in['x2'], 'L0_gnn_eps1': _L0_gnn_in['eps1'], 'L0_gnn_eps2': _L0_gnn_in['eps2'], 'L0_gnn_W1': _L0_gnn_in['W1'], 'L0_gnn_b1': _L0_gnn_in['b1'], 'L0_gnn_W2': _L0_gnn_in['W2'], 'L0_gnn_b2': _L0_gnn_in['b2'], 'L0_gnn_Wm': _L0_gnn_in['Wm'], 'L0_gnn_bm': _L0_gnn_in['bm'], 'L1_gnn_gat_W': _L1_gnn_in['gat_W'], 'L1_gnn_gat_a': _L1_gnn_in['gat_a'], 'L1_gnn_edge_Wih': _L1_gnn_in['edge_Wih'], 'L1_gnn_edge_Whh': _L1_gnn_in['edge_Whh'], 'L1_gnn_edge_bih': _L1_gnn_in['edge_bih'], 'L1_gnn_edge_bhh': _L1_gnn_in['edge_bhh'], 'L1_gnn_node_Wih': _L1_gnn_in['node_Wih'], 'L1_gnn_node_Whh': _L1_gnn_in['node_Whh'], 'L1_gnn_node_bih': _L1_gnn_in['node_bih'], 'L1_gnn_node_bhh': _L1_gnn_in['node_bhh']}

def reference(x, adj, L0_gnn_x2, L0_gnn_eps1, L0_gnn_eps2, L0_gnn_W1, L0_gnn_b1, L0_gnn_W2, L0_gnn_b2, L0_gnn_Wm, L0_gnn_bm, L1_gnn_gat_W, L1_gnn_gat_a, L1_gnn_edge_Wih, L1_gnn_edge_Whh, L1_gnn_edge_bih, L1_gnn_edge_bhh, L1_gnn_node_Wih, L1_gnn_node_Whh, L1_gnn_node_bih, L1_gnn_node_bhh):
    import jax
    import jax.numpy as jnp

    def _L0_gnn_ref(x1, x2, G1, G2, eps1, eps2, W1, b1, W2, b2, Wm, bm):
        import jax, jax.numpy as jnp
        import numpy as np
        N = 4096
        D = 128
        L = 3

        def _cxin_conv(x, a, eps, W, b):
            ax = a @ x
            h = ax + (1.0 + eps[0]) * ax
            for i in range(L):
                h = jax.nn.relu(h @ W[i].T + b[i])
            return h
        out1 = _cxin_conv(x1, G1, eps1, W1, b1)
        out2 = _cxin_conv(x2, G2, eps2, W2, b2)
        merged = jnp.concatenate((out1, out2), axis=1)
        return merged @ Wm.T + bm

    def _L1_gnn_ref(h, node_adj, edge_adj, gat_W, gat_a, edge_Wih, edge_Whh, edge_bih, edge_bhh, node_Wih, node_Whh, node_bih, node_bhh):
        import jax, jax.numpy as jnp
        import numpy as np
        N, H, HEADS = (2048, 128, 3)
        ALPHA = 0.2
        NEG_INF = -9000000000000000.0

        def _sign_adj(key, n, density):
            k1, k2 = jax.random.split(key)
            mask = jax.random.uniform(k1, (n, n)) < density
            sign = jnp.where(jax.random.uniform(k2, (n, n)) < 0.5, -1.0, 1.0)
            adj = jnp.where(mask, sign, 0.0).astype(jnp.float32)
            idx = jnp.arange(n)
            return adj.at[idx, idx].set(1.0)

        def _gru_cell(x, hstate, Wih, Whh, bih, bhh):
            gi = x @ Wih.T + bih
            gh = hstate @ Whh.T + bhh
            ir, iz, inn = jnp.split(gi, 3, axis=1)
            hr, hz, hn = jnp.split(gh, 3, axis=1)
            r = jax.nn.sigmoid(ir + hr)
            z = jax.nn.sigmoid(iz + hz)
            n = jnp.tanh(inn + r * hn)
            return (1.0 - z) * n + z * hstate

        def _gat_head(h, node_adj, edge_adj, W, a):
            hW = h @ W
            hp = (node_adj > 0).astype(hW.dtype) @ hW
            hm = (node_adj < 0).astype(hW.dtype) @ hW
            e_plus = jax.nn.leaky_relu(jnp.concatenate([hp, hm], axis=1) @ a, ALPHA)[:, 0]
            e_minus = jax.nn.leaky_relu(jnp.concatenate([hm, hp], axis=1) @ a, ALPHA)[:, 0]
            att = jnp.where(edge_adj > 0, e_plus[None, :], NEG_INF)
            att = jnp.where(edge_adj < 0, e_minus[None, :], att)
            att = jax.nn.softmax(att, axis=1)
            return att * edge_adj @ hW
        dn = jnp.diag(node_adj)
        de = jnp.diag(edge_adj)
        idx = jnp.arange(node_adj.shape[0])
        node_adj_norm = node_adj.at[idx, idx].add(-dn)
        edge_adj_norm = edge_adj.at[idx, idx].add(-de)
        node_support = node_adj_norm @ h
        edge_output = _gru_cell(node_support, h, edge_Wih, edge_Whh, edge_bih, edge_bhh)
        edge_support = _gat_head(h, node_adj_norm, edge_adj_norm, gat_W[0], gat_a[0])
        for i in range(1, HEADS):
            edge_support = edge_support + _gat_head(h, node_adj_norm, edge_adj_norm, gat_W[i], gat_a[i])
        edge_support = edge_support / HEADS
        node_output = _gru_cell(edge_support, h, node_Wih, node_Whh, node_bih, node_bhh)
        return de[:, None] * edge_output + dn[:, None] * node_output
    x = _layernorm(x + _L0_gnn_ref(x, L0_gnn_x2, adj, adj, L0_gnn_eps1, L0_gnn_eps2, L0_gnn_W1, L0_gnn_b1, L0_gnn_W2, L0_gnn_b2, L0_gnn_Wm, L0_gnn_bm), axis=-1)
    x = _layernorm(x + _L1_gnn_ref(x, adj, adj, L1_gnn_gat_W, L1_gnn_gat_a, L1_gnn_edge_Wih, L1_gnn_edge_Whh, L1_gnn_edge_bih, L1_gnn_edge_bhh, L1_gnn_node_Wih, L1_gnn_node_Whh, L1_gnn_node_bih, L1_gnn_node_bhh), axis=-1)
    return x

_drawn_inputs = setup_inputs


def setup_inputs(seed=0):
    import zlib

    import numpy as np

    out = dict(_drawn_inputs(seed))
    spreads = {'L0_gnn_b1': (0.0, 0.1),
     'L0_gnn_b2': (0.0, 0.1),
     'L0_gnn_bm': (0.0, 0.1),
     'L1_gnn_edge_bih': (0.0, 0.427),
     'L1_gnn_edge_bhh': (0.0, 0.742),
     'L1_gnn_node_bih': (0.0, 0.406),
     'L1_gnn_node_bhh': (0.0, 0.634)}
    factors = {'L1_gnn_gat_W': 6.082,
     'L1_gnn_gat_a': 8.0,
     'L1_gnn_edge_Whh': 4.245,
     'L1_gnn_node_Wih': 6.095,
     'L1_gnn_node_Whh': 4.163}
    for name, (base, spread) in spreads.items():
        noise = np.random.default_rng([zlib.crc32(name.encode()), seed]).standard_normal(out[name].shape)
        drawn = base * np.exp(spread * noise) if base else spread * noise
        out[name] = jnp.asarray(drawn.astype(out[name].dtype))
    for name, factor in factors.items():
        out[name] = (out[name] * factor).astype(out[name].dtype)
    return out
```

```python
import numpy as np
import concourse.bass as bass
from concourse import mybir
from contextlib import ExitStack

F32 = mybir.dt.float32
BF16 = mybir.dt.bfloat16
U8 = mybir.dt.uint8
I32 = mybir.dt.int32
ALU = mybir.AluOpType
ACT = mybir.ActivationFunctionType
AX = mybir.AxisListType

P = 128
N = 4096
T = N // P
BW = 1024
NBLK = N // BW
CH = 512
NCH = N // CH
RB = BW // P
TD = T + RB * (NBLK - 1)
HEADS = 3
LAYERS = 3
EPS = 1e-5
G8 = 8
NG = T // G8
BIG = 2.0 ** 100
ESC = 2.0 ** -40
ALPHA = 0.2


def build(nc, a_tiles, xx, x_nat, diag, eps, w_t, w_b, wm_t, bm, gat_w, gat_wt, gat_a,
          gru_w, gru_b, out):
    h_dram = nc.dram_tensor("h_dram", (TD, P, P), F32, kind="Internal").ap()
    ht_dram = nc.dram_tensor("ht_dram", (P, N), F32, kind="Internal").ap()
    agg_dram = nc.dram_tensor("agg_dram", (NCH, 5, P, CH), F32, kind="Internal").ap()

    ctx = ExitStack()
    with ctx:
        def sb(name, shape, dt):
            return ctx.enter_context(nc.sbuf_tensor(name, shape, dt))

        def sem(name):
            return ctx.enter_context(nc.semaphore(name))

        codes = sb("codes", [P, NBLK * T, BW], U8)
        ring = sb("ring", [P, 4 * BW], F32)
        low = sb("low", [P, 4096], F32)
        high = sb("high", [P, 2, N], F32)
        wt_sb = sb("wt_sb", [P, 2 * LAYERS, P], F32)
        wb_sb = sb("wb_sb", [P, 2 * LAYERS], F32)
        wm_sb = sb("wm_sb", [P, 2, P], F32)
        bm_row = sb("bm_row", [1, P], F32)
        ones_row = sb("ones_row", [1, P], F32)
        gwt_sb = sb("gwt_sb", [P, HEADS, P], F32)
        ga_sb = sb("ga_sb", [P, HEADS, 2], F32)
        eps_sb = sb("eps_sb", [P, 2], F32)
        u_sb = sb("u_sb", [P, 2, HEADS], F32)
        ident = sb("ident", [P, P], F32)
        ident_bf = sb("ident_bf", [P, P], BF16)
        ident_u8 = sb("ident_u8", [P, P], U8)
        penalty = sb("penalty", [P, P], BF16)
        ones3 = sb("ones3", [P, P], BF16)
        zeros = sb("zeros", [P, CH], BF16)
        ones_col = sb("ones_col", [P, 1], F32)
        v_f, v_r = (high[:, 1, i * 6 * T:(i + 1) * 6 * T].rearrange("p (t c) -> p t c", c=6) for i in range(2))
        v3 = sb("v3", [P, 64, 3, 6], BF16)
        e_nat = sb("e_nat", [P, 64, 6], F32)
        e_sc = sb("e_sc", [P, 64, 6], F32)
        w_flat = wt_sb[:, :, :].rearrange("p l n -> p (l n)")
        e_tmp = w_flat[:, 0:RB * 18].rearrange("p (i a c) -> p i a c", i=RB, a=3)
        mv = sb("mv", [P, T, 2], F32)
        rstd = sb("rstd", [P, T], F32)
        bst = sb("bst", [P, 4, 6], F32)
        wmin = sb("wmin", [P, HEADS, 4], F32)
        negm = sb("negm", [P, HEADS, 4], F32)
        off_diag = w_flat[:, 512:768].bitcast(BF16).rearrange("p (g n) -> p g n", g=NG)
        neg_code = w_flat[:, 256:512].bitcast(U8).rearrange("p (s n) -> p s n", s=2)
        ones_u8 = sb("ones_u8", [P, P], U8)
        mparts = sb("mparts", [P, HEADS, 4, 3], BF16)
        flag_f = sb("flag_f", [P, 2], F32)
        flag = sb("flag", [1, 1], I32)
        d_sb = sb("d_sb", [P, T], F32)

        a_slot = [ring[:, s * BW:(s + 1) * BW] for s in range(4)]
        x_slot = [low[:, s * 1024:(s + 1) * 1024].rearrange("p (r n) -> p r n", r=4) for s in range(2)]
        sgn = low[:, 2048:3072].bitcast(BF16).rearrange("p (s n) -> p s n", s=2)
        neg_acc = low[:, 3072:3584].bitcast(BF16)
        hn = low[:, :].rearrange("p (t n) -> p t n", t=T)
        ht = high[:, 0, :]
        p_slot = [ring[:, s * 2048:(s + 1) * 2048].bitcast(BF16).rearrange("p (r n) -> p r n", r=4) for s in range(2)]
        m_slot = [high[:, 1, s * 2048:(s + 1) * 2048].bitcast(BF16).rearrange("p (r n) -> p r n", r=4) for s in range(2)]
        a2_slot = [ring[:, s * 1024:(s + 1) * 1024].rearrange("p (r n) -> p r n", r=2) for s in range(4)]
        h_slot = [low[:, s * 512:(s + 1) * 512].rearrange("p (r n) -> p r n", r=4) for s in range(2)]
        rb = [low[:, 1024 + s * 256:1024 + (s + 1) * 256].bitcast(BF16) for s in range(4)]
        stage = [low[:, 2048 + s * CH:2048 + (s + 1) * CH] for s in range(4)] + [high[:, 1, 3584:4096]]
        ebuf = [high[:, 0, s * CH:(s + 1) * CH] for s in range(6)]
        macc = [high[:, 0, 3072:3584], high[:, 0, 3584:4096], high[:, 1, 0:512]]
        wbuf = [high[:, 1, 512 + s * CH:512 + (s + 1) * CH] for s in range(3)]
        mrow = [high[:, 1, 2048 + s * 768:2048 + (s + 1) * 768].bitcast(BF16).rearrange("p (h n) -> p h n", h=HEADS) for s in range(2)]
        fcodes = codes[:, :, :].rearrange("p t n -> p (t n)").bitcast(F32)
        at = [0]

        def last(n):
            at[0] += n
            return fcodes[:, at[0] - n:at[0]]
        gw_sb = last(12 * P).rearrange("p (g n) -> p g n", g=12)
        pw_sb = last(HEADS * P).rearrange("p (h n) -> p h n", h=HEADS)
        gb_sb = last(12)
        at[0] += 4
        f_num = [last(3 * CH).rearrange("p (h n) -> p h n", h=3) for _ in range(2)]
        f_den = [last(3 * CH).rearrange("p (h n) -> p h n", h=3) for _ in range(2)]
        f_node = [last(CH) for _ in range(2)]
        f_ht = [last(CH) for _ in range(2)]
        f_hn = [last(CH).rearrange("p (t n) -> p t n", t=4) for _ in range(2)]
        f_es = [last(CH) for _ in range(2)]
        f_r, f_z, f_t, f_n = ([last(CH) for _ in range(2)] for _ in range(4))
        f_o = [[last(CH) for _ in range(2)] for _ in range(2)]
        fin = last(N).rearrange("p (t n) -> p t n", t=T)
        assert at[0] <= NBLK * T * BW // 4

        bank = [ctx.enter_context(nc.psum_tensor(f"bank{i}", [P, CH], F32)) for i in range(8)]
        agg_ps = [[[bank[4 * par + 2 * b + u] for u in range(2)] for b in range(2)] for par in range(2)]
        num_ps, node_ps, den_ps, lg_ps, tr_ps = bank[0:3], bank[3], bank[4], bank[5:7], bank[5:8]

        w_in = sem("w_in")
        consts = sem("consts")
        zero_ok = sem("zero_ok")
        scale_ok = sem("scale_ok")
        a_in = [sem(f"a_in{s}") for s in range(4)]
        x_in = [sem(f"x_in{s}") for s in range(2)]
        a_used_pe = sem("a_used_pe")
        a_signed = sem("a_signed")
        neg_step = sem("neg_step")
        ones_ok = sem("ones_ok")
        agg_out = sem("agg_out")
        flag_max = sem("flag_max")
        flag_all = sem("flag_all")
        flag_ok = sem("flag_ok")
        mlp_mm = sem("mlp_mm")
        mlp_act = sem("mlp_act")
        xn_in = sem("xn_in")
        mg_mm = sem("mg_mm")
        res_ok = sem("res_ok")
        var_ok = sem("var_ok")
        std_ok = sem("std_ok")
        ln_ok = sem("ln_ok")
        chain = sem("chain")
        h_out = sem("h_out")
        ht_mm = sem("ht_mm")
        ht_ok = sem("ht_ok")
        ht_out = sem("ht_out")
        u_mm = sem("u_mm")
        u_ok = sem("u_ok")
        v_mm = sem("v_mm")
        v_ok = sem("v_ok")

        def attention_sems(tag):
            names = ["p_ready", "p_used", "e_ready", "e_ps_free", "a2_masked", 
                     "max_step", "rn_step", "macc_tr", "min_ok", "parts_ok", "parts_tr", "mrow_ok", "rb_ready",
                     "lg_ready", "exp_ok", "w_ready", "w_used", "e_used", "evac_act",
                     "evac_dve", "chain2", "stage_out"]
            s = {n: sem(f"{n}_{tag}") for n in names}
            s["a2_in"] = [sem(f"a2_in{i}_{tag}") for i in range(4)]
            s["h_in"] = [sem(f"h_in{i}_{tag}") for i in range(2)]
            return type("Sems", (), s)
        S = {1: attention_sems("pos"), 2: attention_sems("any")}

        fw_in = sem("fw_in")
        bias_ok = sem("bias_ok")
        f_in = [sem(f"f_in{i}") for i in range(2)]
        f_scaled = sem("f_scaled")
        f_slot_free = sem("f_slot_free")
        f_mm = sem("f_mm")
        f_act = sem("f_act")
        f_dve = sem("f_dve")
        f_std = sem("f_std")
        out_ready = sem("out_ready")
        stored = sem("stored")

        def last_mm(c, what):
            return 4 * c + {"edge": 1, "es": 2, "node": 3, "tr": 4}[what]

        PER_DVE = 3 + 10 + 1 + 4

        def last_dve(c, i, what="out"):
            base = c * PER_DVE + 3 + 5 * i
            return base + {"pre": 2, "out": 5}[what]

        def last_act(c, what):
            return 7 * c + {"r0": 1, "z0": 2, "n0": 3, "es": 4, "r1": 5, "z1": 6, "n1": 7}[what]

        block = ctx.enter_context(nc.Block())

        @block.sync
        def _(sp):
            with sp.Fori(0, NBLK) as C:
                with sp.Fori(0, NG) as g:
                    for k in range(G8):
                        tile = sp.snap(C * T + (g * G8 + k))
                        if k % 4 == 0:
                            x_tile = sp.snap(C * RB + (g * G8 + k))
                            sp.wait_ge(a_used_pe, C * T + g * G8 + (k + 4))
                            sp.dma_start(x_slot[k // 4], xx[bass.ds(x_tile, 4), :, :].rearrange("r p n -> p r n")).then_inc(x_in[k // 4], 16)
                        used = sp.snap(tile + 5)
                        sp.wait_ge(a_used_pe, used)
                        sp.wait_ge(a_signed, used)
                        sp.dma_start(a_slot[k % 4], a_tiles[bass.ds(tile, 1), :, :].rearrange("r p n -> p (r n)")).then_inc(a_in[k % 4], 16)
            sp.wait_ge(a_used_pe, NBLK * T + 8)
            sp.wait_ge(flag_max, 1)
            sp.dma_start(hn, x_nat.rearrange("(t p) n -> p t n", p=P)).then_inc(xn_in, 16)
            for q in range(NCH):
                sp.wait_ge(ln_ok, 4 * (q + 1))
                for t0 in (4 * q, 4 * q + T):
                    if t0 < TD:
                        sp.dma_start(h_dram[t0:t0 + 4].rearrange("r p n -> p r n"), hn[:, 4 * q:4 * q + 4, :]).then_inc(h_out, 16)
            for q in range(NCH):
                sp.wait_ge(ht_ok, q + 1)
                sp.dma_start(ht_dram[:, q * CH:(q + 1) * CH], ht[:, q * CH:(q + 1) * CH]).then_inc(ht_out, 16)
            sp.wait_ge(h_out, 16 * (NCH + (TD - T) // 4))
            sp.wait_ge(ht_out, 16 * NCH)
            sp.wait_ge(flag_ok, 1)
            has_neg = sp.value_load(flag[0:1, 0:1], min_val=0, max_val=1)

            def attention_loads(s, NS):
                sp.wait_ge(s.p_used, 2 + NBLK * T // 4)
                with sp.Fori(0, NBLK) as C:
                    for u in range(2):
                        with sp.Fori(0, NG) as g:
                            body = (C * 2 + u) * NG + g
                            for k in range(0, G8, 2):
                                tile = sp.snap(C * T + (g * G8 + k))
                                if k % 4 == 0:
                                    h_tile = sp.snap(C * RB + (g * G8 + k))
                                    sp.wait_ge(s.w_used, (body * 2 + (k // 4 + 1)) * (4 * NS * HEADS) + 3)
                                    sp.dma_start(h_slot[k // 4], h_dram[bass.ds(h_tile, 4), :, :].rearrange("r p n -> p r n")).then_inc(s.h_in[k // 4], 16)
                                sp.wait_ge(s.w_used, (body * G8 + (k + 2)) * (NS * HEADS) + 3)
                                sp.dma_start(a2_slot[k // 2], a_tiles[bass.ds(tile, 2), :, u * CH:(u + 1) * CH].rearrange("r p n -> p r n")).then_inc(s.a2_in[k // 2], 16)
            with sp.If(has_neg != 0):
                attention_loads(S[2], 2)
            with sp.Else():
                attention_loads(S[1], 1)

            sp.wait_ge(f_scaled, 1)
            sp.dma_start(gw_sb, gru_w.rearrange("g p n -> p g n")).then_inc(fw_in, 16)
            sp.dma_start(pw_sb, gat_w.rearrange("h p n -> p h n")).then_inc(fw_in, 16)
            sp.dma_start(gb_sb, gru_b).then_inc(fw_in, 16)
            for c in range(NCH):
                s = c % 2
                if c >= 2:
                    sp.wait_ge(f_slot_free, c - 1)
                sp.dma_start(f_num[s], agg_dram[c, 0:3].rearrange("h p n -> p h n")).then_inc(f_in[s], 16)
                sp.dma_start(f_node[s], agg_dram[c, 3]).then_inc(f_in[s], 16)
                for h in range(HEADS):
                    sp.dma_start(f_den[s][:, h, :], agg_dram[c, 4, 32 * h:32 * h + 1, :].broadcast_to([P, CH])).then_inc(f_in[s], 16)
                sp.dma_start(f_ht[s], ht_dram[:, c * CH:(c + 1) * CH]).then_inc(f_in[s], 16)
                sp.dma_start(f_hn[s], h_dram[4 * c:4 * c + 4].rearrange("r p n -> p r n")).then_inc(f_in[s], 16)
            out_v = out.rearrange("(t p) n -> p t n", p=P)
            for q in range(NCH):
                sp.wait_ge(out_ready, 4 * (q + 1))
                sp.dma_start(out_v[:, 4 * q:4 * q + 4, :], fin[:, 4 * q:4 * q + 4, :]).then_inc(stored, 16)
            sp.wait_ge(stored, 16 * NCH)

        @block.gpsimd
        def _(pool):
            nc.gpsimd.memset(ident[:, :], 0.0).then_inc(zero_ok, 1)
            nc.gpsimd.memset(ones3[:, :], 1.0).then_inc(zero_ok, 1)
            nc.gpsimd.memset(zeros[:, :], 0.0).then_inc(consts, 1)
            nc.gpsimd.memset(ones_col[:, :], 1.0).then_inc(consts, 1)
            nc.gpsimd.memset(ones_row[:, :], 1.0).then_inc(consts, 1)
            pool.wait_ge(zero_ok, 2)
            nc.gpsimd.affine_select(out=ident[:, :], in_=ident[:, :], compare_op=ALU.not_equal, fill=1.0,
                                    base=0, pattern=[[-1, P]], channel_multiplier=1).then_inc(zero_ok, 1)
            nc.gpsimd.affine_select(out=ones3[:, :], in_=ones3[:, :], compare_op=ALU.is_ge, fill=0.0,
                                    base=2, pattern=[[0, P]], channel_multiplier=-1).then_inc(consts, 1)
            pool.wait_ge(zero_ok, 3)
            nc.gpsimd.tensor_copy(ident_bf[:, :], ident[:, :]).then_inc(consts, 1)
            nc.gpsimd.tensor_copy(ident_u8[:, :], ident[:, :]).then_inc(consts, 1)
            nc.gpsimd.tensor_scalar(penalty[:, :], ident[:, :], -BIG, None, ALU.mult).then_inc(consts, 1)
            pool.wait_ge(flag_max, 1)
            nc.gpsimd.partition_all_reduce(flag_f[:, 1:2], flag_f[:, 0:1], P, bass.bass_isa.ReduceOp.max).then_inc(flag_all, 1)
        CONSTS = 7

        @block.scalar
        def _(act):
            act.dma_start(wt_sb[:, :, :], w_t.rearrange("l p n -> p l n")).then_inc(w_in, 16)
            act.dma_start(wb_sb[:, :], w_b).then_inc(w_in, 16)
            act.dma_start(wm_sb[:, :, :], wm_t.rearrange("(b p) n -> p b n", p=P)).then_inc(w_in, 16)
            act.dma_start(bm_row[:, :], bm.rearrange("(o n) -> o n", o=1)).then_inc(w_in, 16)
            act.dma_start(gwt_sb[:, :, :], gat_wt.rearrange("h p n -> p h n")).then_inc(w_in, 16)
            act.dma_start(ga_sb[:, :, :], gat_a).then_inc(w_in, 16)
            act.dma_start(d_sb[:, :], diag).then_inc(w_in, 16)
            act.dma_start(eps_sb[:, :], eps.rearrange("(o n) -> o n", o=1).broadcast_to([P, 2])).then_inc(w_in, 16)
            act.sem_inc(a_signed, 8)
            act.sem_inc(agg_out, 8)
            act.wait_ge(scale_ok, 1)
            with act.Fori(0, NBLK // 2) as Cp:
                for par in range(2):
                    with act.Fori(0, NG) as g:
                        for k in range(G8):
                            act.wait_ge(a_in[k % 4], ((Cp * 2 + par) * 8 + g * 2 + (k // 4 + 1)) * 16)
                            act.wait_ge(neg_step, (Cp * 2 + par) * T + g * G8 + (k + 2))
                            nc.scalar.activation(sgn[:, k % 2, :], a_slot[k % 4], ACT.Sign, scale=-1.0).then_inc(a_signed, 1)
                    act.wait_ge(a_used_pe, (Cp * 2 + par + 1) * T + 8)
                    for b in range(2):
                        for u in range(2):
                            nc.scalar.activation(high[:, b, bass.ds((Cp * 2 + par) * BW + u * CH, CH)], agg_ps[par][b][u][:, :],
                                                 ACT.Copy, scale=eps_sb[:, b:b + 1]).then_inc(agg_out, 1)
            for m in range(LAYERS * 16):
                layer, c, b = m // 16, m % 16 // 2, m % 2
                act.wait_ge(mlp_mm, m + 1)
                nc.scalar.activation(high[:, b, c * CH:(c + 1) * CH], bank[m % 8][:, :], ACT.Relu,
                                     bias=wb_sb[:, b * LAYERS + layer:b * LAYERS + layer + 1]).then_inc(mlp_act, 1)
            act.wait_ge(var_ok, 1)
            nc.scalar.activation(rstd[:, :], rstd[:, :], ACT.Sqrt).then_inc(std_ok, 1)
            for q in range(NCH):
                act.wait_ge(ht_mm, q + 1)
                nc.scalar.activation(ht[:, q * CH:(q + 1) * CH], bank[q][:, :], ACT.Copy).then_inc(ht_ok, 1)
            act.wait_ge(flag_ok, 1)
            has_neg = act.value_load(flag[0:1, 0:1], min_val=0, max_val=1)

            def attention(s, NS):
                NU = NS * HEADS
                act.sem_inc(s.exp_ok, 2)
                act.sem_inc(s.evac_act, 3)
                act.sem_inc(s.stage_out, 48)
                act.wait_ge(h_out, 16 * (NCH + (TD - T) // 4))
                act.wait_ge(ht_out, 16 * NCH)
                with act.Fori(0, NBLK) as C:
                    for u in range(2):
                        cc = C * 2 + u
                        for h in range(HEADS):
                            act.wait_ge(s.parts_tr, cc * HEADS + (h + 1))
                            nc.scalar.activation(mrow[u][0:3, h, :], tr_ps[h][0:3, 0:CH // 2].bitcast(BF16), ACT.Copy).then_inc(s.mrow_ok, 1)
                        with act.Fori(0, NG) as g:
                            tile0 = (cc * NG + g) * G8

                            def codes_to_bf16(k):
                                act.wait_ge(s.lg_ready, (tile0 + (k + 1)) * NU)
                                nc.scalar.activation(rb[k % 4], codes[:, bass.ds(C * T + g * G8 + k, 1), u * CH:(u + 1) * CH].rearrange("p r n -> p (r n)"),
                                                     ACT.Copy).then_inc(s.rb_ready, 1)
                            if NS == 1:
                                codes_to_bf16(0)
                                codes_to_bf16(1)
                            for k in range(G8):
                                for n in range(k * NU, (k + 1) * NU):
                                    v = n % NU
                                    act.wait_ge(s.lg_ready, tile0 * NU + (n + 1 + 4 * NU))
                                    act.wait_ge(s.e_used, tile0 * NU + (n + 1))
                                    nc.scalar.activation(ebuf[n % 6], lg_ps[n % 2][:, :], ACT.Exp,
                                                         bias=e_nat[:, bass.ds(C * RB + g * G8 + k, 1), v:v + 1].rearrange("p a b -> p (a b)")).then_inc(s.exp_ok, 1)
                                if NS == 1 and k + 2 < G8:
                                    codes_to_bf16(k + 2)
                        act.wait_ge(s.e_used, (cc + 1) * (T * NU) + 6)
                        act.wait_ge(s.stage_out, cc * 48 + 48)
                        for h in range(HEADS):
                            nc.scalar.activation(stage[h], num_ps[h][:, :], ACT.Copy).then_inc(s.evac_act, 1)
                        act.wait_ge(s.evac_act, cc * 3 + 6)
                        act.dma_start(agg_dram[bass.ds(cc, 1), 0:3].rearrange("o h p n -> p (o h) n"),
                                      low[:, 2048:2048 + 3 * CH].rearrange("p (h n) -> p h n", h=3)).then_inc(s.stage_out, 16)
                        act.wait_ge(s.evac_dve, cc * 2 + 4)
                        act.dma_start(agg_dram[bass.ds(cc, 1), 3:4].rearrange("o h p n -> p (o h n)"), stage[3]).then_inc(s.stage_out, 16)
                        act.dma_start(agg_dram[bass.ds(cc, 1), 4:5].rearrange("o h p n -> p (o h n)"), stage[4]).then_inc(s.stage_out, 16)
                act.wait_ge(s.stage_out, NCH * 48 + 48)
                act.wait_ge(s.max_step, (NCH + 1) * (HEADS + T * NU))
            with act.If(has_neg != 0):
                attention(S[2], 2)
            with act.Else():
                attention(S[1], 1)
            act.sem_inc(f_scaled, 1)

            act.wait_ge(bias_ok, 2)
            for c in range(NCH):
                s = c % 2
                for i in range(2):
                    bk = bank[4 * i:4 * i + 4]
                    if i == 1:
                        act.wait_ge(f_mm, last_mm(c, "es"))
                        if c >= 2:
                            act.wait_ge(f_mm, last_mm(c - 2, "node"))
                        nc.scalar.activation(f_es[s], bank[0][:, :], ACT.Copy, scale=1.0 / HEADS).then_inc(f_act, 1)
                    act.wait_ge(f_mm, last_mm(c, "edge" if i == 0 else "node"))
                    if c:
                        act.wait_ge(f_dve, last_dve(c - 1, i))
                    nc.scalar.activation(f_r[i], bk[0][:, :], ACT.Sigmoid, bias=gb_sb[:, 6 * i:6 * i + 1]).then_inc(f_act, 1)
                    nc.scalar.activation(f_z[i], bk[1][:, :], ACT.Sigmoid, bias=gb_sb[:, 6 * i + 1:6 * i + 2]).then_inc(f_act, 1)
                    act.wait_ge(f_dve, last_dve(c, i, "pre"))
                    nc.scalar.activation(f_n[i], f_t[i], ACT.Tanh, bias=gb_sb[:, 6 * i + 2:6 * i + 3]).then_inc(f_act, 1)
            act.wait_ge(var_ok, 2)
            nc.scalar.activation(rstd[:, :], rstd[:, :], ACT.Sqrt).then_inc(f_std, 1)

        @block.tensor
        def _(pe):
            pe.sem_inc(a_used_pe, 8)
            pe.wait_ge(consts, CONSTS)
            pe.wait_ge(w_in, 16 * 8)
            with pe.Fori(0, NBLK // 2) as Cp:
                for par in range(2):
                    pe.wait_ge(agg_out, (Cp * 2 + par) * 4 + 4)
                    for b in range(2):
                        for u in range(2):
                            nc.tensor.matmul(agg_ps[par][b][u][:, :], zeros[:, 0:P], zeros[:, :], start=True, stop=True, skip_group_check=True)
                    with pe.Fori(0, NG) as g:
                        for k in range(G8):
                            if k % 4 == 0:
                                pe.wait_ge(x_in[k // 4], ((Cp * 2 + par) * NG + g + 1) * 16)
                            pe.wait_ge(a_in[k % 4], ((Cp * 2 + par) * 8 + g * 2 + (k // 4 + 1)) * 16)
                            for b in range(2):
                                for u in range(2):
                                    mm = nc.tensor.matmul(agg_ps[par][b][u][:, :], x_slot[k // 4][:, k % 4, b * P:(b + 1) * P],
                                                          a_slot[k % 4][:, u * CH:(u + 1) * CH], start=False, stop=True, skip_group_check=True)
                            mm.then_inc(a_used_pe, 1)
            pe.wait_ge(agg_out, 8 + 4 * NBLK)
            for m in range(LAYERS * 16):
                layer, c, b = m // 16, m % 16 // 2, m % 2
                if m >= 8:
                    pe.wait_ge(mlp_act, m - 7)
                nc.tensor.matmul(bank[m % 8][:, :], wt_sb[:, b * LAYERS + layer, :], high[:, b, c * CH:(c + 1) * CH],
                                 start=True, stop=True).then_inc(mlp_mm, 1)
            for q in range(NCH):
                pe.wait_ge(mlp_act, max(41 + q, 34 + 2 * q))
                for g in range(4 * q, 4 * q + 4):
                    o = bank[q][:, (g % 4) * P:(g % 4 + 1) * P]
                    nc.tensor.matmul(o, high[:, 0, g * P:(g + 1) * P], wm_sb[:, 0, :], start=(g % 4 == 0), stop=True, skip_group_check=True)
                    nc.tensor.matmul(o, high[:, 1, g * P:(g + 1) * P], wm_sb[:, 1, :], start=False, stop=True, skip_group_check=True)
                    mm = nc.tensor.matmul(o, ones_row[:, :], bm_row[:, :], start=False, stop=True, skip_group_check=True)
                mm.then_inc(mg_mm, 1)
            pe.wait_ge(res_ok, 1)
            for h in range(HEADS):
                mm = nc.tensor.matmul(bank[0][:, 2 * h:2 * h + 2], gwt_sb[:, h, :], ga_sb[:, h, :], start=(h == 0), stop=True, skip_group_check=True)
            mm.then_inc(u_mm, 1)
            pe.wait_ge(u_ok, 1)
            for q in range(NCH):
                pe.wait_ge(ln_ok, 4 * (q + 1))
                for g in range(4 * q, 4 * q + 4):
                    mm = nc.tensor.transpose(bank[q][:, (g % 4) * P:(g % 4 + 1) * P], hn[:, g, :], ident[:, :])
                mm.then_inc(ht_mm, 1)
            for g in range(T):
                if g % 4 == 0:
                    pe.wait_ge(ht_ok, g // 4 + 1)
                mm = nc.tensor.matmul(bank[0][:, 6 * g:6 * g + 6], ht[:, g * P:(g + 1) * P], u_sb[:, :, :].rearrange("p s h -> p (s h)"),
                                      start=(g == 0), stop=True, skip_group_check=True)
            mm.then_inc(v_mm, 1)
            pe.wait_ge(flag_ok, 1)
            has_neg = pe.value_load(flag[0:1, 0:1], min_val=0, max_val=1)

            def logits(s, NS):
                W = 9 * NS
                with pe.Fori(0, NBLK) as C:
                    pe.wait_ge(s.e_ps_free, C + 1)
                    nc.tensor.matmul(bank[1][:, 0:RB * W], zeros[:, 0:P], zeros[:, 0:RB * W], start=True, stop=True, skip_group_check=True)
                    with pe.Fori(0, NG) as g:
                        for k in range(G8):
                            if k % 4 == 0:
                                pe.wait_ge(s.p_ready, (C * NG + g) * 2 + (k // 4 + 1))
                            t = C * RB + g * G8 + k
                            for i in range(RB):
                                o = bank[1][:, i * W:(i + 1) * W].rearrange("p (a c) -> p a c", a=3)
                                mm = nc.tensor.matmul(o, p_slot[k // 4][:, k % 4, i * P:(i + 1) * P],
                                                      v3[:, bass.ds(t, 1), :, 0:3 * NS].rearrange("p o a c -> p (o a) c"),
                                                      start=False, stop=True, skip_group_check=True)
                                if NS == 2:
                                    for sg in range(2):
                                        mm = nc.tensor.matmul(o[:, :, 3 * sg:3 * sg + 3], m_slot[k // 4][:, k % 4, i * P:(i + 1) * P],
                                                              v3[:, bass.ds(t, 1), :, 3 - 3 * sg:6 - 3 * sg].rearrange("p o a c -> p (o a) c"),
                                                              start=False, stop=True, skip_group_check=True)
                            if k % 4 == 3:
                                mm.then_inc(s.p_used, 1)

            def attention(s, NS):
                NU = NS * HEADS
                pe.sem_inc(s.lg_ready, 4 * NU)
                pe.sem_inc(s.w_used, 8 * NU + 3)
                pe.sem_inc(s.e_used, 6)
                with pe.Fori(0, NBLK) as C:
                    for u in range(2):
                        cc = C * 2 + u
                        pe.wait_ge(s.max_step, (cc + 1) * (HEADS + T * NU))
                        pe.wait_ge(s.exp_ok, cc * T * NU + 2)
                        for h in range(HEADS):
                            for i in range(4):
                                mm = nc.tensor.transpose(tr_ps[h][:, i * P:(i + 1) * P], macc[h][:, i * P:(i + 1) * P], ident[:, :])
                            mm.then_inc(s.macc_tr, 1)
                        pe.wait_ge(s.parts_ok, cc + 1)
                        for h in range(HEADS):
                            for i in range(4):
                                mm = nc.tensor.transpose(tr_ps[h][0:3, i * P // 2:(i + 1) * P // 2].bitcast(BF16), mparts[:, h, i, :], ident_bf[:, :])
                            mm.then_inc(s.parts_tr, 1)
                        pe.wait_ge(s.mrow_ok, (cc + 1) * HEADS)
                        pe.wait_ge(s.evac_act, cc * 3 + 3)
                        pe.wait_ge(s.evac_dve, cc * 2 + 2)
                        for b in range(5):
                            nc.tensor.matmul(bank[b][:, :], zeros[:, 0:P], zeros[:, :], start=True, stop=True, skip_group_check=True)
                        with pe.Fori(0, NG) as g:
                            body = cc * NG + g
                            tile0 = body * G8

                            def logit(n):
                                k, v = n // NU, n % NU
                                if v == 0 and NS == 1:
                                    pe.wait_ge(s.rb_ready, tile0 + (k + 1))
                                if v % HEADS == 0 and NS == 2:
                                    pe.wait_ge(s.rb_ready, (tile0 + k) * 2 + (v // HEADS + 1))
                                mask = rb[k % 4] if NS == 1 else rb[(2 * k + v // HEADS) % 4]
                                pe.wait_ge(s.exp_ok, tile0 * NU + (n + 1))
                                nc.tensor.matmul(lg_ps[n % 2][:, :], penalty[:, :], mask, start=True, stop=False)
                                nc.tensor.matmul(lg_ps[n % 2][:, :], ones3[:, :], mrow[u][:, v % HEADS, :], start=False, stop=True).then_inc(s.lg_ready, 1)
                            logit(0)
                            logit(1)
                            for k in range(G8):
                                hk = h_slot[k // 4][:, k % 4, :]
                                if k % 4 == 0:
                                    pe.wait_ge(s.h_in[k // 4], (body + 1) * 16)
                                if k % 2 == 0:
                                    pe.wait_ge(s.a2_in[k // 2], (body + 1) * 16)
                                if k // 4 == u:
                                    pe.wait_ge(s.a2_masked, body * 4 + (k % 4 + 1))
                                nc.tensor.matmul(node_ps[:, :], hk, a2_slot[k // 2][:, k % 2, :], start=False, stop=True, skip_group_check=True)
                                for n in range(k * NU, (k + 1) * NU):
                                    if n + 2 < G8 * NU:
                                        logit(n + 2)
                                    pe.wait_ge(s.w_ready, tile0 * NU + (n + 1 + 8 * NU))
                                    nc.tensor.matmul(num_ps[n % HEADS][:, :], hk, wbuf[n % 3], start=False, stop=True, skip_group_check=True).then_inc(s.w_used, 1)
                                for n in range(k * NU, (k + 1) * NU):
                                    h = n % HEADS
                                    nc.tensor.matmul(den_ps[32 * h:32 * h + 1, :], ones_col[:, :], ebuf[n % 6], start=False, stop=True,
                                                     skip_group_check=True).then_inc(s.e_used, 1)
            with pe.If(has_neg != 0):
                pe.sem_inc(S[2].p_used, 2)
                pe.wait_ge(v_ok, 1)
                logits(S[2], 2)
                attention(S[2], 2)
            with pe.Else():
                pe.sem_inc(S[1].p_used, 2)
                pe.wait_ge(v_ok, 1)
                logits(S[1], 1)
                attention(S[1], 1)

            pe.wait_ge(fw_in, 48)
            pe.wait_ge(f_scaled, 1)

            def cell(i, x, hh):
                bk = bank[4 * i:4 * i + 4]
                for gate in range(2):
                    nc.tensor.matmul(bk[gate][:, :], gw_sb[:, 6 * i + gate, :], x, start=True, stop=False)
                    nc.tensor.matmul(bk[gate][:, :], gw_sb[:, 6 * i + 3 + gate, :], hh, start=False, stop=True)
                nc.tensor.matmul(bk[2][:, :], gw_sb[:, 6 * i + 2, :], x, start=True, stop=True)
                nc.tensor.matmul(bk[3][:, :], gw_sb[:, 6 * i + 5, :], hh, start=True, stop=True).then_inc(f_mm, 1)

            def rows(c):
                pe.wait_ge(f_dve, c * PER_DVE + 14)
                for i in range(4):
                    mm = nc.tensor.transpose(bank[1][:, i * P:(i + 1) * P], f_o[0][c % 2][:, i * P:(i + 1) * P], ident[:, :])
                mm.then_inc(f_mm, 1)
            for c in range(NCH):
                s = c % 2
                pe.wait_ge(f_in[s], (c // 2 + 1) * 16 * 7)
                if c:
                    pe.wait_ge(f_dve, c * PER_DVE)
                cell(0, f_node[s], f_ht[s])
                pe.wait_ge(f_dve, c * PER_DVE + 3)
                pe.wait_ge(f_act, last_act(c, "r0"))
                for h in range(HEADS):
                    mm = nc.tensor.matmul(bank[0][:, :], pw_sb[:, h, :], f_num[s][:, h, :], start=(h == 0), stop=(h == HEADS - 1))
                mm.then_inc(f_mm, 1)
                pe.wait_ge(f_act, last_act(c, "es"))
                cell(1, f_es[s], f_ht[s])
                rows(c)

        @block.vector
        def _(dve):
            steps = [0]

            def link(ins):
                steps[0] += 1
                ins.then_inc(chain, 1)
                dve.wait_ge(chain, steps[0])

            dve.sem_inc(neg_step, 2)
            nc.vector.memset(neg_acc, 0.0).then_inc(neg_step, 1)
            nc.vector.memset(ones_u8[:, :], 1.0).then_inc(ones_ok, 1)
            dve.wait_ge(w_in, 16 * 8)
            nc.vector.tensor_scalar(eps_sb[:, :], eps_sb[:, :], 1.0, 1.0, ALU.add, ALU.add).then_inc(scale_ok, 1)
            with dve.Fori(0, NBLK) as C:
                with dve.Fori(0, NG) as g:
                    for k in range(G8):
                        n1 = C * T + g * G8 + (k + 1)
                        dve.wait_ge(a_signed, n1 + 8)
                        nc.vector.tensor_scalar(codes[:, bass.ds(C * T + g * G8 + k, 1), :].rearrange("p r n -> p (r n)"),
                                                sgn[:, k % 2, :], 1.0, None, ALU.add)
                        dve.wait_ge(neg_step, n1 + 2)
                        nc.vector.tensor_tensor(neg_acc, neg_acc, sgn[:, k % 2, :], ALU.max).then_inc(neg_step, 1)
            dve.wait_ge(neg_step, NBLK * T + 3)
            nc.vector.tensor_reduce(flag_f[:, 0:1], neg_acc, AX.X, ALU.max).then_inc(flag_max, 1)
            dve.wait_ge(consts, CONSTS)
            dve.wait_ge(ones_ok, 1)
            for C in range(NBLK):
                for r in range(RB):
                    ins = nc.vector.copy_predicated(codes[:, C * T + r, r * P:(r + 1) * P], ident_u8[:, :], ones_u8[:, :])
            link(ins)
            dve.wait_ge(flag_all, 1)
            nc.vector.tensor_scalar(flag[0:1, 0:1], flag_f[0:1, 1:2], 0.0, None, ALU.is_gt).then_inc(flag_ok, 1)

            def statistics(q, rows):
                for i in range(4):
                    ins = nc.vector.bn_stats(bst[:, i, :], rows[:, 4 * q + i, :])
                link(ins)
                for i in range(4):
                    ins = nc.vector.bn_aggr(mv[:, 4 * q + i, :], bst[:, i, :])
                link(ins)

            dve.wait_ge(xn_in, 16)
            for q in range(NCH):
                dve.wait_ge(mg_mm, q + 1)
                r = hn[:, 4 * q:4 * q + 4, :]
                ins = nc.vector.tensor_tensor(r, bank[q][:, :].rearrange("p (t n) -> p t n", t=4), r, ALU.add)
                link(ins)
                dve.sem_inc(res_ok, 1)
                statistics(q, hn)
                if q == 0:
                    dve.wait_ge(u_mm, 1)
                    link(nc.vector.tensor_copy(u_sb[:, :, :], bank[0][:, 0:6].rearrange("p (h s) -> p s h", s=2)))
                    dve.sem_inc(u_ok, 1)

            def normalize(rows, std, ready):
                link(nc.vector.tensor_scalar(rstd[:, :], mv[:, :, 1], EPS, None, ALU.add))
                dve.sem_inc(var_ok, 1)
                dve.wait_ge(std, 1)
                link(nc.vector.reciprocal(rstd[:, :], rstd[:, :]))
                for t in range(T):
                    nc.vector.tensor_scalar(rows[:, t, :], rows[:, t, :], mv[:, t, 0:1], rstd[:, t:t + 1],
                                            ALU.subtract, ALU.mult).then_inc(ready, 1)
            normalize(hn, std_ok, ln_ok)
            dve.wait_ge(v_mm, 1)
            link(nc.vector.tensor_copy(v_f[:, :, :], bank[0][:, 0:6 * T].rearrange("p (t c) -> p t c", c=6)))
            for part in range(3):
                src = v_f if part == 0 else v_r
                nc.vector.tensor_copy(v3[:, T:2 * T, part, :], src[:, :, :])
                link(nc.vector.tensor_copy(v3[:, 0:T, part, :], src[:, :, :]))
                if part < 2:
                    link(nc.vector.tensor_tensor(v_r[:, :, :], src[:, :, :], v3[:, 0:T, part, :], ALU.subtract))
            dve.sem_inc(v_ok, 1)
            has_neg = dve.value_load(flag[0:1, 0:1], min_val=0, max_val=1)

            def logits(s, NS):
                W = 9 * NS
                dve.sem_inc(s.e_ps_free, 1)
                with dve.Fori(0, NBLK) as C:
                    with dve.Fori(0, NG) as g:
                        for k in range(0, G8, 4):
                            q1 = (C * NG + g) * 2 + (k // 4 + 1)
                            dve.wait_ge(s.p_used, q1)
                            src = codes[:, bass.ds(C * T + g * G8 + k, 4), :]
                            if NS == 2:
                                nc.vector.tensor_scalar(m_slot[k // 4], src, 1.0, None, ALU.is_gt).then_inc(s.rn_step, 1)
                                dve.wait_ge(s.rn_step, q1)
                            nc.vector.tensor_scalar(p_slot[k // 4], src, 1.0, None, ALU.is_lt).then_inc(s.p_ready, 1)
                    dve.wait_ge(s.p_used, (C + 1) * 2 * NG + 2)
                    c3 = slice(0, 3 * NS)
                    n = [0]

                    def step(ins):
                        n[0] += 1
                        ins.then_inc(s.chain2, 1)
                        dve.wait_ge(s.chain2, C * 5 + n[0])
                    step(nc.vector.tensor_copy(e_tmp[:, :, :, c3], bank[1][:, 0:RB * W].rearrange("p (i a c) -> p i a c", i=RB, a=3)))
                    step(nc.vector.tensor_tensor(e_tmp[:, :, 1, c3], e_tmp[:, :, 1, c3], e_tmp[:, :, 2, c3], ALU.add))
                    step(nc.vector.tensor_tensor(e_tmp[:, :, 0, c3], e_tmp[:, :, 0, c3], e_tmp[:, :, 1, c3], ALU.add))
                    for dup in range(2):
                        t8 = bass.ds(C * RB + dup * T, RB)
                        ins = nc.vector.scalar_tensor_tensor(out=e_nat[:, t8, c3], in0=e_tmp[:, :, 0, c3], scalar=ALPHA,
                                                             in1=e_tmp[:, :, 0, c3], op0=ALU.mult, op1=ALU.max)
                    step(ins)
                    for dup in range(2):
                        t8 = bass.ds(C * RB + dup * T, RB)
                        ins = nc.vector.tensor_scalar(e_sc[:, t8, c3], e_nat[:, t8, c3], ESC, None, ALU.mult)
                    step(ins)
                    dve.sem_inc(s.e_ps_free, 1)

            def attention(s, NS):
                NU = NS * HEADS
                PASS = HEADS + T * NU
                FIN = 7
                dve.sem_inc(s.w_ready, 8 * NU)
                dve.sem_inc(s.evac_dve, 2)
                dve.wait_ge(ht_out, 16 * NCH)
                dve.wait_ge(h_out, 16 * (NCH + (TD - T) // 4))

                nc.vector.memset(off_diag[:, 1:NG, :], 1.0)
                nc.vector.tensor_scalar(off_diag[:, 0, :], ident[:, :], 0.0, None, ALU.is_equal)
                for b in range(2):
                    nc.vector.memset(mrow[b], 0.0)

                def clear():
                    for h in range(HEADS):
                        nc.vector.memset(macc[h], 4.0).then_inc(s.max_step, 1)

                def search(cc, Cs, us, g, k):
                    code = codes[:, bass.ds(Cs * T + g * G8 + k, 1), us * CH:(us + 1) * CH].rearrange("p r n -> p (r n)")
                    for v in range(NU):
                        if v == HEADS:
                            dve.wait_ge(s.max_step, cc * PASS + g * (G8 * NU) + (k * NU + 1))
                            nc.vector.tensor_scalar(neg_code[:, k % 2, :], code, 2.0, None, ALU.is_lt).then_inc(s.rn_step, 1)
                            dve.wait_ge(s.rn_step, T + cc * T + g * G8 + (k + 1))
                            code = neg_code[:, k % 2, :]
                        dve.wait_ge(s.max_step, cc * PASS + g * (G8 * NU) + (k * NU + v + 1))
                        e = e_sc[:, bass.ds(Cs * RB + g * G8 + k, 1), v:v + 1].rearrange("p a b -> p (a b)")
                        nc.vector.scalar_tensor_tensor(out=macc[v % HEADS], in0=code, scalar=e, in1=macc[v % HEADS],
                                                       op0=ALU.subtract, op1=ALU.min).then_inc(s.max_step, 1)

                clear()
                with dve.Fori(0, NG) as g:
                    for k in range(G8):
                        search(0, 0, 0, g, k)
                with dve.Fori(0, NBLK) as C:
                    for u in range(2):
                        cc = C * 2 + u
                        Cn = C if u == 0 else (C + 1) % NBLK
                        for h in range(HEADS):
                            dve.wait_ge(s.macc_tr, cc * HEADS + (h + 1))
                            red = nc.vector.tensor_reduce(wmin[:, h, :], tr_ps[h][:, :].rearrange("p (i n) -> p i n", i=4), AX.X, ALU.min)
                        n = [0]

                        def step(ins):
                            n[0] += 1
                            ins.then_inc(s.chain2, 1)
                            dve.wait_ge(s.chain2, NBLK * 5 + cc * FIN + n[0])
                        step(red)
                        step(nc.vector.scalar_tensor_tensor(out=negm[:, :, :], in0=wmin[:, :, :], scalar=0.5, in1=wmin[:, :, :], op0=ALU.is_lt, op1=ALU.mult))
                        step(nc.vector.tensor_scalar(negm[:, :, :], negm[:, :, :], 1.0 / ESC, None, ALU.mult))
                        for part in range(3):
                            cut = nc.vector.tensor_copy(mparts[:, :, :, part], negm[:, :, :])
                            if part < 2:
                                step(cut)
                                step(nc.vector.tensor_tensor(negm[:, :, :], negm[:, :, :], mparts[:, :, :, part], ALU.subtract))
                            else:
                                cut.then_inc(s.parts_ok, 1)
                        clear()
                        with dve.Fori(0, NG) as g:
                            body = cc * NG + g
                            tile0 = body * G8

                            def masks(k):
                                code = codes[:, bass.ds(C * T + g * G8 + k, 1), u * CH:(u + 1) * CH].rearrange("p r n -> p (r n)")
                                dve.wait_ge(s.lg_ready, (tile0 + k) * NU + 3 * NU)
                                nc.vector.tensor_scalar(rb[2 * k % 4], code, 0.0, None, ALU.is_gt).then_inc(s.rb_ready, 1)
                                nc.vector.tensor_scalar(rb[(2 * k + 1) % 4], code, 2.0, None, ALU.is_lt).then_inc(s.rb_ready, 1)
                            if NS == 2:
                                masks(0)
                                masks(1)
                            for k in range(G8):
                                if k % 2 == 0:
                                    dve.wait_ge(s.a2_in[k // 2], (body + 1) * 16)
                                if k // 4 == u:
                                    i = k % 4
                                    d = a2_slot[k // 2][:, k % 2, i * P:(i + 1) * P]
                                    nc.vector.tensor_tensor(d, d, off_diag[:, bass.ds(g, 1), :].rearrange("p o n -> p (o n)"), ALU.mult).then_inc(s.a2_masked, 1)
                                    dve.wait_ge(s.a2_masked, body * 4 + (i + 1))
                                for n1 in range(k * NU, (k + 1) * NU):
                                    dve.wait_ge(s.exp_ok, tile0 * NU + (n1 + 3))
                                    dve.wait_ge(s.w_used, tile0 * NU + (n1 + 1 + 8 * NU))
                                    nc.vector.tensor_tensor(wbuf[n1 % 3], ebuf[n1 % 6], a2_slot[k // 2][:, k % 2, :], ALU.mult).then_inc(s.w_ready, 1)
                                search(cc + 1, Cn, 1 - u, g, k)
                                if NS == 2 and k + 2 < G8:
                                    masks(k + 2)
                        dve.wait_ge(s.e_used, (cc + 1) * (T * NU) + 6)
                        dve.wait_ge(s.stage_out, cc * 48 + 48)
                        nc.vector.tensor_copy(stage[3], node_ps[:, :]).then_inc(s.evac_dve, 1)
                        nc.vector.tensor_copy(stage[4], den_ps[:, :]).then_inc(s.evac_dve, 1)
            with dve.If(has_neg != 0):
                logits(S[2], 2)
                attention(S[2], 2)
            with dve.Else():
                logits(S[1], 1)
                attention(S[1], 1)

            dve.wait_ge(fw_in, 48)
            for i in range(2):
                b = gb_sb[:, 6 * i:6 * i + 2]
                nc.vector.tensor_tensor(b, b, gb_sb[:, 6 * i + 4:6 * i + 6], ALU.add).then_inc(bias_ok, 1)
            done = [0]

            def step(ins):
                done[0] += 1
                ins.then_inc(f_dve, 1)
                dve.wait_ge(f_dve, done[0])
            for c in range(NCH):
                s = c % 2
                dve.wait_ge(f_in[s], (c // 2 + 1) * 16 * 7)
                step(nc.vector.tensor_scalar(f_den[s], f_den[s], 1e-30, None, ALU.max))
                step(nc.vector.reciprocal(f_den[s], f_den[s]))
                step(nc.vector.tensor_tensor(f_num[s], f_num[s], f_den[s], ALU.mult))
                for i in range(2):
                    bk = bank[4 * i:4 * i + 4]
                    dve.wait_ge(f_act, last_act(c, f"z{i}"))
                    step(nc.vector.scalar_tensor_tensor(out=f_t[i], in0=bk[3][:, :], scalar=gb_sb[:, 6 * i + 3:6 * i + 4], in1=f_r[i], op0=ALU.add, op1=ALU.mult))
                    step(nc.vector.tensor_tensor(f_t[i], bk[2][:, :], f_t[i], ALU.add))
                    dve.wait_ge(f_act, last_act(c, f"n{i}"))
                    step(nc.vector.tensor_tensor(f_t[i], f_ht[s], f_n[i], ALU.subtract))
                    step(nc.vector.tensor_tensor(f_t[i], f_t[i], f_z[i], ALU.mult))
                    step(nc.vector.tensor_tensor(f_o[i][s], f_n[i], f_t[i], ALU.add))
                step(nc.vector.tensor_tensor(f_o[0][s], f_o[0][s], f_o[1][s], ALU.add))
                dve.wait_ge(f_mm, last_mm(c, "tr"))
                for i in range(4):
                    t = 4 * c + i
                    ins = nc.vector.scalar_tensor_tensor(out=fin[:, t, :], in0=bank[1][:, i * P:(i + 1) * P], scalar=d_sb[:, t:t + 1],
                                                         in1=f_hn[s][:, i, :], op0=ALU.mult, op1=ALU.add)
                    if i < 3:
                        done[0] += 1
                        ins.then_inc(f_dve, 1)
                step(ins)
                dve.sem_inc(f_slot_free, 1)
                statistics(c, fin)
            normalize(fin, f_std, out_ready)


def kernel(x, adj, L0_gnn_x2, L0_gnn_eps1, L0_gnn_eps2, L0_gnn_W1, L0_gnn_b1, L0_gnn_W2, L0_gnn_b2, L0_gnn_Wm, L0_gnn_bm,
           L1_gnn_gat_W, L1_gnn_gat_a, L1_gnn_edge_Wih, L1_gnn_edge_Whh, L1_gnn_edge_bih, L1_gnn_edge_bhh,
           L1_gnn_node_Wih, L1_gnn_node_Whh, L1_gnn_node_bih, L1_gnn_node_bhh):
    import numpy as np
    from concourse import bacc
    from concourse.bass_utils import run_bass_kernel_spmd

    def gates(w):
        return [w[g * P:(g + 1) * P].T for g in range(3)]
    adj = np.asarray(adj)
    at = adj.T.reshape(T, P, NBLK, BW)
    a_tiles = np.concatenate([np.roll(at[:, :, C], -RB * C, axis=0) for C in range(NBLK)])
    both = np.concatenate([np.asarray(x), np.asarray(L0_gnn_x2)], axis=1).reshape(T, P, 2 * P)
    arrays = dict(
        a_tiles=a_tiles,
        xx=np.concatenate([both, both[:TD - T]]),
        x_nat=np.asarray(x),
        diag=np.diagonal(adj).reshape(T, P).T,
        eps=np.concatenate([L0_gnn_eps1, L0_gnn_eps2]),
        w_t=np.concatenate([L0_gnn_W1, L0_gnn_W2]).transpose(0, 2, 1),
        w_b=np.concatenate([L0_gnn_b1, L0_gnn_b2]).T,
        wm_t=np.asarray(L0_gnn_Wm).T,
        bm=np.asarray(L0_gnn_bm),
        gat_w=np.asarray(L1_gnn_gat_W),
        gat_wt=np.asarray(L1_gnn_gat_W).transpose(0, 2, 1),
        gat_a=np.asarray(L1_gnn_gat_a).reshape(HEADS, 2, P).transpose(2, 0, 1),
        gru_w=np.stack(gates(np.asarray(L1_gnn_edge_Wih)) + gates(np.asarray(L1_gnn_edge_Whh))
                       + gates(np.asarray(L1_gnn_node_Wih)) + gates(np.asarray(L1_gnn_node_Whh))),
        gru_b=np.stack([np.asarray(b)[g * P:(g + 1) * P] for bi, bh in ((L1_gnn_edge_bih, L1_gnn_edge_bhh), (L1_gnn_node_bih, L1_gnn_node_bhh))
                        for b, g in ((bi, 0), (bi, 1), (bi, 2), (bh, 2), (bh, 0), (bh, 1))]).T,
    )
    arrays = {k: np.ascontiguousarray(v) for k, v in arrays.items()}
    nc = bacc.Bacc("TRN2", target_bir_lowering=False, num_devices=1)
    aps = {k: nc.dram_tensor(k, v.shape, F32, kind="ExternalInput").ap() for k, v in arrays.items()}
    out = nc.dram_tensor("out", (N, P), F32, kind="ExternalOutput").ap()
    build(nc, **aps, out=out)
    return run_bass_kernel_spmd(nc, [arrays], core_ids=[0]).results[0]["out"]
```

```python
import numpy as np
import concourse.bass as bass
from concourse import mybir
from contextlib import ExitStack

F32 = mybir.dt.float32
BF16 = mybir.dt.bfloat16
U8 = mybir.dt.uint8
I32 = mybir.dt.int32
ALU = mybir.AluOpType
ACT = mybir.ActivationFunctionType
AX = mybir.AxisListType

P = 128
N = 4096
T = N // P
BW = 1024
NBLK = N // BW
CH = 512
NCH = N // CH
RB = BW // P
TD = T + RB * (NBLK - 1)
HEADS = 3
LAYERS = 3
EPS = 1e-5
G8 = 8
NG = T // G8
BIG = 2.0 ** 100
ESC = 2.0 ** -40
ALPHA = 0.2


def chunk_after(C, u, n):
    return (C, 1) if (u, n) == (0, 1) else ((C + 1) % NBLK, (u + n) % 2)


def build(nc, a_tiles, xx, x_nat, diag, eps, w_t, w_b, wm_t, bm, gat_w, gat_wt, gat_a,
          gru_w, gru_b, out):
    h_dram = nc.dram_tensor("h_dram", (TD, P, P), F32, kind="Internal").ap()
    ht_dram = nc.dram_tensor("ht_dram", (P, N), F32, kind="Internal").ap()
    den_dram = nc.dram_tensor("den_dram", (4, HEADS, N), F32, kind="Internal").ap()
    rden_dram = nc.dram_tensor("rden_dram", (HEADS, N), F32, kind="Internal").ap()
    agg_dram = nc.dram_tensor("agg_dram", (NCH, 4, P, CH), F32, kind="Internal").ap()

    ctx = ExitStack()
    with ctx:
        def sb(name, shape, dt):
            return ctx.enter_context(nc.sbuf_tensor(name, shape, dt))

        def sem(name):
            return ctx.enter_context(nc.semaphore(name))

        codes = sb("codes", [P, NBLK * T, BW], U8)
        ring = sb("ring", [P, 4 * BW], F32)
        low = sb("low", [P, 4096], F32)
        high = sb("high", [P, 2, N], F32)
        weights = sb("weights", [P, 13 * P], F32)
        wt_sb = weights[:, 0:6 * P].rearrange("p (l n) -> p l n", l=2 * LAYERS)
        gwt_sb = weights[:, 6 * P:9 * P].rearrange("p (h n) -> p h n", h=HEADS)
        wm_sb = weights[:, 9 * P:11 * P].rearrange("p (b n) -> p b n", b=2)
        bm_row = weights[0:1, 11 * P:12 * P]
        ones_row = weights[0:1, 12 * P:13 * P]
        wb_sb = sb("wb_sb", [P, 2 * LAYERS], F32)
        ga_sb = sb("ga_sb", [P, HEADS, 2], F32)
        eps_sb = sb("eps_sb", [P, 2], F32)
        u_sb = sb("u_sb", [P, 2, HEADS], F32)
        ident = sb("ident", [P, P], F32)
        ident_bf = sb("ident_bf", [P, P], BF16)
        ident_u8 = sb("ident_u8", [P, P], U8)
        penalty = sb("penalty", [P, P], BF16)
        ones3 = sb("ones3", [P, P], BF16)
        zeros = sb("zeros", [P, CH], BF16)
        minus_one = sb("minus_one", [P, 1], F32)
        head_col = sb("head_col", [P, HEADS, HEADS], F32)
        v_f, v_r = (high[:, 1, i * 6 * T:(i + 1) * 6 * T].rearrange("p (t c) -> p t c", c=6) for i in range(2))
        v3 = sb("v3", [P, 64, 3, 6], BF16)
        e_nat = sb("e_nat", [P, 64, 6], F32)
        e_sc = sb("e_sc", [P, 64, 6], F32)
        e_tmp = weights[:, 0:RB * 18].rearrange("p (i a c) -> p i a c", i=RB, a=3)
        mv = sb("mv", [P, T, 2], F32)
        rstd = sb("rstd", [P, T], F32)
        bst = sb("bst", [P, 4, 6], F32)
        wmin = sb("wmin", [P, HEADS, 4], F32)
        negm = sb("negm", [P, HEADS, 4], F32)
        off_diag = weights[:, 8 * P:10 * P].bitcast(BF16).rearrange("p (g n) -> p g n", g=NG)
        neg_code = weights[:, 10 * P:12 * P].bitcast(U8).rearrange("p (s n) -> p s n", s=2)
        ones_u8 = sb("ones_u8", [P, P], U8)
        mparts = sb("mparts", [P, HEADS, 4, 3], BF16)
        flag_f = sb("flag_f", [P, 2], F32)
        flag = sb("flag", [1, 1], I32)
        d_sb = sb("d_sb", [P, T], F32)

        a_slot = [ring[:, s * BW:(s + 1) * BW] for s in range(4)]
        x_slot = [low[:, s * 1024:(s + 1) * 1024].rearrange("p (r n) -> p r n", r=4) for s in range(2)]
        sgn = low[:, 2048:3072].bitcast(BF16).rearrange("p (s n) -> p s n", s=2)
        neg_acc = low[:, 3072:3584].bitcast(BF16)
        hn = low[:, :].rearrange("p (t n) -> p t n", t=T)
        ht = high[:, 0, :]
        p_slot = [ring[:, s * 2048:(s + 1) * 2048].bitcast(BF16).rearrange("p (r n) -> p r n", r=4) for s in range(2)]
        m_slot = [low[:, s * 2048:(s + 1) * 2048].bitcast(BF16).rearrange("p (r n) -> p r n", r=4) for s in range(2)]
        a2_slot = [ring[:, s * 1024:(s + 1) * 1024].rearrange("p (r n) -> p r n", r=2) for s in range(4)]
        h_slot = [low[:, s * 512:(s + 1) * 512].rearrange("p (r n) -> p r n", r=4) for s in range(2)]
        rb = [low[:, 1024 + s * 256:1024 + (s + 1) * 256].bitcast(BF16) for s in range(4)]
        stage = [low[:, 2048 + s * CH:2048 + (s + 1) * CH] for s in range(4)] + [high[:, 1, 3584:4096]]
        ebuf = [high[:, 0, s * CH:(s + 1) * CH] for s in range(6)]
        macc = [high[:, 0, 3072:3584], high[:, 0, 3584:4096], high[:, 1, 0:512]]
        wbuf = [high[:, 1, 512 + s * CH:512 + (s + 1) * CH] for s in range(3)]
        mrow = [high[:, 1, 2048 + s * 768:2048 + (s + 1) * 768].bitcast(BF16).rearrange("p (h n) -> p h n", h=HEADS) for s in range(2)]
        lgs = [weights[:, s * CH:(s + 1) * CH] for s in range(2)]
        max_all = v3[:, :, :, :].rearrange("p t a c -> p (t a c)")[:, 0:2 * CH].bitcast(F32)
        fcodes = codes[:, :, :].rearrange("p t n -> p (t n)").bitcast(F32)
        at = [T * BW // 4]

        def last(n):
            at[0] += n
            return fcodes[:, at[0] - n:at[0]]
        gw_sb = last(12 * P).rearrange("p (g n) -> p g n", g=12)
        pw_sb = last(HEADS * P).rearrange("p (h n) -> p h n", h=HEADS)
        gb_sb = last(12)
        at[0] += 4
        f_num = [last(3 * CH).rearrange("p (h n) -> p h n", h=3) for _ in range(2)]
        f_node = [last(CH) for _ in range(2)]
        f_ht = [last(CH) for _ in range(2)]
        f_hn = [last(CH).rearrange("p (t n) -> p t n", t=4) for _ in range(2)]
        WD = N // P
        den_c = last(4 * HEADS * WD).rearrange("p (g n) -> p g n", g=4)
        f_den = [last(3 * CH).rearrange("p (h n) -> p h n", h=3) for _ in range(2)]
        assert at[0] <= 3 * T * BW // 4
        f_es = [last(CH) for _ in range(2)]
        f_r, f_z, f_t, f_n = ([last(CH) for _ in range(2)] for _ in range(4))
        f_o = [[last(CH) for _ in range(2)] for _ in range(2)]
        fin = last(N).rearrange("p (t n) -> p t n", t=T)
        assert at[0] <= NBLK * T * BW // 4

        bank = [ctx.enter_context(nc.psum_tensor(f"bank{i}", [P, CH], F32)) for i in range(8)]
        agg_ps = [[[bank[4 * par + 2 * b + u] for u in range(2)] for b in range(2)] for par in range(2)]
        num_ps, node_ps, den_ps, lg_ps, tr_ps = bank[0:3], bank[3], bank[4], bank[5:7], bank[7]

        w_in = sem("w_in")
        consts = sem("consts")
        zero_ok = sem("zero_ok")
        scale_ok = sem("scale_ok")
        a_in = [sem(f"a_in{s}") for s in range(4)]
        x_in = [sem(f"x_in{s}") for s in range(2)]
        a_used_pe = sem("a_used_pe")
        a_signed = sem("a_signed")
        neg_step = sem("neg_step")
        ones_ok = sem("ones_ok")
        agg_out = sem("agg_out")
        flag_max = sem("flag_max")
        flag_all = sem("flag_all")
        flag_ok = sem("flag_ok")
        mlp_mm = sem("mlp_mm")
        mlp_act = sem("mlp_act")
        xn_in = sem("xn_in")
        mg_mm = sem("mg_mm")
        res_ok = sem("res_ok")
        var_ok = sem("var_ok")
        std_ok = sem("std_ok")
        ln_ok = sem("ln_ok")
        chain = sem("chain")
        h_out = sem("h_out")
        ht_mm = sem("ht_mm")
        ht_ok = sem("ht_ok")
        ht_out = sem("ht_out")
        u_mm = sem("u_mm")
        u_ok = sem("u_ok")
        v_mm = sem("v_mm")
        v_ok = sem("v_ok")

        def attention_sems(tag):
            names = ["p_act", "p_dve", "p_used", "e_ps_free", "a2_masked", "max_step", "rn_step", "macc_tr", "min_ok", "parts_ok", "parts_tr", "mrow_ok", "rb_ready",
                     "lg_ready", "lgs_ready", "max_mm", "max_ok", "exp_ok", "w_ready", "w_used", "e_used", "evac_act",
                     "evac_dve", "chain2", "stage_out"]
            s = {n: sem(f"{n}_{tag}") for n in names}
            s["a2_in"] = [sem(f"a2_in{i}_{tag}") for i in range(4)]
            s["h_in"] = [sem(f"h_in{i}_{tag}") for i in range(2)]
            return type("Sems", (), s)
        S = {1: attention_sems("pos"), 2: attention_sems("any")}

        fw_in = sem("fw_in")
        bias_ok = sem("bias_ok")
        f_in = [sem(f"f_in{i}") for i in range(2)]
        den_in = sem("den_in")
        rden_ok = sem("rden_ok")
        rden_st = sem("rden_st")
        d_in = [sem(f"d_in{i}") for i in range(2)]
        f_tr = sem("f_tr")
        f_mm = sem("f_mm")
        f_act = sem("f_act")
        f_dve = sem("f_dve")
        f_std = sem("f_std")
        out_ready = sem("out_ready")
        stored = sem("stored")

        def mm_at(c, what):
            return 7 * c + ["r0", "z0", "g0", "es", "r1", "z1", "g1"].index(what) + 1

        def act_at(c, what):
            return 7 * c + ["r0", "z0", "n0", "es", "r1", "z1", "n1"].index(what) + 1

        dve_at, count = {}, 0
        for c in range(-1, NCH + 1):
            for part, of, n in (("pre0", c, 2), ("rows", c - 1, 4), ("out0", c, 3), ("pre1", c, 2), ("scaled", c + 1, 1), ("out1", c, 4)):
                if 0 <= of < NCH:
                    count += n
                    dve_at[part, of] = count

        MLP_HALF = LAYERS * 8

        def mlp_step(m):
            return m % MLP_HALF // 8, m // MLP_HALF * 4 + m % 8 // 2, m % 2

        block = ctx.enter_context(nc.Block())

        @block.sync
        def _(sp):
            with sp.Fori(0, NBLK) as C:
                with sp.Fori(0, NG) as g:
                    for k in range(G8):
                        tile = sp.snap(C * T + (g * G8 + k))
                        if k % 4 == 0:
                            x_tile = sp.snap(C * RB + (g * G8 + k))
                            sp.wait_ge(a_used_pe, C * T + g * G8 + (k + 4))
                            sp.dma_start(x_slot[k // 4], xx[bass.ds(x_tile, 4), :, :].rearrange("r p n -> p r n")).then_inc(x_in[k // 4], 16)
                        used = sp.snap(tile + 5)
                        sp.wait_ge(a_used_pe, used)
                        sp.wait_ge(a_signed, used)
                        sp.dma_start(a_slot[k % 4], a_tiles[bass.ds(tile, 1), :, :].rearrange("r p n -> p (r n)")).then_inc(a_in[k % 4], 16)
            sp.wait_ge(a_used_pe, NBLK * T + 8)
            sp.wait_ge(flag_max, 1)
            sp.dma_start(hn, x_nat.rearrange("(t p) n -> p t n", p=P)).then_inc(xn_in, 16)
            for q in range(NCH):
                sp.wait_ge(ln_ok, 4 * (q + 1))
                for t0 in (4 * q, 4 * q + T):
                    if t0 < TD:
                        sp.dma_start(h_dram[t0:t0 + 4].rearrange("r p n -> p r n"), hn[:, 4 * q:4 * q + 4, :]).then_inc(h_out, 16)
            for q in range(NCH):
                sp.wait_ge(ht_ok, q + 1)
                sp.dma_start(ht_dram[:, q * CH:(q + 1) * CH], ht[:, q * CH:(q + 1) * CH]).then_inc(ht_out, 16)
            sp.wait_ge(h_out, 16 * (NCH + (TD - T) // 4))
            sp.wait_ge(ht_out, 16 * NCH)
            sp.wait_ge(flag_ok, 1)
            has_neg = sp.value_load(flag[0:1, 0:1], min_val=0, max_val=1)

            def attention_loads(s, NS):
                sp.wait_ge(s.p_used, 2 + NBLK * T // 4)
                with sp.Fori(0, NBLK) as C:
                    for u in range(2):
                        with sp.Fori(0, NG) as g:
                            body = (C * 2 + u) * NG + g
                            for k in range(0, G8, 2):
                                tile = sp.snap(C * T + (g * G8 + k))
                                if k % 4 == 0:
                                    h_tile = sp.snap(C * RB + (g * G8 + k))
                                    sp.wait_ge(s.w_used, (body * 2 + (k // 4 + 1)) * (4 * NS * HEADS) + 3)
                                    sp.dma_start(h_slot[k // 4], h_dram[bass.ds(h_tile, 4), :, :].rearrange("r p n -> p r n")).then_inc(s.h_in[k // 4], 16)
                                sp.wait_ge(s.w_used, (body * G8 + (k + 2)) * (NS * HEADS) + 3)
                                sp.dma_start(a2_slot[k // 2], a_tiles[bass.ds(tile, 2), :, u * CH:(u + 1) * CH].rearrange("r p n -> p r n")).then_inc(s.a2_in[k // 2], 16)

            def chunk_loads(c):
                s = c % 2
                sp.dma_start(f_node[s], agg_dram[c, 3]).then_inc(f_in[s], 16)
                sp.dma_start(f_ht[s], ht_dram[:, c * CH:(c + 1) * CH]).then_inc(f_in[s], 16)
                sp.dma_start(f_num[s], agg_dram[c, 0:3].rearrange("h p n -> p h n")).then_inc(f_in[s], 16)
                sp.dma_start(f_hn[s], h_dram[4 * c:4 * c + 4].rearrange("r p n -> p r n")).then_inc(f_in[s], 16)

            def denominators(c):
                sp.dma_start(f_den[c % 2], rden_dram[:, c * CH:(c + 1) * CH].rearrange("(o h) n -> o h n", o=1).broadcast_to([P, HEADS, CH])).then_inc(d_in[c % 2], 16)

            def half_loads(half):
                p = slice(half * P // 2, (half + 1) * P // 2)
                n = slice(half * N // 2, (half + 1) * N // 2)
                sp.dma_start(den_c[p].rearrange("p g (h w) -> p (g h) w", h=HEADS), den_dram[:, :, n].rearrange("g h (p w) -> p (g h) w", w=WD)).then_inc(den_in, 16)

            def half_inverted(half):
                p = slice(half * P // 2, (half + 1) * P // 2)
                n = slice(half * N // 2, (half + 1) * N // 2)
                sp.wait_ge(rden_ok, half + 1)
                sp.dma_start(rden_dram[:, n].rearrange("h (p w) -> p h w", w=WD), den_c[p, 0, :].rearrange("p (h w) -> p h w", h=HEADS)).then_inc(rden_st, 16)
                sp.wait_ge(rden_st, 16 * (half + 1))

            def loads_ahead(s, NS):
                before = NCH - 2
                sp.wait_ge(s.rb_ready, before * T * NS)
                sp.wait_ge(s.lgs_ready, before * T * NS)
                sp.wait_ge(s.max_step, HEADS + before * T * NS * HEADS)
                sp.wait_ge(s.stage_out, (before + 1) * 16 * 6)
                sp.dma_start(gw_sb, gru_w.rearrange("g p n -> p g n")).then_inc(fw_in, 16)
                sp.dma_start(pw_sb, gat_w.rearrange("h p n -> p h n")).then_inc(fw_in, 16)
                sp.dma_start(gb_sb, gru_b).then_inc(fw_in, 16)
                half_loads(0)
                chunk_loads(0)
                chunk_loads(1)
                half_inverted(0)
                denominators(0)
                denominators(1)
                sp.wait_ge(s.stage_out, (NCH + 1) * 16 * 6)
            with sp.If(has_neg != 0):
                attention_loads(S[2], 2)
                loads_ahead(S[2], 2)
            with sp.Else():
                attention_loads(S[1], 1)
                loads_ahead(S[1], 1)
            half_loads(1)
            half_inverted(1)
            for c in range(2, NCH):
                sp.wait_ge(f_dve, dve_at["rows", c - 2])
                chunk_loads(c)
                denominators(c)
            out_v = out.rearrange("(t p) n -> p t n", p=P)
            for q in range(NCH):
                sp.wait_ge(out_ready, 4 * (q + 1))
                sp.dma_start(out_v[:, 4 * q:4 * q + 4, :], fin[:, 4 * q:4 * q + 4, :]).then_inc(stored, 16)
            sp.wait_ge(stored, 16 * NCH)

        @block.gpsimd
        def _(pool):
            nc.gpsimd.memset(ident[:, :], 0.0).then_inc(zero_ok, 1)
            nc.gpsimd.memset(ones3[:, :], 1.0).then_inc(zero_ok, 1)
            nc.gpsimd.memset(zeros[:, :], 0.0).then_inc(consts, 1)
            nc.gpsimd.memset(minus_one[:, :], -1.0).then_inc(consts, 1)
            nc.gpsimd.memset(head_col[:, :, :], 0.0).then_inc(zero_ok, 1)
            nc.gpsimd.memset(ones_row, 1.0).then_inc(consts, 1)
            pool.wait_ge(zero_ok, 3)
            for h in range(HEADS):
                ins = nc.gpsimd.memset(head_col[:, h, h:h + 1], 1.0)
            ins.then_inc(consts, 1)
            nc.gpsimd.affine_select(out=ident[:, :], in_=ident[:, :], compare_op=ALU.not_equal, fill=1.0,
                                    base=0, pattern=[[-1, P]], channel_multiplier=1).then_inc(zero_ok, 1)
            nc.gpsimd.affine_select(out=ones3[:, :], in_=ones3[:, :], compare_op=ALU.is_ge, fill=0.0,
                                    base=2, pattern=[[0, P]], channel_multiplier=-1).then_inc(consts, 1)
            pool.wait_ge(zero_ok, 4)
            nc.gpsimd.tensor_copy(ident_bf[:, :], ident[:, :]).then_inc(consts, 1)
            nc.gpsimd.tensor_copy(ident_u8[:, :], ident[:, :]).then_inc(consts, 1)
            nc.gpsimd.tensor_scalar(penalty[:, :], ident[:, :], -BIG, None, ALU.mult).then_inc(consts, 1)
            pool.wait_ge(flag_max, 1)
            nc.gpsimd.partition_all_reduce(flag_f[:, 1:2], flag_f[:, 0:1], P, bass.bass_isa.ReduceOp.max).then_inc(flag_all, 1)
        CONSTS = 8

        @block.scalar
        def _(act):
            act.dma_start(wt_sb[:, :, :], w_t.rearrange("l p n -> p l n")).then_inc(w_in, 16)
            act.dma_start(wb_sb[:, :], w_b).then_inc(w_in, 16)
            act.dma_start(wm_sb[:, :, :], wm_t.rearrange("(b p) n -> p b n", p=P)).then_inc(w_in, 16)
            act.dma_start(bm_row, bm.rearrange("(o n) -> o n", o=1)).then_inc(w_in, 16)
            act.dma_start(gwt_sb[:, :, :], gat_wt.rearrange("h p n -> p h n")).then_inc(w_in, 16)
            act.dma_start(ga_sb[:, :, :], gat_a).then_inc(w_in, 16)
            act.dma_start(d_sb[:, :], diag).then_inc(w_in, 16)
            act.dma_start(eps_sb[:, :], eps.rearrange("(o n) -> o n", o=1).broadcast_to([P, 2])).then_inc(w_in, 16)
            act.sem_inc(a_signed, 8)
            act.sem_inc(agg_out, 8)
            act.wait_ge(scale_ok, 1)
            with act.Fori(0, NBLK // 2) as Cp:
                for par in range(2):
                    with act.Fori(0, NG) as g:
                        for k in range(G8):
                            act.wait_ge(a_in[k % 4], ((Cp * 2 + par) * 8 + g * 2 + (k // 4 + 1)) * 16)
                            act.wait_ge(neg_step, (Cp * 2 + par) * T + g * G8 + (k + 2))
                            nc.scalar.activation(sgn[:, k % 2, :], a_slot[k % 4], ACT.Sign, scale=-1.0).then_inc(a_signed, 1)
                    act.wait_ge(a_used_pe, (Cp * 2 + par + 1) * T + 8)
                    for b in range(2):
                        for u in range(2):
                            nc.scalar.activation(high[:, b, bass.ds((Cp * 2 + par) * BW + u * CH, CH)], agg_ps[par][b][u][:, :],
                                                 ACT.Copy, scale=eps_sb[:, b:b + 1]).then_inc(agg_out, 1)
            for m in range(LAYERS * 16):
                layer, c, b = mlp_step(m)
                act.wait_ge(mlp_mm, m + 1)
                nc.scalar.activation(high[:, b, c * CH:(c + 1) * CH], bank[m % 4][:, :], ACT.Relu,
                                     bias=wb_sb[:, b * LAYERS + layer:b * LAYERS + layer + 1]).then_inc(mlp_act, 1)
            for half in range(2):
                act.wait_ge(var_ok, half + 1)
                t = slice(half * T // 2, (half + 1) * T // 2)
                nc.scalar.activation(rstd[:, t], rstd[:, t], ACT.Sqrt).then_inc(std_ok, 1)
            for q in range(NCH):
                act.wait_ge(ht_mm, q + 1)
                nc.scalar.activation(ht[:, q * CH:(q + 1) * CH], bank[q % 3][:, :], ACT.Copy).then_inc(ht_ok, 1)
            act.wait_ge(flag_ok, 1)
            has_neg = act.value_load(flag[0:1, 0:1], min_val=0, max_val=1)

            def edge_tiles(s, NS):
                if NS == 2:
                    act.wait_ge(h_out, 16 * (NCH + (TD - T) // 4))
                with act.Fori(0, NBLK) as C:
                    with act.Fori(0, NG) as g:
                        src = codes[:, bass.ds(C * T + g * G8, 4), :]
                        act.wait_ge(s.p_used, (C * NG + g) * 2 + 1)
                        if NS == 2:
                            nc.scalar.activation(m_slot[0], src, ACT.Relu, bias=minus_one[:, :]).then_inc(s.p_act, 1)
                        nc.scalar.activation(p_slot[0], src, ACT.Relu, scale=-1.0, bias=1.0).then_inc(s.p_act, 1)

            def attention(s, NS):
                NU = NS * HEADS
                act.sem_inc(s.exp_ok, 6)
                act.sem_inc(s.evac_act, 3)
                act.sem_inc(s.stage_out, 16 * 6)
                act.wait_ge(h_out, 16 * (NCH + (TD - T) // 4))
                act.wait_ge(ht_out, 16 * NCH)

                def max_rows(p, par, h):
                    act.wait_ge(s.parts_tr, p * HEADS + max(h + 1, 2))
                    nc.scalar.activation(mrow[par][0:3, h, :], tr_ps[0:3, (h % 2) * (CH // 2):(h % 2 + 1) * (CH // 2)].bitcast(BF16),
                                         ACT.Copy).then_inc(s.mrow_ok, 1)

                def max_to_all(p):
                    act.wait_ge(s.max_mm, p + 1)
                    nc.scalar.activation(max_all, tr_ps[:, :], ACT.Copy).then_inc(s.max_ok, 1)

                def codes_to_bf16(tile0, k, C, u, r0):
                    act.wait_ge(s.lg_ready, (tile0 + (k + 1)) * 2)
                    nc.scalar.activation(rb[k % 4], codes[:, bass.ds(C * T + r0 + k, 1), u * CH:(u + 1) * CH].rearrange("p r n -> p (r n)"),
                                         ACT.Copy).then_inc(s.rb_ready, 1)

                def body(C, u, g, closing):
                    cc = C * 2 + u
                    tile0 = (cc * NG + g) * G8

                    for k in range(G8):
                        for n in range(k * NU, (k + 1) * NU):
                            v = n % NU
                            if n % HEADS < 2:
                                act.wait_ge(s.lg_ready, tile0 * (2 * NS) + (n // HEADS * 2 + n % HEADS + 1 + 8 * NS))
                                logits_in = lg_ps[n % HEADS][:, :]
                            else:
                                act.wait_ge(s.lgs_ready, tile0 * NS + (n // HEADS + 1))
                                logits_in = lgs[n // HEADS % 2]
                            act.wait_ge(s.e_used, tile0 * NU + (n + 1))
                            nc.scalar.activation(ebuf[n % 6], logits_in, ACT.Exp,
                                                 bias=e_nat[:, bass.ds(C * RB + g * G8 + k, 1), v:v + 1].rearrange("p a b -> p (a b)")).then_inc(s.exp_ok, 1)
                        if NS == 1:
                            if closing and k + 2 >= G8:
                                codes_to_bf16(tile0, k + 2, *chunk_after(C, u, 1), -G8)
                            else:
                                codes_to_bf16(tile0, k + 2, C, u, g * G8)
                        if closing and k == 5:
                            max_rows(cc + 1, 1 - u, 0)
                            max_rows(cc + 1, 1 - u, 1)
                        if closing and k == 6:
                            max_rows(cc + 1, 1 - u, 2)

                if NS == 1:
                    codes_to_bf16(0, 0, 0, 0, 0)
                    codes_to_bf16(0, 1, 0, 0, 0)
                for h in range(HEADS):
                    max_rows(0, 0, h)
                max_to_all(0)
                with act.Fori(0, NBLK) as C:
                    for u in range(2):
                        cc = C * 2 + u
                        with act.Fori(0, NG - 1) as g:
                            body(C, u, g, False)
                        with act.Fori(NG - 1, NG) as g:
                            body(C, u, g, True)
                        max_to_all(cc + 1)
                        act.wait_ge(s.e_used, (cc + 1) * (T * NU) + 6)
                        act.wait_ge(s.stage_out, cc * (16 * 6) + 16 * 6)
                        for h in range(HEADS):
                            nc.scalar.activation(stage[h], num_ps[h][:, :], ACT.Copy).then_inc(s.evac_act, 1)
                        act.wait_ge(s.evac_act, cc * 3 + 6)
                        act.dma_start(agg_dram[bass.ds(cc, 1), 0:3].rearrange("o h p n -> p (o h) n"),
                                      low[:, 2048:2048 + 3 * CH].rearrange("p (h n) -> p h n", h=3)).then_inc(s.stage_out, 16)
                        act.wait_ge(s.evac_dve, cc * 2 + 4)
                        act.dma_start(agg_dram[bass.ds(cc, 1), 3:4].rearrange("o h p n -> p (o h n)"), stage[3]).then_inc(s.stage_out, 16)
                        for q in range(4):
                            act.dma_start(den_dram[q, :, bass.ds(cc * CH, CH)], stage[4][32 * q:32 * q + HEADS, :]).then_inc(s.stage_out, 16)
                act.wait_ge(s.max_step, HEADS + (NCH + 1) * (T * NU) + G8 * NU)
                act.wait_ge(s.lgs_ready, NCH * T * NS + 1)
                act.wait_ge(s.rb_ready, (NCH * T + 2) * NS)
            with act.If(has_neg != 0):
                edge_tiles(S[2], 2)
                attention(S[2], 2)
            with act.Else():
                edge_tiles(S[1], 1)
                attention(S[1], 1)

            act.wait_ge(bias_ok, 2)
            for c in range(NCH):
                s = c % 2
                for i in range(2):
                    bk = bank[4 * i:4 * i + 4]
                    if i == 1:
                        act.wait_ge(f_mm, mm_at(c, "es"))
                        if c >= 2:
                            act.wait_ge(f_mm, mm_at(c - 2, "g1"))
                        nc.scalar.activation(f_es[s], bank[0][:, :], ACT.Copy, scale=1.0 / HEADS).then_inc(f_act, 1)
                    if c:
                        act.wait_ge(f_dve, dve_at[f"out{i}", c - 1])
                    for j, gate in enumerate("rz"):
                        act.wait_ge(f_mm, mm_at(c, f"{gate}{i}"))
                        nc.scalar.activation((f_r, f_z)[j][i], bk[j][:, :], ACT.Sigmoid, bias=gb_sb[:, 6 * i + j:6 * i + j + 1]).then_inc(f_act, 1)
                    act.wait_ge(f_dve, dve_at[f"pre{i}", c])
                    nc.scalar.activation(f_n[i], f_t[i], ACT.Tanh, bias=gb_sb[:, 6 * i + 2:6 * i + 3]).then_inc(f_act, 1)
            act.wait_ge(var_ok, 3)
            nc.scalar.activation(rstd[:, :], rstd[:, :], ACT.Sqrt).then_inc(f_std, 1)

        @block.tensor
        def _(pe):
            pe.sem_inc(a_used_pe, 8)
            pe.wait_ge(consts, CONSTS)
            pe.wait_ge(w_in, 16 * 8)
            with pe.Fori(0, NBLK // 2) as Cp:
                for par in range(2):
                    pe.wait_ge(agg_out, (Cp * 2 + par) * 4 + 4)
                    for b in range(2):
                        for u in range(2):
                            nc.tensor.matmul(agg_ps[par][b][u][:, :], zeros[:, 0:P], zeros[:, :], start=True, stop=True, skip_group_check=True)
                    with pe.Fori(0, NG) as g:
                        for k in range(G8):
                            if k % 4 == 0:
                                pe.wait_ge(x_in[k // 4], ((Cp * 2 + par) * NG + g + 1) * 16)
                            pe.wait_ge(a_in[k % 4], ((Cp * 2 + par) * 8 + g * 2 + (k // 4 + 1)) * 16)
                            for b in range(2):
                                for u in range(2):
                                    mm = nc.tensor.matmul(agg_ps[par][b][u][:, :], x_slot[k // 4][:, k % 4, b * P:(b + 1) * P],
                                                          a_slot[k % 4][:, u * CH:(u + 1) * CH], start=False, stop=True, skip_group_check=True)
                            mm.then_inc(a_used_pe, 1)
            pe.wait_ge(agg_out, 8 + 4 * NBLK)
            def mlp(first, last):
                for m in range(first, last):
                    layer, c, b = mlp_step(m)
                    if m >= 4:
                        pe.wait_ge(mlp_act, m - 3)
                    nc.tensor.matmul(bank[m % 4][:, :], wt_sb[:, b * LAYERS + layer, :], high[:, b, c * CH:(c + 1) * CH],
                                     start=True, stop=True).then_inc(mlp_mm, 1)

            def merge(half):
                for q in range(4 * half, 4 * half + 4):
                    pe.wait_ge(mlp_act, half * MLP_HALF + 2 * 8 + 2 * (q % 4) + 2)
                    if half:
                        pe.wait_ge(res_ok, q - 3)
                    for g in range(4 * q, 4 * q + 4):
                        o = bank[4 + q % 4][:, (g % 4) * P:(g % 4 + 1) * P]
                        nc.tensor.matmul(o, high[:, 0, g * P:(g + 1) * P], wm_sb[:, 0, :], start=(g % 4 == 0), stop=True, skip_group_check=True)
                        nc.tensor.matmul(o, high[:, 1, g * P:(g + 1) * P], wm_sb[:, 1, :], start=False, stop=True, skip_group_check=True)
                        mm = nc.tensor.matmul(o, ones_row, bm_row, start=False, stop=True, skip_group_check=True)
                    mm.then_inc(mg_mm, 1)
            mlp(0, MLP_HALF + 8)
            merge(0)
            mlp(MLP_HALF + 8, 2 * MLP_HALF)
            merge(1)
            for h in range(HEADS):
                mm = nc.tensor.matmul(bank[3][:, 2 * h:2 * h + 2], gwt_sb[:, h, :], ga_sb[:, h, :], start=(h == 0), stop=True, skip_group_check=True)
            mm.then_inc(u_mm, 1)
            for half in range(2):
                for q in range(4 * half, 4 * half + 4):
                    pe.wait_ge(ln_ok, 4 * (q + 1))
                    if q >= 3:
                        pe.wait_ge(ht_ok, q - 2)
                    for g in range(4 * q, 4 * q + 4):
                        mm = nc.tensor.transpose(bank[q % 3][:, (g % 4) * P:(g % 4 + 1) * P], hn[:, g, :], ident[:, :])
                    mm.then_inc(ht_mm, 1)
                pe.wait_ge(u_ok, 1)
                for g in range(half * T // 2, (half + 1) * T // 2):
                    if g % 4 == 0:
                        pe.wait_ge(ht_ok, g // 4 + 1)
                    mm = nc.tensor.matmul(bank[3][:, 6 * g:6 * g + 6], ht[:, g * P:(g + 1) * P], u_sb[:, :, :].rearrange("p s h -> p (s h)"),
                                          start=(g == 0), stop=True, skip_group_check=True)
            mm.then_inc(v_mm, 1)
            pe.wait_ge(flag_ok, 1)
            has_neg = pe.value_load(flag[0:1, 0:1], min_val=0, max_val=1)

            def logits(s, NS):
                W = 9 * NS
                with pe.Fori(0, NBLK) as C:
                    pe.wait_ge(s.e_ps_free, C + 1)
                    nc.tensor.matmul(bank[1][:, 0:RB * W], zeros[:, 0:P], zeros[:, 0:RB * W], start=True, stop=True, skip_group_check=True)
                    with pe.Fori(0, NG) as g:
                        for k in range(G8):
                            if k % 4 == 0:
                                pe.wait_ge((s.p_act, s.p_dve)[k // 4], (C * NG + g) * NS + NS)
                            t = C * RB + g * G8 + k
                            for i in range(RB):
                                o = bank[1][:, i * W:(i + 1) * W].rearrange("p (a c) -> p a c", a=3)
                                mm = nc.tensor.matmul(o, p_slot[k // 4][:, k % 4, i * P:(i + 1) * P],
                                                      v3[:, bass.ds(t, 1), :, 0:3 * NS].rearrange("p o a c -> p (o a) c"),
                                                      start=False, stop=True, skip_group_check=True)
                                if NS == 2:
                                    for sg in range(2):
                                        mm = nc.tensor.matmul(o[:, :, 3 * sg:3 * sg + 3], m_slot[k // 4][:, k % 4, i * P:(i + 1) * P],
                                                              v3[:, bass.ds(t, 1), :, 3 - 3 * sg:6 - 3 * sg].rearrange("p o a c -> p (o a) c"),
                                                              start=False, stop=True, skip_group_check=True)
                            if k % 4 == 3:
                                mm.then_inc(s.p_used, 1)

            def attention(s, NS):
                NU = NS * HEADS
                pe.sem_inc(s.lg_ready, 8 * NS)
                pe.sem_inc(s.w_used, 8 * NU + 3)
                pe.sem_inc(s.e_used, 6)

                def turn_minima(p, h):
                    if h == 0:
                        pe.wait_ge(s.max_step, (p + 1) * (T * NU) + HEADS)
                        if not (isinstance(p, int) and p == 0):
                            pe.wait_ge(s.max_ok, p)
                    else:
                        pe.wait_ge(s.min_ok, p * HEADS + h)
                    for i in range(4):
                        mm = nc.tensor.transpose(tr_ps[:, i * P:(i + 1) * P], macc[h][:, i * P:(i + 1) * P], ident[:, :])
                    mm.then_inc(s.macc_tr, 1)

                def turn_parts(p, h):
                    if h == 0:
                        pe.wait_ge(s.parts_ok, p + 1)
                    if h == 2:
                        pe.wait_ge(s.mrow_ok, p * HEADS + 2)
                    for i in range(4):
                        o = (h % 2) * (CH // 2) + i * P // 2
                        mm = nc.tensor.transpose(tr_ps[0:3, o:o + P // 2].bitcast(BF16), mparts[:, h, i, :], ident_bf[:, :])
                    mm.then_inc(s.parts_tr, 1)

                def max_to_all(p, rows):
                    pe.wait_ge(s.mrow_ok, (p + 1) * HEADS)
                    nc.tensor.matmul(tr_ps[:, :], ones3[:, :], rows[:, 2, :], start=True, stop=True).then_inc(s.max_mm, 1)

                def logit(tile0, n, rows):
                    k, v = n // NU, n % NU
                    if v == 0 and NS == 1:
                        pe.wait_ge(s.rb_ready, tile0 + (k + 1))
                    if v % HEADS == 0 and NS == 2:
                        pe.wait_ge(s.rb_ready, (tile0 + k) * 2 + (v // HEADS + 1))
                    mask = rb[k % 4] if NS == 1 else rb[(2 * k + v // HEADS) % 4]
                    pe.wait_ge(s.exp_ok, tile0 * NU + (n + 4))
                    nc.tensor.matmul(lg_ps[v % HEADS][:, :], penalty[:, :], mask, start=True, stop=False)
                    nc.tensor.matmul(lg_ps[v % HEADS][:, :], ones3[:, :], rows[:, v % HEADS, :], start=False, stop=True).then_inc(s.lg_ready, 1)

                def body(C, u, g, closing):
                    cc = C * 2 + u
                    body_n = cc * NG + g
                    tile0 = body_n * G8
                    for k in range(G8):
                        hk = h_slot[k // 4][:, k % 4, :]
                        if k % 4 == 0:
                            pe.wait_ge(s.h_in[k // 4], (body_n + 1) * 16)
                        if k % 2 == 0:
                            pe.wait_ge(s.a2_in[k // 2], (body_n + 1) * 16)
                        if k // 4 == u:
                            pe.wait_ge(s.a2_masked, body_n * 4 + (k % 4 + 1))
                        nc.tensor.matmul(node_ps[:, :], hk, a2_slot[k // 2][:, k % 2, :], start=False, stop=True, skip_group_check=True)
                        for n in range(k * NU, (k + 1) * NU):
                            if closing and n + 2 == G8 * NU:
                                pe.wait_ge(s.mrow_ok, (cc + 1) * HEADS + 2)
                            if (n + 2) % HEADS < 2:
                                logit(tile0, n + 2, mrow[1 - u if closing and n + 2 >= G8 * NU else u])
                            pe.wait_ge(s.w_ready, tile0 * NU + (n + 1 + 8 * NU))
                            nc.tensor.matmul(num_ps[n % HEADS][:, :], hk, wbuf[n % 3], start=False, stop=True, skip_group_check=True).then_inc(s.w_used, 1)
                            if n % 4 == 3:
                                for m in range(n - 3, n + 1):
                                    q = m % 4
                                    mm = nc.tensor.matmul(den_ps[32 * q:32 * q + HEADS, :], head_col[:, m % HEADS, :], ebuf[m % 6], start=False, stop=True,
                                                          skip_group_check=True)
                                mm.then_inc(s.e_used, 4)
                            if closing and n == k * NU:
                                if k < 3:
                                    turn_minima(cc + 1, k)
                                if k == 5:
                                    turn_parts(cc + 1, 0)
                                    turn_parts(cc + 1, 1)
                                if k == 6:
                                    turn_parts(cc + 1, 2)
                                if k == 7:
                                    max_to_all(cc + 1, mrow[1 - u])

                for h in range(HEADS):
                    turn_minima(0, h)
                for h in range(HEADS):
                    turn_parts(0, h)
                max_to_all(0, mrow[0])
                logit(0, 0, mrow[0])
                logit(0, 1, mrow[0])
                with pe.Fori(0, NBLK) as C:
                    for u in range(2):
                        cc = C * 2 + u
                        pe.wait_ge(s.evac_act, cc * 3 + 3)
                        pe.wait_ge(s.evac_dve, cc * 2 + 2)
                        for b in range(5):
                            nc.tensor.matmul(bank[b][:, :], zeros[:, 0:P], zeros[:, :], start=True, stop=True, skip_group_check=True)
                        with pe.Fori(0, NG - 1) as g:
                            body(C, u, g, False)
                        with pe.Fori(NG - 1, NG) as g:
                            body(C, u, g, True)
                pe.wait_ge(s.evac_act, NCH * 3 + 3)
                pe.wait_ge(s.evac_dve, NCH * 2 + 2)
                pe.wait_ge(s.exp_ok, NCH * T * NU + 6)
                pe.wait_ge(s.max_ok, NCH + 1)
            with pe.If(has_neg != 0):
                pe.sem_inc(S[2].p_used, 2)
                pe.wait_ge(v_ok, 1)
                logits(S[2], 2)
                attention(S[2], 2)
            with pe.Else():
                pe.sem_inc(S[1].p_used, 2)
                pe.wait_ge(v_ok, 1)
                logits(S[1], 1)
                attention(S[1], 1)

            pe.wait_ge(fw_in, 48)

            def rows(c):
                pe.wait_ge(f_dve, dve_at["out1", c])
                for i in range(4):
                    mm = nc.tensor.transpose(bank[1][:, i * P:(i + 1) * P], f_o[0][c % 2][:, i * P:(i + 1) * P], ident[:, :])
                mm.then_inc(f_tr, 1)

            for c in range(NCH):
                s = c % 2
                pe.wait_ge(f_in[s], (c // 2 + 1) * 16 * 4)
                if c:
                    pe.wait_ge(f_dve, dve_at["pre0", c - 1])
                    pe.wait_ge(f_act, act_at(c - 1, "es"))
                if c >= 2:
                    pe.wait_ge(f_dve, dve_at["rows", c - 2])
                for gate in range(2):
                    nc.tensor.matmul(bank[gate][:, :], gw_sb[:, gate, :], f_node[s], start=True, stop=False)
                    nc.tensor.matmul(bank[gate][:, :], gw_sb[:, 3 + gate, :], f_ht[s], start=False, stop=True).then_inc(f_mm, 1)
                nc.tensor.matmul(bank[2][:, :], gw_sb[:, 2, :], f_node[s], start=True, stop=True)
                nc.tensor.matmul(bank[3][:, :], gw_sb[:, 5, :], f_ht[s], start=True, stop=True).then_inc(f_mm, 1)
                pe.wait_ge(f_dve, dve_at["scaled", c])
                pe.wait_ge(f_act, act_at(c, "r0"))
                for h in range(HEADS):
                    mm = nc.tensor.matmul(bank[0][:, :], pw_sb[:, h, :], f_num[s][:, h, :], start=(h == 0), stop=(h == HEADS - 1))
                mm.then_inc(f_mm, 1)
                if c:
                    pe.wait_ge(f_act, act_at(c, "z0"))
                    rows(c - 1)
                    pe.wait_ge(f_dve, dve_at["pre1", c - 1])
                for gate in range(2):
                    nc.tensor.matmul(bank[4 + gate][:, :], gw_sb[:, 9 + gate, :], f_ht[s], start=True, stop=False)
                nc.tensor.matmul(bank[7][:, :], gw_sb[:, 11, :], f_ht[s], start=True, stop=True)
                pe.wait_ge(f_act, act_at(c, "es"))
                for gate in range(2):
                    nc.tensor.matmul(bank[4 + gate][:, :], gw_sb[:, 6 + gate, :], f_es[s], start=False, stop=True).then_inc(f_mm, 1)
                nc.tensor.matmul(bank[6][:, :], gw_sb[:, 8, :], f_es[s], start=True, stop=True).then_inc(f_mm, 1)
            rows(NCH - 1)

        @block.vector
        def _(dve):
            steps = [0]

            def link(ins):
                steps[0] += 1
                ins.then_inc(chain, 1)
                dve.wait_ge(chain, steps[0])

            dve.sem_inc(neg_step, 2)
            nc.vector.memset(neg_acc, 0.0).then_inc(neg_step, 1)
            nc.vector.memset(ones_u8[:, :], 1.0).then_inc(ones_ok, 1)
            dve.wait_ge(w_in, 16 * 8)
            nc.vector.tensor_scalar(eps_sb[:, :], eps_sb[:, :], 1.0, 1.0, ALU.add, ALU.add).then_inc(scale_ok, 1)
            with dve.Fori(0, NBLK) as C:
                with dve.Fori(0, NG) as g:
                    for k in range(G8):
                        n1 = C * T + g * G8 + (k + 1)
                        dve.wait_ge(a_signed, n1 + 8)
                        nc.vector.tensor_scalar(codes[:, bass.ds(C * T + g * G8 + k, 1), :].rearrange("p r n -> p (r n)"),
                                                sgn[:, k % 2, :], 1.0, None, ALU.add)
                        dve.wait_ge(neg_step, n1 + 2)
                        nc.vector.tensor_tensor(neg_acc, neg_acc, sgn[:, k % 2, :], ALU.max).then_inc(neg_step, 1)
            dve.wait_ge(neg_step, NBLK * T + 3)
            nc.vector.tensor_reduce(flag_f[:, 0:1], neg_acc, AX.X, ALU.max).then_inc(flag_max, 1)
            dve.wait_ge(consts, CONSTS)
            dve.wait_ge(ones_ok, 1)
            for C in range(NBLK):
                for r in range(RB):
                    ins = nc.vector.copy_predicated(codes[:, C * T + r, r * P:(r + 1) * P], ident_u8[:, :], ones_u8[:, :])
            link(ins)
            dve.wait_ge(flag_all, 1)
            nc.vector.tensor_scalar(flag[0:1, 0:1], flag_f[0:1, 1:2], 0.0, None, ALU.is_gt).then_inc(flag_ok, 1)

            def statistics(q, rows):
                for i in range(4):
                    ins = nc.vector.bn_stats(bst[:, i, :], rows[:, 4 * q + i, :])
                link(ins)
                for i in range(4):
                    ins = nc.vector.bn_aggr(mv[:, 4 * q + i, :], bst[:, i, :])
                link(ins)

            def normalize(rows, first, last, std, count, ready):
                t = slice(first, last)
                link(nc.vector.tensor_scalar(rstd[:, t], mv[:, t, 1], EPS, None, ALU.add))
                dve.sem_inc(var_ok, 1)
                dve.wait_ge(std, count)
                link(nc.vector.reciprocal(rstd[:, t], rstd[:, t]))
                for t in range(first, last):
                    nc.vector.tensor_scalar(rows[:, t, :], rows[:, t, :], mv[:, t, 0:1], rstd[:, t:t + 1],
                                            ALU.subtract, ALU.mult).then_inc(ready, 1)

            dve.wait_ge(xn_in, 16)
            for half in range(2):
                for q in range(4 * half, 4 * half + 4):
                    dve.wait_ge(mg_mm, q + 1)
                    r = hn[:, 4 * q:4 * q + 4, :]
                    ins = nc.vector.tensor_tensor(r, bank[4 + q % 4][:, :].rearrange("p (t n) -> p t n", t=4), r, ALU.add)
                    link(ins)
                    dve.sem_inc(res_ok, 1)
                    statistics(q, hn)
                normalize(hn, half * T // 2, (half + 1) * T // 2, std_ok, half + 1, ln_ok)
            dve.wait_ge(u_mm, 1)
            link(nc.vector.tensor_copy(u_sb[:, :, :], bank[3][:, 0:6].rearrange("p (h s) -> p s h", s=2)))
            dve.sem_inc(u_ok, 1)
            dve.wait_ge(v_mm, 1)
            link(nc.vector.tensor_copy(v_f[:, :, :], bank[3][:, 0:6 * T].rearrange("p (t c) -> p t c", c=6)))
            for part in range(3):
                src = v_f if part == 0 else v_r
                nc.vector.tensor_copy(v3[:, T:2 * T, part, :], src[:, :, :])
                link(nc.vector.tensor_copy(v3[:, 0:T, part, :], src[:, :, :]))
                if part < 2:
                    link(nc.vector.tensor_tensor(v_r[:, :, :], src[:, :, :], v3[:, 0:T, part, :], ALU.subtract))
            dve.sem_inc(v_ok, 1)
            has_neg = dve.value_load(flag[0:1, 0:1], min_val=0, max_val=1)

            def attention(s, NS):
                NU = NS * HEADS
                PASS = T * NU
                FIN = 6
                dve.sem_inc(s.w_ready, 8 * NU)
                dve.sem_inc(s.evac_dve, 2)

                def search(p, Cs, us, r0, k, v):
                    code = codes[:, bass.ds(Cs * T + r0 + k, 1), us * CH:(us + 1) * CH].rearrange("p r n -> p (r n)")
                    e = e_sc[:, bass.ds(Cs * RB + r0 + k, 1), v:v + 1].rearrange("p a b -> p (a b)")
                    dve.wait_ge(s.max_step, p * PASS + r0 * NU + (k * NU + v + 1))
                    if v >= HEADS:
                        neg = neg_code[:, k % 2, :]
                        if v == HEADS:
                            nc.vector.tensor_scalar(neg, code, 2.0, None, ALU.is_lt).then_inc(s.rn_step, 1)
                            dve.wait_ge(s.rn_step, p * T + r0 + (k + 1))
                        code = neg
                    if v < HEADS and k == 0 and isinstance(r0, int):
                        nc.vector.tensor_scalar(macc[v], code, e, None, ALU.subtract).then_inc(s.max_step, 1)
                    else:
                        nc.vector.scalar_tensor_tensor(out=macc[v % HEADS], in0=code, scalar=e, in1=macc[v % HEADS],
                                                       op0=ALU.subtract, op1=ALU.min).then_inc(s.max_step, 1)

                def minimum(p, h):
                    dve.wait_ge(s.macc_tr, p * HEADS + (h + 1))
                    nc.vector.tensor_reduce(wmin[:, h, :], tr_ps[:, :].rearrange("p (i n) -> p i n", i=4), AX.X, ALU.min).then_inc(s.min_ok, 1)

                def parts(p, i):
                    if i == 0:
                        dve.wait_ge(s.min_ok, p * HEADS + HEADS)
                    else:
                        dve.wait_ge(s.chain2, NBLK * 5 + p * FIN + i)
                    if i == 0:
                        ins = nc.vector.scalar_tensor_tensor(out=negm[:, :, :], in0=wmin[:, :, :], scalar=0.5, in1=wmin[:, :, :], op0=ALU.is_lt, op1=ALU.mult)
                    elif i == 1:
                        ins = nc.vector.tensor_scalar(negm[:, :, :], negm[:, :, :], 1.0 / ESC, None, ALU.mult)
                    elif i % 2 == 0:
                        ins = nc.vector.tensor_copy(mparts[:, :, :, i // 2 - 1], negm[:, :, :])
                    else:
                        ins = nc.vector.tensor_tensor(negm[:, :, :], negm[:, :, :], mparts[:, :, :, i // 2 - 1], ALU.subtract)
                    ins.then_inc(s.parts_ok if i == FIN else s.chain2, 1)

                def masks(tile0, k, C, u, r0):
                    code = codes[:, bass.ds(C * T + r0 + k, 1), u * CH:(u + 1) * CH].rearrange("p r n -> p (r n)")
                    dve.wait_ge(s.lg_ready, (tile0 + (k + 3)) * 4)
                    nc.vector.tensor_scalar(rb[2 * k % 4], code, 0.0, None, ALU.is_gt).then_inc(s.rb_ready, 1)
                    nc.vector.tensor_scalar(rb[(2 * k + 1) % 4], code, 2.0, None, ALU.is_lt).then_inc(s.rb_ready, 1)

                def last_head_logits(tile0, m, C, u, r0):
                    if NS == 2:
                        dve.wait_ge(s.rb_ready, tile0 * 2 + (m + 1))
                        code = rb[m % 4]
                    else:
                        code = codes[:, bass.ds(C * T + r0 + m, 1), u * CH:(u + 1) * CH].rearrange("p r n -> p (r n)")
                    dve.wait_ge(s.exp_ok, tile0 * NU + (m * HEADS + 3))
                    nc.vector.scalar_tensor_tensor(out=lgs[m % 2], in0=code, scalar=-BIG, in1=max_all, op0=ALU.mult, op1=ALU.add).then_inc(s.lgs_ready, 1)

                def body(C, u, g, closing):
                    cc = C * 2 + u
                    body_n = cc * NG + g
                    tile0 = body_n * G8

                    for k in range(G8):
                        if k % 2 == 0:
                            dve.wait_ge(s.a2_in[k // 2], (body_n + 1) * 16)
                        if k // 4 == u:
                            i = k % 4
                            d = a2_slot[k // 2][:, k % 2, i * P:(i + 1) * P]
                            nc.vector.tensor_tensor(d, d, off_diag[:, bass.ds(g, 1), :].rearrange("p o n -> p (o n)"), ALU.mult).then_inc(s.a2_masked, 1)
                            dve.wait_ge(s.a2_masked, body_n * 4 + (i + 1))
                        for n in range(k * NU, (k + 1) * NU):
                            v = n % NU
                            dve.wait_ge(s.exp_ok, tile0 * NU + (n + 7))
                            dve.wait_ge(s.w_used, tile0 * NU + (n + 1 + 8 * NU))
                            nc.vector.tensor_tensor(wbuf[n % 3], ebuf[n % 6], a2_slot[k // 2][:, k % 2, :], ALU.mult).then_inc(s.w_ready, 1)
                            if v % HEADS == 1 and not (closing and n // HEADS + 1 == G8 * NS):
                                last_head_logits(tile0, n // HEADS + 1, C, u, g * G8)
                            if not closing:
                                search(cc + 1, *chunk_after(C, u, 1), g * G8 + G8, k, v)
                            elif k < 3:
                                if v == NU - 1:
                                    minimum(cc + 1, k)
                            elif k == 3:
                                if v < 3:
                                    parts(cc + 1, 2 * v)
                                    parts(cc + 1, 2 * v + 1)
                            else:
                                if n == 4 * NU:
                                    parts(cc + 1, FIN)
                                for j in range(2 * (n - 4 * NU), 2 * (n - 4 * NU) + 2):
                                    search(cc + 2, *chunk_after(C, u, 2), 0, j // NU, j % NU)
                        if NS == 2:
                            if closing and k + 2 >= G8:
                                masks(tile0, k + 2, *chunk_after(C, u, 1), -G8)
                            else:
                                masks(tile0, k + 2, C, u, g * G8)

                def edge_tiles(C, g):
                    src = codes[:, bass.ds(C * T + g * G8 + 4, 4), :]
                    dve.wait_ge(s.p_used, (C * NG + g) * 2 + 2)
                    if NS == 2:
                        nc.vector.tensor_scalar(m_slot[1], src, 1.0, None, ALU.is_gt).then_inc(s.p_dve, 1)
                    nc.vector.tensor_scalar(p_slot[1], src, 1.0, None, ALU.is_lt).then_inc(s.p_dve, 1)

                def node_logits(C):
                    dve.wait_ge(s.p_used, (C + 1) * 2 * NG + 2)
                    c3 = slice(0, 3 * NS)
                    n = [0]

                    def step(ins):
                        n[0] += 1
                        ins.then_inc(s.chain2, 1)
                        dve.wait_ge(s.chain2, C * 5 + n[0])
                    step(nc.vector.tensor_copy(e_tmp[:, :, :, c3], bank[1][:, 0:RB * 9 * NS].rearrange("p (i a c) -> p i a c", i=RB, a=3)))
                    dve.sem_inc(s.e_ps_free, 1)
                    step(nc.vector.tensor_tensor(e_tmp[:, :, 1, c3], e_tmp[:, :, 1, c3], e_tmp[:, :, 2, c3], ALU.add))
                    step(nc.vector.tensor_tensor(e_tmp[:, :, 0, c3], e_tmp[:, :, 0, c3], e_tmp[:, :, 1, c3], ALU.add))
                    for dup in range(2):
                        t8 = bass.ds(C * RB + dup * T, RB)
                        ins = nc.vector.scalar_tensor_tensor(out=e_nat[:, t8, c3], in0=e_tmp[:, :, 0, c3], scalar=ALPHA,
                                                             in1=e_tmp[:, :, 0, c3], op0=ALU.mult, op1=ALU.max)
                    step(ins)
                    for dup in range(2):
                        t8 = bass.ds(C * RB + dup * T, RB)
                        ins = nc.vector.tensor_scalar(e_sc[:, t8, c3], e_nat[:, t8, c3], ESC, None, ALU.mult)
                    step(ins)

                dve.sem_inc(s.e_ps_free, 1)
                dve.wait_ge(h_out, 16 * (NCH + (TD - T) // 4))
                with dve.Fori(0, NG) as g:
                    edge_tiles(0, g)
                dve.wait_ge(ht_out, 16 * NCH)
                nc.vector.memset(off_diag[:, 1:NG, :], 1.0)
                nc.vector.tensor_scalar(off_diag[:, 0, :], ident[:, :], 0.0, None, ALU.is_equal)
                for b in range(2):
                    nc.vector.memset(mrow[b], 0.0)
                for h in range(HEADS):
                    nc.vector.memset(macc[h], 4.0).then_inc(s.max_step, 1)
                node_logits(0)
                with dve.Fori(1, NBLK) as C:
                    with dve.Fori(0, NG) as g:
                        edge_tiles(C, g)
                        for j in range(2 * NU):
                            search(0, 0, 0, (C - 1) * RB + g * 2, j // NU, j % NU)
                    node_logits(C)
                with dve.Fori(0, 2) as g:
                    for j in range(G8 // 2 * NU):
                        search(0, 0, 0, g * (G8 // 2) + (T - RB), j // NU, j % NU)
                for h in range(HEADS):
                    minimum(0, h)
                for i in range(FIN + 1):
                    parts(0, i)
                for j in range(G8 * NU):
                    search(1, 0, 1, 0, j // NU, j % NU)
                if NS == 2:
                    masks(0, 0, 0, 0, 0)
                    masks(0, 1, 0, 0, 0)
                dve.wait_ge(s.max_ok, 1)
                last_head_logits(0, 0, 0, 0, 0)
                with dve.Fori(0, NBLK) as C:
                    for u in range(2):
                        cc = C * 2 + u
                        with dve.Fori(0, NG - 1) as g:
                            body(C, u, g, False)
                        with dve.Fori(NG - 1, NG) as g:
                            body(C, u, g, True)
                        dve.wait_ge(s.e_used, (cc + 1) * (T * NU) + 6)
                        dve.wait_ge(s.stage_out, cc * (16 * 6) + 16 * 6)
                        nc.vector.tensor_copy(stage[3], node_ps[:, :]).then_inc(s.evac_dve, 1)
                        nc.vector.tensor_copy(stage[4], den_ps[:, :]).then_inc(s.evac_dve, 1)
                        dve.wait_ge(s.max_ok, cc + 2)
                        last_head_logits((cc + 1) * T, 0, *chunk_after(C, u, 1), 0)
            with dve.If(has_neg != 0):
                attention(S[2], 2)
            with dve.Else():
                attention(S[1], 1)

            def invert(half):
                d = den_c[half * P // 2:(half + 1) * P // 2]
                dve.wait_ge(den_in, 16 * (half + 1))
                link(nc.vector.tensor_tensor(d[:, 0:2, :], d[:, 0:2, :], d[:, 2:4, :], ALU.add))
                link(nc.vector.tensor_tensor(d[:, 0, :], d[:, 0, :], d[:, 1, :], ALU.add))
                link(nc.vector.tensor_scalar(d[:, 0, :], d[:, 0, :], 1e-30, None, ALU.max))
                nc.vector.reciprocal(d[:, 0, :], d[:, 0, :]).then_inc(rden_ok, 1)
            invert(0)
            dve.wait_ge(fw_in, 48)
            for i in range(2):
                b = gb_sb[:, 6 * i:6 * i + 2]
                nc.vector.tensor_tensor(b, b, gb_sb[:, 6 * i + 4:6 * i + 6], ALU.add).then_inc(bias_ok, 1)
            done = [0]

            def step(ins):
                done[0] += 1
                ins.then_inc(f_dve, 1)
                dve.wait_ge(f_dve, done[0])

            def scaled(c):
                s = c % 2
                dve.wait_ge(f_in[s], (c // 2 + 1) * 16 * 4)
                dve.wait_ge(d_in[s], (c // 2 + 1) * 16)
                step(nc.vector.tensor_tensor(f_num[s], f_num[s], f_den[s], ALU.mult))

            def pre(c, i):
                dve.wait_ge(f_mm, mm_at(c, f"g{i}"))
                dve.wait_ge(f_act, act_at(c, f"r{i}"))
                step(nc.vector.scalar_tensor_tensor(out=f_t[i], in0=bank[4 * i + 3][:, :], scalar=gb_sb[:, 6 * i + 3:6 * i + 4], in1=f_r[i],
                                                    op0=ALU.add, op1=ALU.mult))
                step(nc.vector.tensor_tensor(f_t[i], bank[4 * i + 2][:, :], f_t[i], ALU.add))

            def cell_out(c, i):
                s = c % 2
                dve.wait_ge(f_act, act_at(c, f"n{i}"))
                step(nc.vector.tensor_tensor(f_t[i], f_ht[s], f_n[i], ALU.subtract))
                step(nc.vector.tensor_tensor(f_t[i], f_t[i], f_z[i], ALU.mult))
                step(nc.vector.tensor_tensor(f_o[i][s], f_n[i], f_t[i], ALU.add))
                if i:
                    step(nc.vector.tensor_tensor(f_o[0][s], f_o[0][s], f_o[1][s], ALU.add))

            def rows(c):
                dve.wait_ge(f_tr, c + 1)
                for i in range(4):
                    t = 4 * c + i
                    ins = nc.vector.scalar_tensor_tensor(out=fin[:, t, :], in0=bank[1][:, i * P:(i + 1) * P], scalar=d_sb[:, t:t + 1],
                                                         in1=f_hn[c % 2][:, i, :], op0=ALU.mult, op1=ALU.add)
                    if i < 3:
                        done[0] += 1
                        ins.then_inc(f_dve, 1)
                step(ins)
                statistics(c, fin)

            scaled(0)
            for c in range(NCH):
                if c == 1:
                    invert(1)
                pre(c, 0)
                if c:
                    rows(c - 1)
                cell_out(c, 0)
                pre(c, 1)
                if c + 1 < NCH:
                    scaled(c + 1)
                cell_out(c, 1)
            rows(NCH - 1)
            normalize(fin, 0, T, f_std, 1, out_ready)


def kernel(x, adj, L0_gnn_x2, L0_gnn_eps1, L0_gnn_eps2, L0_gnn_W1, L0_gnn_b1, L0_gnn_W2, L0_gnn_b2, L0_gnn_Wm, L0_gnn_bm,
           L1_gnn_gat_W, L1_gnn_gat_a, L1_gnn_edge_Wih, L1_gnn_edge_Whh, L1_gnn_edge_bih, L1_gnn_edge_bhh,
           L1_gnn_node_Wih, L1_gnn_node_Whh, L1_gnn_node_bih, L1_gnn_node_bhh):
    import numpy as np
    from concourse import bacc
    from concourse.bass_utils import run_bass_kernel_spmd

    def gates(w):
        return [w[g * P:(g + 1) * P].T for g in range(3)]
    adj = np.asarray(adj)
    at = adj.T.reshape(T, P, NBLK, BW)
    a_tiles = np.concatenate([np.roll(at[:, :, C], -RB * C, axis=0) for C in range(NBLK)])
    both = np.concatenate([np.asarray(x), np.asarray(L0_gnn_x2)], axis=1).reshape(T, P, 2 * P)
    arrays = dict(
        a_tiles=a_tiles,
        xx=np.concatenate([both, both[:TD - T]]),
        x_nat=np.asarray(x),
        diag=np.diagonal(adj).reshape(T, P).T,
        eps=np.concatenate([L0_gnn_eps1, L0_gnn_eps2]),
        w_t=np.concatenate([L0_gnn_W1, L0_gnn_W2]).transpose(0, 2, 1),
        w_b=np.concatenate([L0_gnn_b1, L0_gnn_b2]).T,
        wm_t=np.asarray(L0_gnn_Wm).T,
        bm=np.asarray(L0_gnn_bm),
        gat_w=np.asarray(L1_gnn_gat_W),
        gat_wt=np.asarray(L1_gnn_gat_W).transpose(0, 2, 1),
        gat_a=np.asarray(L1_gnn_gat_a).reshape(HEADS, 2, P).transpose(2, 0, 1),
        gru_w=np.stack(gates(np.asarray(L1_gnn_edge_Wih)) + gates(np.asarray(L1_gnn_edge_Whh))
                       + gates(np.asarray(L1_gnn_node_Wih)) + gates(np.asarray(L1_gnn_node_Whh))),
        gru_b=np.stack([np.asarray(b)[g * P:(g + 1) * P] for bi, bh in ((L1_gnn_edge_bih, L1_gnn_edge_bhh), (L1_gnn_node_bih, L1_gnn_node_bhh))
                        for b, g in ((bi, 0), (bi, 1), (bi, 2), (bh, 2), (bh, 0), (bh, 1))]).T,
    )
    arrays = {k: np.ascontiguousarray(v) for k, v in arrays.items()}
    nc = bacc.Bacc("TRN2", target_bir_lowering=False, num_devices=1)
    aps = {k: nc.dram_tensor(k, v.shape, F32, kind="ExternalInput").ap() for k, v in arrays.items()}
    out = nc.dram_tensor("out", (N, P), F32, kind="ExternalOutput").ap()
    build(nc, **aps, out=out)
    return run_bass_kernel_spmd(nc, [arrays], core_ids=[0]).results[0]["out"]
```

```python
import numpy as np
import concourse.bass as bass
from concourse import mybir
from contextlib import ExitStack

F32 = mybir.dt.float32
F32R = mybir.dt.float32r
BF16 = mybir.dt.bfloat16
U8 = mybir.dt.uint8
I32 = mybir.dt.int32
ALU = mybir.AluOpType
ACT = mybir.ActivationFunctionType
AX = mybir.AxisListType

P = 128
N = 4096
T = N // P
BW = 1024
NBLK = N // BW
CH = 512
NCH = N // CH
RB = BW // P
TD = T + RB * (NBLK - 1)
HEADS = 3
LAYERS = 3
EPS = 1e-5
G8 = 8
NG = T // G8
BIG = 2.0 ** 100
ESC = 2.0 ** -40
ALPHA = 0.2
STORES = 3 * 16


def chunk_after(C, u, n):
    return (C, 1) if (u, n) == (0, 1) else ((C + 1) % NBLK, (u + n) % 2)


def build(nc, a_tiles, xx, x_nat, diag, eps, w_t, w_b, wm_t, bm, gat_w, gat_wt, gat_a,
          gru_w, gru_b, out):
    h_dram = nc.dram_tensor("h_dram", (TD, P, P), F32, kind="Internal").ap()
    ht_dram = nc.dram_tensor("ht_dram", (P, N), F32, kind="Internal").ap()
    den_dram = nc.dram_tensor("den_dram", (P, N), F32, kind="Internal").ap()
    rden_dram = nc.dram_tensor("rden_dram", (HEADS, N), F32, kind="Internal").ap()
    agg_dram = nc.dram_tensor("agg_dram", (NCH, 4, P, CH), F32, kind="Internal").ap()

    ctx = ExitStack()
    with ctx:
        def sb(name, shape, dt):
            return ctx.enter_context(nc.sbuf_tensor(name, shape, dt))

        def sem(name):
            return ctx.enter_context(nc.semaphore(name))

        codes = sb("codes", [P, NBLK * T, BW], U8)
        with ExitStack() as first_layer:
            def over(name, shape, dt=F32R):
                return first_layer.enter_context(nc.sbuf_tensor(name, shape, dt))
            over("over_ring_low", [P, 6144], F32)
            a_parts = [over(f"a_parts{i}", [P, 2, CH]) for i in range(2)]
            over("over_high0", [P, N - 1024], F32)
            a_parts.append(over("a_parts2", [P, 2, CH]))
            over("over_high1", [P, N - 1024], F32)
            a_parts.append(over("a_parts3", [P, 2, CH]))
            x_parts = over("x_parts", [P, 2, 2, 2 * P])
        ring = sb("ring", [P, 4 * BW], F32)
        low = sb("low", [P, 4096], F32)
        high = sb("high", [P, 2, N], F32)
        v3 = sb("v3", [P, 64, 3, 6], BF16)
        e_nat = sb("e_nat", [P, 64, 6], F32)
        e_sc = sb("e_sc", [P, 64, 6], F32)
        weights = sb("weights", [P, 13 * P], F32)
        wt_sb = weights[:, 0:6 * P].rearrange("p (l n) -> p l n", l=2 * LAYERS)
        gwt_sb = weights[:, 6 * P:9 * P].rearrange("p (h n) -> p h n", h=HEADS)
        wm_sb = weights[:, 9 * P:11 * P].rearrange("p (b n) -> p b n", b=2)
        bm_row = weights[0:1, 11 * P:12 * P]
        ones_row = weights[0:1, 12 * P:13 * P]
        wb_sb = sb("wb_sb", [P, 2 * LAYERS], F32)
        ga_sb = sb("ga_sb", [P, HEADS, 2], F32)
        eps_sb = sb("eps_sb", [P, 2], F32)
        u_sb = sb("u_sb", [P, 2, HEADS], F32)
        ident = sb("ident", [P, P], F32)
        ident_bf = sb("ident_bf", [P, P], BF16)
        ident_u8 = sb("ident_u8", [P, P], U8)
        penalty = sb("penalty", [P, P], BF16)
        ones3 = sb("ones3", [P, P], BF16)
        zeros = sb("zeros", [P, CH], BF16)
        minus_one = sb("minus_one", [P, 1], F32)
        head_col = sb("head_col", [P, HEADS, HEADS], F32)
        v_f, v_r = (high[:, 1, i * 6 * T:(i + 1) * 6 * T].rearrange("p (t c) -> p t c", c=6) for i in range(2))
        e_tmp = weights[:, 0:RB * 18].rearrange("p (i a c) -> p i a c", i=RB, a=3)
        mv = sb("mv", [P, T, 2], F32)
        rstd = sb("rstd", [P, T], F32)
        bst = sb("bst", [P, 4, 6], F32)
        wmin = sb("wmin", [P, HEADS, 4], F32)
        negm = sb("negm", [P, HEADS, 4], F32)
        off_diag = weights[:, 8 * P:10 * P].bitcast(BF16).rearrange("p (g n) -> p g n", g=NG)
        neg_code = weights[:, 10 * P:12 * P].bitcast(U8).rearrange("p (s n) -> p s n", s=2)
        ones_u8 = sb("ones_u8", [P, P], U8)
        mparts = sb("mparts", [P, HEADS, 4, 3], BF16)
        flag_f = sb("flag_f", [P, 2], F32)
        flag = sb("flag", [1, 1], I32)
        d_sb = sb("d_sb", [P, T], F32)

        a_slot = [ring[:, s * BW:(s + 1) * BW] for s in range(4)]
        x_slot = [low[:, s * 256:(s + 1) * 256] for s in range(2)]
        sgn = low[:, 512:1536].bitcast(BF16).rearrange("p (s n) -> p s n", s=2)
        code_bits = low[:, 1536:2048].bitcast(I32)
        hn = low[:, :].rearrange("p (t n) -> p t n", t=T)
        ht = high[:, 0, :]
        p_slot = [ring[:, s * 2048:(s + 1) * 2048].bitcast(BF16).rearrange("p (r n) -> p r n", r=4) for s in range(2)]
        m_slot = [low[:, s * 2048:(s + 1) * 2048].bitcast(BF16).rearrange("p (r n) -> p r n", r=4) for s in range(2)]
        a2_slot = [ring[:, s * 1024:(s + 1) * 1024].rearrange("p (r n) -> p r n", r=2) for s in range(4)]
        h_slot = [low[:, s * 512:(s + 1) * 512].rearrange("p (r n) -> p r n", r=4) for s in range(2)]
        rb = [low[:, 1024 + s * 256:1024 + (s + 1) * 256].bitcast(BF16) for s in range(4)]
        stage = [low[:, 2048 + s * CH:2048 + (s + 1) * CH] for s in range(4)] + [high[:, 1, 3584:4096]]
        ebuf = [high[:, 0, s * CH:(s + 1) * CH] for s in range(6)]
        macc = [high[:, 0, 3072:3584], high[:, 0, 3584:4096], high[:, 1, 0:512]]
        wbuf = [high[:, 1, 512 + s * CH:512 + (s + 1) * CH] for s in range(3)]
        mrow = [high[:, 1, 2048 + s * 768:2048 + (s + 1) * 768].bitcast(BF16).rearrange("p (h n) -> p h n", h=HEADS) for s in range(2)]
        lgs = [weights[:, s * CH:(s + 1) * CH] for s in range(2)]
        max_all = v3[:, :, :, :].rearrange("p t a c -> p (t a c)")[:, 0:2 * CH].bitcast(F32)
        fcodes = codes[:, :, :].rearrange("p t n -> p (t n)").bitcast(F32)
        at = [T * BW // 4]

        def last(n):
            at[0] += n
            return fcodes[:, at[0] - n:at[0]]
        gw_sb = last(12 * P).rearrange("p (g n) -> p g n", g=12)
        pw_sb = last(HEADS * P).rearrange("p (h n) -> p h n", h=HEADS)
        gb_sb = last(12)
        at[0] += 4
        f_num = [last(3 * CH).rearrange("p (h n) -> p h n", h=3) for _ in range(2)]
        f_node = [last(CH) for _ in range(2)]
        f_ht = [last(CH) for _ in range(2)]
        f_hn = [last(CH).rearrange("p (t n) -> p t n", t=4) for _ in range(2)]
        WD = N // P
        den_c = last(4 * HEADS * WD).rearrange("p (g n) -> p g n", g=4)
        f_den = [last(3 * CH).rearrange("p (h n) -> p h n", h=3) for _ in range(2)]
        assert at[0] <= 3 * T * BW // 4
        f_es = [last(CH) for _ in range(2)]
        f_r, f_z, f_t, f_n = ([last(CH) for _ in range(2)] for _ in range(4))
        f_o = [[last(CH) for _ in range(2)] for _ in range(2)]
        fin = last(N).rearrange("p (t n) -> p t n", t=T)
        assert at[0] <= NBLK * T * BW // 4

        bank = [ctx.enter_context(nc.psum_tensor(f"bank{i}", [P, CH], F32)) for i in range(8)]
        agg_ps = [[[bank[4 * par + 2 * b + u] for u in range(2)] for b in range(2)] for par in range(2)]
        num_ps, node_ps, den_ps, lg_ps, tr_ps = bank[0:3], bank[3], bank[4], bank[5:7], bank[7]

        w_in = sem("w_in")
        eps_in = sem("eps_in")
        consts = sem("consts")
        shapes_step = sem("shapes_step")
        scale_ok = sem("scale_ok")
        a_in = [sem(f"a_in{s}") for s in range(4)]
        x_in = [sem(f"x_in{s}") for s in range(2)]
        halves_used = sem("halves_used")
        x_high = sem("x_high")
        x_parted = sem("x_parted")
        a_high = sem("a_high")
        a_parted = sem("a_parted")
        a_signed = sem("a_signed")
        coded = sem("coded")
        bits_step = sem("bits_step")
        ones_ok = sem("ones_ok")
        agg_out = sem("agg_out")
        flag_max = sem("flag_max")
        flag_all = sem("flag_all")
        flag_ok = sem("flag_ok")
        mlp_mm = sem("mlp_mm")
        mlp_act = sem("mlp_act")
        xn_in = sem("xn_in")
        mg_mm = sem("mg_mm")
        res_ok = sem("res_ok")
        var_ok = sem("var_ok")
        std_ok = sem("std_ok")
        ln_ok = sem("ln_ok")
        chain = sem("chain")
        h_out = sem("h_out")
        ht_mm = sem("ht_mm")
        ht_ok = sem("ht_ok")
        ht_out = sem("ht_out")
        u_mm = sem("u_mm")
        u_ok = sem("u_ok")
        v_mm = sem("v_mm")
        v_ok = sem("v_ok")

        def attention_sems(tag):
            names = [
                "p_act", "p_dve", "p_used",
                "e_ps_free", "chain2",
                "max_step", "rn_step",
                "macc_tr", "min_ok",
                "parts_ok", "parts_tr", "mrow_ok",
                "max_mm", "max_ok",
                "rb_ready", "lg_ready", "lgs_ready",
                "exp_ok", "a2_masked",
                "w_ready", "w_used", "e_used",
                "evac_act", "evac_dve",
                "stage_out", "stage_free"]
            s = {n: sem(f"{n}_{tag}") for n in names}
            s["a2_in"] = [sem(f"a2_in{i}_{tag}") for i in range(4)]
            s["h_in"] = [sem(f"h_in{i}_{tag}") for i in range(2)]
            return type("Sems", (), s)
        S = {1: attention_sems("pos"), 2: attention_sems("any")}

        fw_in = sem("fw_in")
        bias_ok = sem("bias_ok")
        f_in = [sem(f"f_in{i}") for i in range(2)]
        hn_in = [sem(f"hn_in{i}") for i in range(2)]
        den_in = sem("den_in")
        rden_ok = sem("rden_ok")
        rden_st = sem("rden_st")
        d_in = [sem(f"d_in{i}") for i in range(2)]
        f_tr = sem("f_tr")
        f_mm = sem("f_mm")
        f_act = sem("f_act")
        f_dve = sem("f_dve")
        f_std = sem("f_std")
        out_ready = sem("out_ready")
        stored = sem("stored")

        def mm_at(c, what):
            return 7 * c + ["r0", "z0", "g0", "es", "r1", "z1", "g1"].index(what) + 1

        def act_at(c, what):
            return 7 * c + ["r0", "z0", "n0", "es", "r1", "z1", "n1"].index(what) + 1

        dve_at, count = {}, 0
        for c in range(-1, NCH + 1):
            for part, of, n in (("pre0", c, 2), ("rows", c - 1, 4), ("out0", c, 3), ("pre1", c, 2), ("scaled", c + 1, 1), ("out1", c, 4)):
                if 0 <= of < NCH:
                    count += n
                    dve_at[part, of] = count

        MLP_HALF = LAYERS * 8

        def mlp_step(m):
            return m % MLP_HALF // 8, m // MLP_HALF * 4 + m % 8 // 2, m % 2

        block = ctx.enter_context(nc.Block())

        @block.sync
        def _(sp):
            with sp.Fori(0, NBLK) as C:
                with sp.Fori(0, NG) as g:
                    for k in range(G8):
                        tile = sp.snap(C * T + (g * G8 + k))
                        x_tile = sp.snap(C * RB + (g * G8 + k))
                        x_free, signed, parted = sp.snap(tile + 1), sp.snap(tile + 5), sp.snap(tile * 2 + 2)
                        sp.wait_ge(x_parted, x_free)
                        sp.dma_start(x_slot[k % 2], xx[bass.ds(x_tile, 1), :, :].rearrange("r p n -> p (r n)")).then_inc(x_in[k % 2], 16)
                        sp.wait_ge(a_signed, signed)
                        sp.wait_ge(a_parted, parted)
                        sp.dma_start(a_slot[k % 4], a_tiles[bass.ds(tile, 1), :, :].rearrange("r p n -> p (r n)")).then_inc(a_in[k % 4], 16)
            sp.wait_ge(halves_used, NBLK * T * 2 + 4)
            sp.wait_ge(flag_max, 1)
            sp.dma_start(hn, x_nat.rearrange("(t p) n -> p t n", p=P)).then_inc(xn_in, 16)
            for q in range(NCH):
                sp.wait_ge(ln_ok, 4 * (q + 1))
                for t0 in (4 * q, 4 * q + T):
                    if t0 < TD:
                        sp.dma_start(h_dram[t0:t0 + 4].rearrange("r p n -> p r n"), hn[:, 4 * q:4 * q + 4, :]).then_inc(h_out, 16)
            for q in range(NCH):
                sp.wait_ge(ht_ok, q + 1)
                sp.dma_start(ht_dram[:, q * CH:(q + 1) * CH], ht[:, q * CH:(q + 1) * CH]).then_inc(ht_out, 16)
            sp.wait_ge(h_out, 16 * (NCH + (TD - T) // 4))
            sp.wait_ge(ht_out, 16 * NCH)
            sp.wait_ge(flag_ok, 1)
            has_neg = sp.value_load(flag[0:1, 0:1], min_val=0, max_val=1)

            def attention_loads(s, NS):
                sp.wait_ge(s.p_used, 2 + NBLK * T // 4)
                with sp.Fori(0, NBLK) as C:
                    for u in range(2):
                        with sp.Fori(0, NG) as g:
                            body = (C * 2 + u) * NG + g
                            for k in range(0, G8, 2):
                                tile = sp.snap(C * T + (g * G8 + k))
                                if k % 4 == 0:
                                    h_tile = sp.snap(C * RB + (g * G8 + k))
                                    sp.wait_ge(s.w_used, (body * 2 + (k // 4 + 1)) * (4 * NS * HEADS) + 3)
                                    sp.dma_start(h_slot[k // 4], h_dram[bass.ds(h_tile, 4), :, :].rearrange("r p n -> p r n")).then_inc(s.h_in[k // 4], 16)
                                sp.wait_ge(s.w_used, (body * G8 + (k + 2)) * (NS * HEADS) + 3)
                                sp.dma_start(a2_slot[k // 2], a_tiles[bass.ds(tile, 2), :, u * CH:(u + 1) * CH].rearrange("r p n -> p r n")).then_inc(s.a2_in[k // 2], 16)

            def chunk_loads(c):
                s = c % 2
                if c >= 2:
                    sp.wait_ge(f_dve, dve_at["out1", c - 2])
                sp.dma_start(f_node[s], agg_dram[c, 3]).then_inc(f_in[s], 16)
                sp.dma_start(f_ht[s], ht_dram[:, c * CH:(c + 1) * CH]).then_inc(f_in[s], 16)
                sp.dma_start(f_num[s], agg_dram[c, 0:3].rearrange("h p n -> p h n")).then_inc(f_in[s], 16)

            def row_loads(c):
                if c >= 2:
                    sp.wait_ge(f_dve, dve_at["rows", c - 2])
                sp.dma_start(f_hn[c % 2], h_dram[4 * c:4 * c + 4].rearrange("r p n -> p r n")).then_inc(hn_in[c % 2], 16)

            def denominators(c):
                sp.dma_start(f_den[c % 2], rden_dram[:, c * CH:(c + 1) * CH].rearrange("(o h) n -> o h n", o=1).broadcast_to([P, HEADS, CH])).then_inc(d_in[c % 2], 16)

            def half_loads(half):
                p = slice(half * P // 2, (half + 1) * P // 2)
                n = slice(half * N // 2, (half + 1) * N // 2)
                for q in range(4):
                    sp.dma_start(den_c[p, q, :].rearrange("p (h w) -> p h w", h=HEADS),
                                 den_dram[32 * q:32 * q + HEADS, n].rearrange("h (p w) -> p h w", w=WD)).then_inc(den_in, 16)

            def half_inverted(half):
                p = slice(half * P // 2, (half + 1) * P // 2)
                n = slice(half * N // 2, (half + 1) * N // 2)
                sp.wait_ge(rden_ok, half + 1)
                sp.dma_start(rden_dram[:, n].rearrange("h (p w) -> p h w", w=WD), den_c[p, 0, :].rearrange("p (h w) -> p h w", h=HEADS)).then_inc(rden_st, 16)
                sp.wait_ge(rden_st, 16 * (half + 1))

            def loads_ahead(s, NS):
                before = NCH - 2
                sp.wait_ge(s.rb_ready, before * T * NS)
                sp.wait_ge(s.lgs_ready, before * T * NS)
                sp.wait_ge(s.max_step, HEADS + before * T * NS * HEADS)
                sp.wait_ge(s.stage_out, before * STORES)
                sp.dma_start(gw_sb, gru_w.rearrange("g p n -> p g n")).then_inc(fw_in, 16)
                sp.dma_start(pw_sb, gat_w.rearrange("h p n -> p h n")).then_inc(fw_in, 16)
                sp.dma_start(gb_sb, gru_b).then_inc(fw_in, 16)
                half_loads(0)
                for c in range(2):
                    chunk_loads(c)
                    row_loads(c)
                half_inverted(0)
                denominators(0)
                denominators(1)
                sp.wait_ge(s.stage_out, NCH * STORES)
            with sp.If(has_neg != 0):
                attention_loads(S[2], 2)
                loads_ahead(S[2], 2)
            with sp.Else():
                attention_loads(S[1], 1)
                loads_ahead(S[1], 1)
            half_loads(1)
            half_inverted(1)
            for c in range(2, NCH):
                chunk_loads(c)
                denominators(c)
                row_loads(c)
            out_v = out.rearrange("(t p) n -> p t n", p=P)
            for q in range(NCH):
                sp.wait_ge(out_ready, 4 * (q + 1))
                sp.dma_start(out_v[:, 4 * q:4 * q + 4, :], fin[:, 4 * q:4 * q + 4, :]).then_inc(stored, 16)
            sp.wait_ge(stored, 16 * NCH)

        @block.gpsimd
        def _(pool):
            pool.dma_start(eps_sb[:, :], eps.rearrange("(o n) -> o n", o=1).broadcast_to([P, 2])).then_inc(eps_in, 16)
            nc.gpsimd.memset(ident[:, :], 0.0).then_inc(shapes_step, 1)
            nc.gpsimd.memset(ones3[:, :], 1.0).then_inc(shapes_step, 1)
            nc.gpsimd.memset(zeros[:, :], 0.0).then_inc(consts, 1)
            nc.gpsimd.memset(minus_one[:, :], -1.0).then_inc(consts, 1)
            nc.gpsimd.memset(head_col[:, :, :], 0.0).then_inc(shapes_step, 1)
            nc.gpsimd.memset(ones_row, 1.0).then_inc(consts, 1)
            pool.wait_ge(shapes_step, 3)
            for h in range(HEADS):
                ins = nc.gpsimd.memset(head_col[:, h, h:h + 1], 1.0)
            ins.then_inc(consts, 1)
            nc.gpsimd.affine_select(out=ident[:, :], in_=ident[:, :], compare_op=ALU.not_equal, fill=1.0,
                                    base=0, pattern=[[-1, P]], channel_multiplier=1).then_inc(shapes_step, 1)
            nc.gpsimd.affine_select(out=ones3[:, :], in_=ones3[:, :], compare_op=ALU.is_ge, fill=0.0,
                                    base=2, pattern=[[0, P]], channel_multiplier=-1).then_inc(consts, 1)
            pool.wait_ge(shapes_step, 4)
            nc.gpsimd.tensor_copy(ident_bf[:, :], ident[:, :]).then_inc(consts, 1)
            nc.gpsimd.tensor_copy(ident_u8[:, :], ident[:, :]).then_inc(consts, 1)
            nc.gpsimd.tensor_scalar(penalty[:, :], ident[:, :], -BIG, None, ALU.mult).then_inc(consts, 1)
            pool.dma_start(wt_sb[:, :, :], w_t.rearrange("l p n -> p l n")).then_inc(w_in, 16)
            pool.dma_start(wb_sb[:, :], w_b).then_inc(w_in, 16)
            pool.dma_start(wm_sb[:, :, :], wm_t.rearrange("(b p) n -> p b n", p=P)).then_inc(w_in, 16)
            pool.dma_start(bm_row, bm.rearrange("(o n) -> o n", o=1)).then_inc(w_in, 16)
            pool.dma_start(gwt_sb[:, :, :], gat_wt.rearrange("h p n -> p h n")).then_inc(w_in, 16)
            pool.dma_start(ga_sb[:, :, :], gat_a).then_inc(w_in, 16)
            pool.dma_start(d_sb[:, :], diag).then_inc(w_in, 16)
            pool.wait_ge(flag_max, 1)
            nc.gpsimd.partition_all_reduce(flag_f[:, 1:2], flag_f[:, 0:1], P, bass.bass_isa.ReduceOp.max).then_inc(flag_all, 1)
            pool.wait_ge(flag_ok, 1)
            has_neg = pool.value_load(flag[0:1, 0:1], min_val=0, max_val=1)

            def stores(s):
                with pool.Fori(0, NBLK) as C:
                    for u in range(2):
                        cc = C * 2 + u
                        heads_out, rest_out, stored_all = pool.snap(cc * 3 + 6), pool.snap(cc * 2 + 4), pool.snap(cc * STORES + STORES)
                        pool.wait_ge(s.evac_act, heads_out)
                        pool.dma_start(agg_dram[bass.ds(cc, 1), 0:3].rearrange("o h p n -> p (o h) n"),
                                       low[:, 2048:2048 + 3 * CH].rearrange("p (h n) -> p h n", h=3)).then_inc(s.stage_out, 16)
                        pool.wait_ge(s.evac_dve, rest_out)
                        pool.dma_start(agg_dram[bass.ds(cc, 1), 3:4].rearrange("o h p n -> p (o h n)"), stage[3]).then_inc(s.stage_out, 16)
                        pool.dma_start(den_dram[:, bass.ds(cc * CH, CH)], stage[4]).then_inc(s.stage_out, 16)
                        pool.wait_ge(s.stage_out, stored_all)
                        pool.sem_inc(s.stage_free, 1)
            with pool.If(has_neg != 0):
                stores(S[2])
            with pool.Else():
                stores(S[1])
        CONSTS = 8

        @block.scalar
        def _(act):
            act.sem_inc(a_signed, 8)
            act.sem_inc(agg_out, 8)

            def parts_and_signs(C, g):
                for k in range(G8):
                    n = C * T + g * G8
                    act.wait_ge(x_in[k % 2], (C * (T // 2) + g * (G8 // 2) + (k // 2 + 1)) * 16)
                    act.wait_ge(halves_used, n * 2 + (2 * k + 2))
                    nc.scalar.activation(x_parts[:, k % 2, 0, :], x_slot[k % 2], ACT.Copy).then_inc(x_high, 1)
                    act.wait_ge(a_in[k % 4], (C * (T // 4) + g * 2 + (k // 4 + 1)) * 16)
                    for u in range(2):
                        act.wait_ge(halves_used, n * 2 + (2 * k + u + 1))
                        nc.scalar.activation(a_parts[(2 * k + u) % 4][:, 0, :], a_slot[k % 4][:, u * CH:(u + 1) * CH], ACT.Copy).then_inc(a_high, 1)
                    act.wait_ge(coded, n + (k + 1))
                    nc.scalar.activation(sgn[:, k % 2, :], a_slot[k % 4], ACT.Sign, scale=-1.0).then_inc(a_signed, 1)

            def sums_out(C):
                act.wait_ge(halves_used, (C + 1) * (T * 2) + 4)
                for b in range(2):
                    for u in range(2):
                        nc.scalar.activation(high[:, b, C * BW + u * CH:C * BW + (u + 1) * CH], agg_ps[C % 2][b][u][:, :],
                                             ACT.Copy, scale=eps_sb[:, b:b + 1]).then_inc(agg_out, 1)
            for C in range(NBLK):
                parts_and_signs(C, 0)
                if C == 1:
                    act.wait_ge(scale_ok, 1)
                if C:
                    sums_out(C - 1)
                with act.Fori(1, NG) as g:
                    parts_and_signs(C, g)
            sums_out(NBLK - 1)
            act.wait_ge(w_in, 16 * 7)
            for m in range(LAYERS * 16):
                layer, c, b = mlp_step(m)
                act.wait_ge(mlp_mm, m + 1)
                nc.scalar.activation(high[:, b, c * CH:(c + 1) * CH], bank[m % 4][:, :], ACT.Relu,
                                     bias=wb_sb[:, b * LAYERS + layer:b * LAYERS + layer + 1]).then_inc(mlp_act, 1)
            for half in range(2):
                act.wait_ge(var_ok, half + 1)
                t = slice(half * T // 2, (half + 1) * T // 2)
                nc.scalar.activation(rstd[:, t], rstd[:, t], ACT.Sqrt).then_inc(std_ok, 1)
            for q in range(NCH):
                act.wait_ge(ht_mm, q + 1)
                nc.scalar.activation(ht[:, q * CH:(q + 1) * CH], bank[q % 3][:, :], ACT.Copy).then_inc(ht_ok, 1)
            act.wait_ge(flag_ok, 1)
            has_neg = act.value_load(flag[0:1, 0:1], min_val=0, max_val=1)

            def edge_tiles(s, NS):
                if NS == 2:
                    act.wait_ge(h_out, 16 * (NCH + (TD - T) // 4))
                with act.Fori(0, NBLK) as C:
                    with act.Fori(0, NG) as g:
                        src = codes[:, bass.ds(C * T + g * G8, 4), :]
                        act.wait_ge(s.p_used, (C * NG + g) * 2 + 1)
                        if NS == 2:
                            nc.scalar.activation(m_slot[0], src, ACT.Relu, bias=minus_one[:, :]).then_inc(s.p_act, 1)
                        nc.scalar.activation(p_slot[0], src, ACT.Relu, scale=-1.0, bias=1.0).then_inc(s.p_act, 1)

            def attention(s, NS):
                NU = NS * HEADS
                act.sem_inc(s.exp_ok, 6)
                act.sem_inc(s.evac_act, 3)
                act.sem_inc(s.stage_free, 1)
                act.wait_ge(h_out, 16 * (NCH + (TD - T) // 4))
                act.wait_ge(ht_out, 16 * NCH)

                def max_rows(p, par, h):
                    act.wait_ge(s.parts_tr, p * HEADS + max(h + 1, 2))
                    nc.scalar.activation(mrow[par][0:3, h, :], tr_ps[0:3, (h % 2) * (CH // 2):(h % 2 + 1) * (CH // 2)].bitcast(BF16),
                                         ACT.Copy).then_inc(s.mrow_ok, 1)

                def max_to_all(p):
                    act.wait_ge(s.max_mm, p + 1)
                    nc.scalar.activation(max_all, tr_ps[:, :], ACT.Copy).then_inc(s.max_ok, 1)

                def codes_to_bf16(tile0, k, C, u, r0):
                    act.wait_ge(s.lg_ready, (tile0 + (k + 1)) * 2)
                    nc.scalar.activation(rb[k % 4], codes[:, bass.ds(C * T + r0 + k, 1), u * CH:(u + 1) * CH].rearrange("p r n -> p (r n)"),
                                         ACT.Copy).then_inc(s.rb_ready, 1)

                def body(C, u, g, closing):
                    cc = C * 2 + u
                    tile0 = (cc * NG + g) * G8

                    for k in range(G8):
                        for n in range(k * NU, (k + 1) * NU):
                            v = n % NU
                            if n % HEADS < 2:
                                act.wait_ge(s.lg_ready, tile0 * (2 * NS) + (n // HEADS * 2 + n % HEADS + 1 + 8 * NS))
                                logits_in = lg_ps[n % HEADS][:, :]
                            else:
                                act.wait_ge(s.lgs_ready, tile0 * NS + (n // HEADS + 1))
                                logits_in = lgs[n // HEADS % 2]
                            act.wait_ge(s.e_used, tile0 * NU + (n + 1))
                            nc.scalar.activation(ebuf[n % 6], logits_in, ACT.Exp,
                                                 bias=e_nat[:, bass.ds(C * RB + g * G8 + k, 1), v:v + 1].rearrange("p a b -> p (a b)")).then_inc(s.exp_ok, 1)
                        if NS == 1:
                            if closing and k + 2 >= G8:
                                codes_to_bf16(tile0, k + 2, *chunk_after(C, u, 1), -G8)
                            else:
                                codes_to_bf16(tile0, k + 2, C, u, g * G8)
                        if closing and k == 5:
                            max_rows(cc + 1, 1 - u, 0)
                            max_rows(cc + 1, 1 - u, 1)
                        if closing and k == 6:
                            max_rows(cc + 1, 1 - u, 2)

                if NS == 1:
                    codes_to_bf16(0, 0, 0, 0, 0)
                    codes_to_bf16(0, 1, 0, 0, 0)
                for h in range(HEADS):
                    max_rows(0, 0, h)
                max_to_all(0)
                with act.Fori(0, NBLK) as C:
                    for u in range(2):
                        cc = C * 2 + u
                        with act.Fori(0, NG - 1) as g:
                            body(C, u, g, False)
                        with act.Fori(NG - 1, NG) as g:
                            body(C, u, g, True)
                        max_to_all(cc + 1)
                        act.wait_ge(s.e_used, (cc + 1) * (T * NU) + 6)
                        act.wait_ge(s.stage_free, cc + 1)
                        for h in range(HEADS):
                            nc.scalar.activation(stage[h], num_ps[h][:, :], ACT.Copy).then_inc(s.evac_act, 1)
                act.wait_ge(s.max_step, HEADS + (NCH + 1) * (T * NU) + G8 * NU)
                act.wait_ge(s.lgs_ready, NCH * T * NS + 1)
                act.wait_ge(s.rb_ready, (NCH * T + 2) * NS)
            with act.If(has_neg != 0):
                edge_tiles(S[2], 2)
                attention(S[2], 2)
            with act.Else():
                edge_tiles(S[1], 1)
                attention(S[1], 1)

            act.wait_ge(bias_ok, 2)
            for c in range(NCH):
                s = c % 2
                for i in range(2):
                    bk = bank[4 * i:4 * i + 4]
                    if i == 1:
                        act.wait_ge(f_mm, mm_at(c, "es"))
                        if c >= 2:
                            act.wait_ge(f_mm, mm_at(c - 2, "g1"))
                        nc.scalar.activation(f_es[s], bank[0][:, :], ACT.Copy, scale=1.0 / HEADS).then_inc(f_act, 1)
                    if c:
                        act.wait_ge(f_dve, dve_at[f"out{i}", c - 1])
                    for j, gate in enumerate("rz"):
                        act.wait_ge(f_mm, mm_at(c, f"{gate}{i}"))
                        nc.scalar.activation((f_r, f_z)[j][i], bk[j][:, :], ACT.Sigmoid, bias=gb_sb[:, 6 * i + j:6 * i + j + 1]).then_inc(f_act, 1)
                    act.wait_ge(f_dve, dve_at[f"pre{i}", c])
                    nc.scalar.activation(f_n[i], f_t[i], ACT.Tanh, bias=gb_sb[:, 6 * i + 2:6 * i + 3]).then_inc(f_act, 1)
            for i, t in enumerate((slice(0, T - 4), slice(T - 4, T))):
                act.wait_ge(var_ok, i + 3)
                nc.scalar.activation(rstd[:, t], rstd[:, t], ACT.Sqrt).then_inc(f_std, 1)

        @block.tensor
        def _(pe):
            pe.sem_inc(halves_used, 4)
            pe.wait_ge(consts, CONSTS)
            with pe.Fori(0, NBLK // 2) as Cp:
                for par in range(2):
                    pe.wait_ge(agg_out, (Cp * 2 + par) * 4 + 4)
                    for b in range(2):
                        for u in range(2):
                            nc.tensor.matmul(agg_ps[par][b][u][:, :], zeros[:, 0:P], zeros[:, :], start=True, stop=True, skip_group_check=True)
                    with pe.Fori(0, NG) as g:
                        for k in range(G8):
                            n = (Cp * 2 + par) * T + g * G8
                            pe.wait_ge(x_parted, n + (k + 3))
                            for u in range(2):
                                a_high_part, a_low_part = (a_parts[(2 * k + u) % 4][:, part, :] for part in range(2))
                                pe.wait_ge(a_parted, n * 2 + (2 * k + u + 9))
                                for b in range(2):
                                    x_high_part, x_low_part = (x_parts[:, k % 2, part, b * P:(b + 1) * P] for part in range(2))
                                    o = agg_ps[par][b][u][:, :]
                                    nc.tensor.matmul(o, x_low_part, a_high_part, start=False, stop=True, skip_group_check=True)
                                    nc.tensor.matmul(o, x_high_part, a_low_part, start=False, stop=True, skip_group_check=True)
                                    mm = nc.tensor.matmul(o, x_high_part, a_high_part, start=False, stop=True, skip_group_check=True)
                                mm.then_inc(halves_used, 1)
            pe.wait_ge(agg_out, 8 + 4 * NBLK)
            def mlp(first, last):
                for m in range(first, last):
                    layer, c, b = mlp_step(m)
                    if m >= 4:
                        pe.wait_ge(mlp_act, m - 3)
                    nc.tensor.matmul(bank[m % 4][:, :], wt_sb[:, b * LAYERS + layer, :], high[:, b, c * CH:(c + 1) * CH],
                                     start=True, stop=True).then_inc(mlp_mm, 1)

            def merge(half):
                for q in range(4 * half, 4 * half + 4):
                    pe.wait_ge(mlp_act, half * MLP_HALF + 2 * 8 + 2 * (q % 4) + 2)
                    if half:
                        pe.wait_ge(res_ok, q - 3)
                    for g in range(4 * q, 4 * q + 4):
                        o = bank[4 + q % 4][:, (g % 4) * P:(g % 4 + 1) * P]
                        nc.tensor.matmul(o, high[:, 0, g * P:(g + 1) * P], wm_sb[:, 0, :], start=(g % 4 == 0), stop=True, skip_group_check=True)
                        nc.tensor.matmul(o, high[:, 1, g * P:(g + 1) * P], wm_sb[:, 1, :], start=False, stop=True, skip_group_check=True)
                        mm = nc.tensor.matmul(o, ones_row, bm_row, start=False, stop=True, skip_group_check=True)
                    mm.then_inc(mg_mm, 1)
            pe.wait_ge(w_in, 16 * 7)
            mlp(0, MLP_HALF + 8)
            merge(0)
            mlp(MLP_HALF + 8, 2 * MLP_HALF)
            merge(1)
            for h in range(HEADS):
                mm = nc.tensor.matmul(bank[3][:, 2 * h:2 * h + 2], gwt_sb[:, h, :], ga_sb[:, h, :], start=(h == 0), stop=True, skip_group_check=True)
            mm.then_inc(u_mm, 1)
            for half in range(2):
                for q in range(4 * half, 4 * half + 4):
                    pe.wait_ge(ln_ok, 4 * (q + 1))
                    if q >= 3:
                        pe.wait_ge(ht_ok, q - 2)
                    for g in range(4 * q, 4 * q + 4):
                        mm = nc.tensor.transpose(bank[q % 3][:, (g % 4) * P:(g % 4 + 1) * P], hn[:, g, :], ident[:, :])
                    mm.then_inc(ht_mm, 1)
                pe.wait_ge(u_ok, 1)
                for g in range(half * T // 2, (half + 1) * T // 2):
                    if g % 4 == 0:
                        pe.wait_ge(ht_ok, g // 4 + 1)
                    mm = nc.tensor.matmul(bank[3][:, 6 * g:6 * g + 6], ht[:, g * P:(g + 1) * P], u_sb[:, :, :].rearrange("p s h -> p (s h)"),
                                          start=(g == 0), stop=True, skip_group_check=True)
            mm.then_inc(v_mm, 1)
            pe.wait_ge(flag_ok, 1)
            has_neg = pe.value_load(flag[0:1, 0:1], min_val=0, max_val=1)

            def logits(s, NS):
                W = 9 * NS
                with pe.Fori(0, NBLK) as C:
                    pe.wait_ge(s.e_ps_free, C + 1)
                    nc.tensor.matmul(bank[1][:, 0:RB * W], zeros[:, 0:P], zeros[:, 0:RB * W], start=True, stop=True, skip_group_check=True)
                    with pe.Fori(0, NG) as g:
                        for k in range(G8):
                            if k % 4 == 0:
                                pe.wait_ge((s.p_act, s.p_dve)[k // 4], (C * NG + g) * NS + NS)
                            t = C * RB + g * G8 + k
                            for i in range(RB):
                                o = bank[1][:, i * W:(i + 1) * W].rearrange("p (a c) -> p a c", a=3)
                                mm = nc.tensor.matmul(o, p_slot[k // 4][:, k % 4, i * P:(i + 1) * P],
                                                      v3[:, bass.ds(t, 1), :, 0:3 * NS].rearrange("p o a c -> p (o a) c"),
                                                      start=False, stop=True, skip_group_check=True)
                                if NS == 2:
                                    for sg in range(2):
                                        mm = nc.tensor.matmul(o[:, :, 3 * sg:3 * sg + 3], m_slot[k // 4][:, k % 4, i * P:(i + 1) * P],
                                                              v3[:, bass.ds(t, 1), :, 3 - 3 * sg:6 - 3 * sg].rearrange("p o a c -> p (o a) c"),
                                                              start=False, stop=True, skip_group_check=True)
                            if k % 4 == 3:
                                mm.then_inc(s.p_used, 1)

            def attention(s, NS):
                NU = NS * HEADS
                pe.sem_inc(s.lg_ready, 8 * NS)
                pe.sem_inc(s.w_used, 8 * NU + 3)
                pe.sem_inc(s.e_used, 6)

                def turn_minima(p, h):
                    if h == 0:
                        pe.wait_ge(s.max_step, (p + 1) * (T * NU) + HEADS)
                        if not (isinstance(p, int) and p == 0):
                            pe.wait_ge(s.max_ok, p)
                    else:
                        pe.wait_ge(s.min_ok, p * HEADS + h)
                    for i in range(4):
                        mm = nc.tensor.transpose(tr_ps[:, i * P:(i + 1) * P], macc[h][:, i * P:(i + 1) * P], ident[:, :])
                    mm.then_inc(s.macc_tr, 1)

                def turn_parts(p, h):
                    if h == 0:
                        pe.wait_ge(s.parts_ok, p + 1)
                    if h == 2:
                        pe.wait_ge(s.mrow_ok, p * HEADS + 2)
                    for i in range(4):
                        o = (h % 2) * (CH // 2) + i * P // 2
                        mm = nc.tensor.transpose(tr_ps[0:3, o:o + P // 2].bitcast(BF16), mparts[:, h, i, :], ident_bf[:, :])
                    mm.then_inc(s.parts_tr, 1)

                def max_to_all(p, rows):
                    pe.wait_ge(s.mrow_ok, (p + 1) * HEADS)
                    nc.tensor.matmul(tr_ps[:, :], ones3[:, :], rows[:, 2, :], start=True, stop=True).then_inc(s.max_mm, 1)

                def logit(tile0, n, rows):
                    k, v = n // NU, n % NU
                    if v == 0 and NS == 1:
                        pe.wait_ge(s.rb_ready, tile0 + (k + 1))
                    if v % HEADS == 0 and NS == 2:
                        pe.wait_ge(s.rb_ready, (tile0 + k) * 2 + (v // HEADS + 1))
                    mask = rb[k % 4] if NS == 1 else rb[(2 * k + v // HEADS) % 4]
                    pe.wait_ge(s.exp_ok, tile0 * NU + (n + 4))
                    nc.tensor.matmul(lg_ps[v % HEADS][:, :], penalty[:, :], mask, start=True, stop=False)
                    nc.tensor.matmul(lg_ps[v % HEADS][:, :], ones3[:, :], rows[:, v % HEADS, :], start=False, stop=True).then_inc(s.lg_ready, 1)

                def body(C, u, g, closing):
                    cc = C * 2 + u
                    body_n = cc * NG + g
                    tile0 = body_n * G8
                    for k in range(G8):
                        hk = h_slot[k // 4][:, k % 4, :]
                        if k % 4 == 0:
                            pe.wait_ge(s.h_in[k // 4], (body_n + 1) * 16)
                        if k % 2 == 0:
                            pe.wait_ge(s.a2_in[k // 2], (body_n + 1) * 16)
                        if k // 4 == u:
                            pe.wait_ge(s.a2_masked, body_n * 4 + (k % 4 + 1))
                        nc.tensor.matmul(node_ps[:, :], hk, a2_slot[k // 2][:, k % 2, :], start=False, stop=True, skip_group_check=True)
                        for n in range(k * NU, (k + 1) * NU):
                            if closing and n + 2 == G8 * NU:
                                pe.wait_ge(s.mrow_ok, (cc + 1) * HEADS + 2)
                            if (n + 2) % HEADS < 2:
                                logit(tile0, n + 2, mrow[1 - u if closing and n + 2 >= G8 * NU else u])
                            pe.wait_ge(s.w_ready, tile0 * NU + (n + 1 + 8 * NU))
                            nc.tensor.matmul(num_ps[n % HEADS][:, :], hk, wbuf[n % 3], start=False, stop=True, skip_group_check=True).then_inc(s.w_used, 1)
                            if n % 4 == 3:
                                for m in range(n - 3, n + 1):
                                    q = m % 4
                                    mm = nc.tensor.matmul(den_ps[32 * q:32 * q + HEADS, :], head_col[:, m % HEADS, :], ebuf[m % 6], start=False, stop=True,
                                                          skip_group_check=True)
                                mm.then_inc(s.e_used, 4)
                            if closing and n == k * NU:
                                if k < 3:
                                    turn_minima(cc + 1, k)
                                if k == 5:
                                    turn_parts(cc + 1, 0)
                                    turn_parts(cc + 1, 1)
                                if k == 6:
                                    turn_parts(cc + 1, 2)
                                if k == 7:
                                    max_to_all(cc + 1, mrow[1 - u])

                for h in range(HEADS):
                    turn_minima(0, h)
                for h in range(HEADS):
                    turn_parts(0, h)
                max_to_all(0, mrow[0])
                logit(0, 0, mrow[0])
                logit(0, 1, mrow[0])
                with pe.Fori(0, NBLK) as C:
                    for u in range(2):
                        cc = C * 2 + u
                        for b in range(5):
                            if b < 3:
                                pe.wait_ge(s.evac_act, cc * 3 + (b + 1))
                            if b == 3:
                                pe.wait_ge(s.evac_dve, cc * 2 + 2)
                            nc.tensor.matmul(bank[b][:, :], zeros[:, 0:P], zeros[:, :], start=True, stop=True, skip_group_check=True)
                        with pe.Fori(0, NG - 1) as g:
                            body(C, u, g, False)
                        with pe.Fori(NG - 1, NG) as g:
                            body(C, u, g, True)
                pe.wait_ge(s.evac_act, NCH * 3 + 3)
                pe.wait_ge(s.evac_dve, NCH * 2 + 2)
                pe.wait_ge(s.exp_ok, NCH * T * NU + 6)
                pe.wait_ge(s.max_ok, NCH + 1)
            with pe.If(has_neg != 0):
                pe.sem_inc(S[2].p_used, 2)
                pe.wait_ge(v_ok, 1)
                logits(S[2], 2)
                attention(S[2], 2)
            with pe.Else():
                pe.sem_inc(S[1].p_used, 2)
                pe.wait_ge(v_ok, 1)
                logits(S[1], 1)
                attention(S[1], 1)

            pe.wait_ge(fw_in, 48)

            def rows(c):
                pe.wait_ge(f_dve, dve_at["out1", c])
                for i in range(4):
                    mm = nc.tensor.transpose(bank[1][:, i * P:(i + 1) * P], f_o[0][c % 2][:, i * P:(i + 1) * P], ident[:, :])
                mm.then_inc(f_tr, 1)

            for c in range(NCH):
                s = c % 2
                pe.wait_ge(f_in[s], (c // 2 + 1) * 16 * 3)
                if c:
                    pe.wait_ge(f_dve, dve_at["pre0", c - 1])
                    pe.wait_ge(f_act, act_at(c - 1, "es"))
                if c >= 2:
                    pe.wait_ge(f_dve, dve_at["rows", c - 2])
                for gate in range(2):
                    nc.tensor.matmul(bank[gate][:, :], gw_sb[:, gate, :], f_node[s], start=True, stop=False)
                    nc.tensor.matmul(bank[gate][:, :], gw_sb[:, 3 + gate, :], f_ht[s], start=False, stop=True).then_inc(f_mm, 1)
                nc.tensor.matmul(bank[2][:, :], gw_sb[:, 2, :], f_node[s], start=True, stop=True)
                nc.tensor.matmul(bank[3][:, :], gw_sb[:, 5, :], f_ht[s], start=True, stop=True).then_inc(f_mm, 1)
                pe.wait_ge(f_dve, dve_at["scaled", c])
                pe.wait_ge(f_act, act_at(c, "r0"))
                for h in range(HEADS):
                    mm = nc.tensor.matmul(bank[0][:, :], pw_sb[:, h, :], f_num[s][:, h, :], start=(h == 0), stop=(h == HEADS - 1))
                mm.then_inc(f_mm, 1)
                if c:
                    pe.wait_ge(f_act, act_at(c, "z0"))
                    rows(c - 1)
                    pe.wait_ge(f_dve, dve_at["pre1", c - 1])
                for gate in range(2):
                    nc.tensor.matmul(bank[4 + gate][:, :], gw_sb[:, 9 + gate, :], f_ht[s], start=True, stop=False)
                nc.tensor.matmul(bank[7][:, :], gw_sb[:, 11, :], f_ht[s], start=True, stop=True)
                pe.wait_ge(f_act, act_at(c, "es"))
                for gate in range(2):
                    nc.tensor.matmul(bank[4 + gate][:, :], gw_sb[:, 6 + gate, :], f_es[s], start=False, stop=True).then_inc(f_mm, 1)
                nc.tensor.matmul(bank[6][:, :], gw_sb[:, 8, :], f_es[s], start=True, stop=True).then_inc(f_mm, 1)
            rows(NCH - 1)

        @block.vector
        def _(dve):
            steps = [0]

            def link(ins):
                steps[0] += 1
                ins.then_inc(chain, 1)
                dve.wait_ge(chain, steps[0])

            dve.sem_inc(coded, 2)
            dve.sem_inc(x_parted, 2)
            dve.sem_inc(a_parted, 8)
            nc.vector.memset(code_bits, 0).then_inc(bits_step, 1)
            nc.vector.memset(ones_u8[:, :], 1.0).then_inc(ones_ok, 1)
            dve.wait_ge(eps_in, 16)
            nc.vector.tensor_scalar(eps_sb[:, :], eps_sb[:, :], 1.0, 1.0, ALU.add, ALU.add).then_inc(scale_ok, 1)
            with dve.Fori(0, NBLK) as C:
                with dve.Fori(0, NG) as g:
                    for k in range(G8):
                        n1 = C * T + g * G8 + (k + 1)
                        dve.wait_ge(x_high, n1)
                        nc.vector.tensor_tensor(x_parts[:, k % 2, 1, :], x_slot[k % 2], x_parts[:, k % 2, 0, :], ALU.subtract).then_inc(x_parted, 1)
                        for u in range(2):
                            a = a_parts[(2 * k + u) % 4]
                            dve.wait_ge(a_high, C * (2 * T) + g * (2 * G8) + (2 * k + u + 1))
                            nc.vector.tensor_tensor(a[:, 1, :], a_slot[k % 4][:, u * CH:(u + 1) * CH], a[:, 0, :], ALU.subtract).then_inc(a_parted, 1)
                        dve.wait_ge(a_signed, n1 + 8)
                        nc.vector.tensor_scalar(codes[:, bass.ds(C * T + g * G8 + k, 1), :].rearrange("p r n -> p (r n)"),
                                                sgn[:, k % 2, :], 1.0, None, ALU.add).then_inc(coded, 1)
                        if k % 2:
                            dve.wait_ge(coded, n1 + 2)
                            dve.wait_ge(bits_step, C * (T // 2) + g * (G8 // 2) + (k // 2 + 1))
                            nc.vector.tensor_tensor(code_bits.rearrange("p (t n) -> p t n", t=2), code_bits.rearrange("p (t n) -> p t n", t=2),
                                                    codes[:, bass.ds(C * T + g * G8 + (k - 1), 2), :].bitcast(I32), ALU.bitwise_or).then_inc(bits_step, 1)
            dve.wait_ge(bits_step, NBLK * T // 2 + 1)
            nc.vector.tensor_reduce(flag_f[:, 0:1], code_bits.bitcast(U8), AX.X, ALU.max).then_inc(flag_max, 1)
            dve.wait_ge(consts, CONSTS)
            dve.wait_ge(ones_ok, 1)
            for C in range(NBLK):
                for r in range(RB):
                    ins = nc.vector.copy_predicated(codes[:, C * T + r, r * P:(r + 1) * P], ident_u8[:, :], ones_u8[:, :])
            link(ins)
            dve.wait_ge(flag_all, 1)
            nc.vector.tensor_scalar(flag[0:1, 0:1], flag_f[0:1, 1:2], 2.0, None, ALU.is_ge).then_inc(flag_ok, 1)

            def statistics(q, rows):
                for i in range(4):
                    ins = nc.vector.bn_stats(bst[:, i, :], rows[:, 4 * q + i, :])
                link(ins)
                for i in range(4):
                    ins = nc.vector.bn_aggr(mv[:, 4 * q + i, :], bst[:, i, :])
                link(ins)

            def variance(first, last):
                t = slice(first, last)
                link(nc.vector.tensor_scalar(rstd[:, t], mv[:, t, 1], EPS, None, ALU.add))
                dve.sem_inc(var_ok, 1)

            def normalize(rows, first, last, std, count, ready):
                t = slice(first, last)
                dve.wait_ge(std, count)
                link(nc.vector.reciprocal(rstd[:, t], rstd[:, t]))
                for t in range(first, last):
                    nc.vector.tensor_scalar(rows[:, t, :], rows[:, t, :], mv[:, t, 0:1], rstd[:, t:t + 1],
                                            ALU.subtract, ALU.mult).then_inc(ready, 1)

            dve.wait_ge(w_in, 16 * 7)
            dve.wait_ge(xn_in, 16)
            for half in range(2):
                for q in range(4 * half, 4 * half + 4):
                    dve.wait_ge(mg_mm, q + 1)
                    r = hn[:, 4 * q:4 * q + 4, :]
                    ins = nc.vector.tensor_tensor(r, bank[4 + q % 4][:, :].rearrange("p (t n) -> p t n", t=4), r, ALU.add)
                    link(ins)
                    dve.sem_inc(res_ok, 1)
                    statistics(q, hn)
                variance(half * T // 2, (half + 1) * T // 2)
                normalize(hn, half * T // 2, (half + 1) * T // 2, std_ok, half + 1, ln_ok)
            dve.wait_ge(u_mm, 1)
            link(nc.vector.tensor_copy(u_sb[:, :, :], bank[3][:, 0:6].rearrange("p (h s) -> p s h", s=2)))
            dve.sem_inc(u_ok, 1)
            dve.wait_ge(v_mm, 1)
            link(nc.vector.tensor_copy(v_f[:, :, :], bank[3][:, 0:6 * T].rearrange("p (t c) -> p t c", c=6)))
            for part in range(3):
                src = v_f if part == 0 else v_r
                nc.vector.tensor_copy(v3[:, T:2 * T, part, :], src[:, :, :])
                link(nc.vector.tensor_copy(v3[:, 0:T, part, :], src[:, :, :]))
                if part < 2:
                    link(nc.vector.tensor_tensor(v_r[:, :, :], src[:, :, :], v3[:, 0:T, part, :], ALU.subtract))
            dve.sem_inc(v_ok, 1)
            has_neg = dve.value_load(flag[0:1, 0:1], min_val=0, max_val=1)

            def attention(s, NS):
                NU = NS * HEADS
                PASS = T * NU
                FIN = 6
                dve.sem_inc(s.w_ready, 8 * NU)
                dve.sem_inc(s.evac_dve, 2)

                def search(p, Cs, us, r0, k, v):
                    code = codes[:, bass.ds(Cs * T + r0 + k, 1), us * CH:(us + 1) * CH].rearrange("p r n -> p (r n)")
                    e = e_sc[:, bass.ds(Cs * RB + r0 + k, 1), v:v + 1].rearrange("p a b -> p (a b)")
                    dve.wait_ge(s.max_step, p * PASS + r0 * NU + (k * NU + v + 1))
                    if v >= HEADS:
                        neg = neg_code[:, k % 2, :]
                        if v == HEADS:
                            nc.vector.tensor_scalar(neg, code, 2.0, None, ALU.is_lt).then_inc(s.rn_step, 1)
                            dve.wait_ge(s.rn_step, p * T + r0 + (k + 1))
                        code = neg
                    if v < HEADS and k == 0 and isinstance(r0, int):
                        nc.vector.tensor_scalar(macc[v], code, e, None, ALU.subtract).then_inc(s.max_step, 1)
                    else:
                        nc.vector.scalar_tensor_tensor(out=macc[v % HEADS], in0=code, scalar=e, in1=macc[v % HEADS],
                                                       op0=ALU.subtract, op1=ALU.min).then_inc(s.max_step, 1)

                def minimum(p, h):
                    dve.wait_ge(s.macc_tr, p * HEADS + (h + 1))
                    nc.vector.tensor_reduce(wmin[:, h, :], tr_ps[:, :].rearrange("p (i n) -> p i n", i=4), AX.X, ALU.min).then_inc(s.min_ok, 1)

                def parts(p, i):
                    if i == 0:
                        dve.wait_ge(s.min_ok, p * HEADS + HEADS)
                    else:
                        dve.wait_ge(s.chain2, NBLK * 5 + p * FIN + i)
                    if i == 0:
                        ins = nc.vector.scalar_tensor_tensor(out=negm[:, :, :], in0=wmin[:, :, :], scalar=0.5, in1=wmin[:, :, :], op0=ALU.is_lt, op1=ALU.mult)
                    elif i == 1:
                        ins = nc.vector.tensor_scalar(negm[:, :, :], negm[:, :, :], 1.0 / ESC, None, ALU.mult)
                    elif i % 2 == 0:
                        ins = nc.vector.tensor_copy(mparts[:, :, :, i // 2 - 1], negm[:, :, :])
                    else:
                        ins = nc.vector.tensor_tensor(negm[:, :, :], negm[:, :, :], mparts[:, :, :, i // 2 - 1], ALU.subtract)
                    ins.then_inc(s.parts_ok if i == FIN else s.chain2, 1)

                def masks(tile0, k, C, u, r0):
                    code = codes[:, bass.ds(C * T + r0 + k, 1), u * CH:(u + 1) * CH].rearrange("p r n -> p (r n)")
                    dve.wait_ge(s.lg_ready, (tile0 + (k + 3)) * 4)
                    nc.vector.tensor_scalar(rb[2 * k % 4], code, 0.0, None, ALU.is_gt).then_inc(s.rb_ready, 1)
                    nc.vector.tensor_scalar(rb[(2 * k + 1) % 4], code, 2.0, None, ALU.is_lt).then_inc(s.rb_ready, 1)

                def last_head_logits(tile0, m, C, u, r0):
                    if NS == 2:
                        dve.wait_ge(s.rb_ready, tile0 * 2 + (m + 1))
                        code = rb[m % 4]
                    else:
                        code = codes[:, bass.ds(C * T + r0 + m, 1), u * CH:(u + 1) * CH].rearrange("p r n -> p (r n)")
                    dve.wait_ge(s.exp_ok, tile0 * NU + (m * HEADS + 3))
                    nc.vector.scalar_tensor_tensor(out=lgs[m % 2], in0=code, scalar=-BIG, in1=max_all, op0=ALU.mult, op1=ALU.add).then_inc(s.lgs_ready, 1)

                def body(C, u, g, closing):
                    cc = C * 2 + u
                    body_n = cc * NG + g
                    tile0 = body_n * G8

                    for k in range(G8):
                        if k % 2 == 0:
                            dve.wait_ge(s.a2_in[k // 2], (body_n + 1) * 16)
                        if k // 4 == u:
                            i = k % 4
                            d = a2_slot[k // 2][:, k % 2, i * P:(i + 1) * P]
                            nc.vector.tensor_tensor(d, d, off_diag[:, bass.ds(g, 1), :].rearrange("p o n -> p (o n)"), ALU.mult).then_inc(s.a2_masked, 1)
                            dve.wait_ge(s.a2_masked, body_n * 4 + (i + 1))
                        for n in range(k * NU, (k + 1) * NU):
                            v = n % NU
                            dve.wait_ge(s.exp_ok, tile0 * NU + (n + 7))
                            dve.wait_ge(s.w_used, tile0 * NU + (n + 1 + 8 * NU))
                            nc.vector.tensor_tensor(wbuf[n % 3], ebuf[n % 6], a2_slot[k // 2][:, k % 2, :], ALU.mult).then_inc(s.w_ready, 1)
                            if v % HEADS == 1 and not (closing and n // HEADS + 1 == G8 * NS):
                                last_head_logits(tile0, n // HEADS + 1, C, u, g * G8)
                            if not closing:
                                search(cc + 1, *chunk_after(C, u, 1), g * G8 + G8, k, v)
                            elif k < 3:
                                if v == NU - 1:
                                    minimum(cc + 1, k)
                            elif k == 3:
                                if v < 3:
                                    parts(cc + 1, 2 * v)
                                    parts(cc + 1, 2 * v + 1)
                            elif n == 4 * NU:
                                parts(cc + 1, FIN)
                            if closing and n >= 3 * NU - 1:
                                left, of = n - (3 * NU - 1), 5 * NU + 1
                                for j in range(G8 * NU * left // of, G8 * NU * (left + 1) // of):
                                    search(cc + 2, *chunk_after(C, u, 2), 0, j // NU, j % NU)
                        if NS == 2:
                            if closing and k + 2 >= G8:
                                masks(tile0, k + 2, *chunk_after(C, u, 1), -G8)
                            else:
                                masks(tile0, k + 2, C, u, g * G8)

                def edge_tiles(C, g):
                    src = codes[:, bass.ds(C * T + g * G8 + 4, 4), :]
                    dve.wait_ge(s.p_used, (C * NG + g) * 2 + 2)
                    if NS == 2:
                        nc.vector.tensor_scalar(m_slot[1], src, 1.0, None, ALU.is_gt).then_inc(s.p_dve, 1)
                    nc.vector.tensor_scalar(p_slot[1], src, 1.0, None, ALU.is_lt).then_inc(s.p_dve, 1)

                def node_logits(C):
                    dve.wait_ge(s.p_used, (C + 1) * 2 * NG + 2)
                    c3 = slice(0, 3 * NS)
                    n = [0]

                    def step(ins):
                        n[0] += 1
                        ins.then_inc(s.chain2, 1)
                        dve.wait_ge(s.chain2, C * 5 + n[0])
                    step(nc.vector.tensor_copy(e_tmp[:, :, :, c3], bank[1][:, 0:RB * 9 * NS].rearrange("p (i a c) -> p i a c", i=RB, a=3)))
                    dve.sem_inc(s.e_ps_free, 1)
                    step(nc.vector.tensor_tensor(e_tmp[:, :, 1, c3], e_tmp[:, :, 1, c3], e_tmp[:, :, 2, c3], ALU.add))
                    step(nc.vector.tensor_tensor(e_tmp[:, :, 0, c3], e_tmp[:, :, 0, c3], e_tmp[:, :, 1, c3], ALU.add))
                    for dup in range(2):
                        t8 = bass.ds(C * RB + dup * T, RB)
                        ins = nc.vector.scalar_tensor_tensor(out=e_nat[:, t8, c3], in0=e_tmp[:, :, 0, c3], scalar=ALPHA,
                                                             in1=e_tmp[:, :, 0, c3], op0=ALU.mult, op1=ALU.max)
                    step(ins)
                    for dup in range(2):
                        t8 = bass.ds(C * RB + dup * T, RB)
                        ins = nc.vector.tensor_scalar(e_sc[:, t8, c3], e_nat[:, t8, c3], ESC, None, ALU.mult)
                    step(ins)

                dve.sem_inc(s.e_ps_free, 1)
                dve.wait_ge(h_out, 16 * (NCH + (TD - T) // 4))
                with dve.Fori(0, NG) as g:
                    edge_tiles(0, g)
                dve.wait_ge(ht_out, 16 * NCH)
                nc.vector.memset(off_diag[:, 1:NG, :], 1.0)
                nc.vector.tensor_scalar(off_diag[:, 0, :], ident[:, :], 0.0, None, ALU.is_equal)
                for b in range(2):
                    nc.vector.memset(mrow[b], 0.0)
                for h in range(HEADS):
                    nc.vector.memset(macc[h], 4.0).then_inc(s.max_step, 1)
                node_logits(0)
                with dve.Fori(1, NBLK) as C:
                    with dve.Fori(0, NG) as g:
                        edge_tiles(C, g)
                        for j in range(2 * NU):
                            search(0, 0, 0, (C - 1) * RB + g * 2, j // NU, j % NU)
                    node_logits(C)
                with dve.Fori(0, 2) as g:
                    for j in range(G8 // 2 * NU):
                        search(0, 0, 0, g * (G8 // 2) + (T - RB), j // NU, j % NU)
                for h in range(HEADS):
                    minimum(0, h)
                for i in range(FIN + 1):
                    parts(0, i)
                for j in range(G8 * NU):
                    search(1, 0, 1, 0, j // NU, j % NU)
                if NS == 2:
                    masks(0, 0, 0, 0, 0)
                    masks(0, 1, 0, 0, 0)
                dve.wait_ge(s.max_ok, 1)
                last_head_logits(0, 0, 0, 0, 0)
                with dve.Fori(0, NBLK) as C:
                    for u in range(2):
                        cc = C * 2 + u
                        with dve.Fori(0, NG - 1) as g:
                            body(C, u, g, False)
                        with dve.Fori(NG - 1, NG) as g:
                            body(C, u, g, True)
                        dve.wait_ge(s.e_used, (cc + 1) * (T * NU) + 6)
                        dve.wait_ge(s.stage_free, cc + 1)
                        nc.vector.tensor_copy(stage[3], node_ps[:, :]).then_inc(s.evac_dve, 1)
                        nc.vector.tensor_copy(stage[4], den_ps[:, :]).then_inc(s.evac_dve, 1)
                        dve.wait_ge(s.max_ok, cc + 2)
                        last_head_logits((cc + 1) * T, 0, *chunk_after(C, u, 1), 0)
            with dve.If(has_neg != 0):
                attention(S[2], 2)
            with dve.Else():
                attention(S[1], 1)

            def invert(half):
                d = den_c[half * P // 2:(half + 1) * P // 2]
                dve.wait_ge(den_in, 16 * 4 * (half + 1))
                link(nc.vector.tensor_tensor(d[:, 0:2, :], d[:, 0:2, :], d[:, 2:4, :], ALU.add))
                link(nc.vector.tensor_tensor(d[:, 0, :], d[:, 0, :], d[:, 1, :], ALU.add))
                link(nc.vector.tensor_scalar(d[:, 0, :], d[:, 0, :], 1e-30, None, ALU.max))
                nc.vector.reciprocal(d[:, 0, :], d[:, 0, :]).then_inc(rden_ok, 1)
            invert(0)
            dve.wait_ge(fw_in, 48)
            for i in range(2):
                b = gb_sb[:, 6 * i:6 * i + 2]
                nc.vector.tensor_tensor(b, b, gb_sb[:, 6 * i + 4:6 * i + 6], ALU.add).then_inc(bias_ok, 1)
            done = [0]

            def step(ins):
                done[0] += 1
                ins.then_inc(f_dve, 1)
                dve.wait_ge(f_dve, done[0])

            def scaled(c):
                s = c % 2
                dve.wait_ge(f_in[s], (c // 2 + 1) * 16 * 3)
                dve.wait_ge(d_in[s], (c // 2 + 1) * 16)
                step(nc.vector.tensor_tensor(f_num[s], f_num[s], f_den[s], ALU.mult))

            def pre(c, i):
                dve.wait_ge(f_mm, mm_at(c, f"g{i}"))
                dve.wait_ge(f_act, act_at(c, f"r{i}"))
                step(nc.vector.scalar_tensor_tensor(out=f_t[i], in0=bank[4 * i + 3][:, :], scalar=gb_sb[:, 6 * i + 3:6 * i + 4], in1=f_r[i],
                                                    op0=ALU.add, op1=ALU.mult))
                step(nc.vector.tensor_tensor(f_t[i], bank[4 * i + 2][:, :], f_t[i], ALU.add))

            def cell_out(c, i):
                s = c % 2
                dve.wait_ge(f_act, act_at(c, f"n{i}"))
                step(nc.vector.tensor_tensor(f_t[i], f_ht[s], f_n[i], ALU.subtract))
                step(nc.vector.tensor_tensor(f_t[i], f_t[i], f_z[i], ALU.mult))
                step(nc.vector.tensor_tensor(f_o[i][s], f_n[i], f_t[i], ALU.add))
                if i:
                    step(nc.vector.tensor_tensor(f_o[0][s], f_o[0][s], f_o[1][s], ALU.add))

            def rows(c):
                dve.wait_ge(f_tr, c + 1)
                dve.wait_ge(hn_in[c % 2], (c // 2 + 1) * 16)
                for i in range(4):
                    t = 4 * c + i
                    ins = nc.vector.scalar_tensor_tensor(out=fin[:, t, :], in0=bank[1][:, i * P:(i + 1) * P], scalar=d_sb[:, t:t + 1],
                                                         in1=f_hn[c % 2][:, i, :], op0=ALU.mult, op1=ALU.add)
                    if i < 3:
                        done[0] += 1
                        ins.then_inc(f_dve, 1)
                step(ins)
                statistics(c, fin)

            scaled(0)
            for c in range(NCH):
                if c == 1:
                    invert(1)
                pre(c, 0)
                if c:
                    rows(c - 1)
                cell_out(c, 0)
                pre(c, 1)
                if c + 1 < NCH:
                    scaled(c + 1)
                else:
                    variance(0, T - 4)
                cell_out(c, 1)
            normalize(fin, 0, T - 4, f_std, 1, out_ready)
            rows(NCH - 1)
            variance(T - 4, T)
            normalize(fin, T - 4, T, f_std, 2, out_ready)


def kernel(x, adj, L0_gnn_x2, L0_gnn_eps1, L0_gnn_eps2, L0_gnn_W1, L0_gnn_b1, L0_gnn_W2, L0_gnn_b2, L0_gnn_Wm, L0_gnn_bm,
           L1_gnn_gat_W, L1_gnn_gat_a, L1_gnn_edge_Wih, L1_gnn_edge_Whh, L1_gnn_edge_bih, L1_gnn_edge_bhh,
           L1_gnn_node_Wih, L1_gnn_node_Whh, L1_gnn_node_bih, L1_gnn_node_bhh):
    import numpy as np
    from concourse import bacc
    from concourse.bass_utils import run_bass_kernel_spmd

    def gates(w):
        return [w[g * P:(g + 1) * P].T for g in range(3)]
    adj = np.asarray(adj)
    at = adj.T.reshape(T, P, NBLK, BW)
    a_tiles = np.concatenate([np.roll(at[:, :, C], -RB * C, axis=0) for C in range(NBLK)])
    both = np.concatenate([np.asarray(x), np.asarray(L0_gnn_x2)], axis=1).reshape(T, P, 2 * P)
    arrays = dict(
        a_tiles=a_tiles,
        xx=np.concatenate([both, both[:TD - T]]),
        x_nat=np.asarray(x),
        diag=np.diagonal(adj).reshape(T, P).T,
        eps=np.concatenate([L0_gnn_eps1, L0_gnn_eps2]),
        w_t=np.concatenate([L0_gnn_W1, L0_gnn_W2]).transpose(0, 2, 1),
        w_b=np.concatenate([L0_gnn_b1, L0_gnn_b2]).T,
        wm_t=np.asarray(L0_gnn_Wm).T,
        bm=np.asarray(L0_gnn_bm),
        gat_w=np.asarray(L1_gnn_gat_W),
        gat_wt=np.asarray(L1_gnn_gat_W).transpose(0, 2, 1),
        gat_a=np.asarray(L1_gnn_gat_a).reshape(HEADS, 2, P).transpose(2, 0, 1),
        gru_w=np.stack(gates(np.asarray(L1_gnn_edge_Wih)) + gates(np.asarray(L1_gnn_edge_Whh))
                       + gates(np.asarray(L1_gnn_node_Wih)) + gates(np.asarray(L1_gnn_node_Whh))),
        gru_b=np.stack([np.asarray(b)[g * P:(g + 1) * P] for bi, bh in ((L1_gnn_edge_bih, L1_gnn_edge_bhh), (L1_gnn_node_bih, L1_gnn_node_bhh))
                        for b, g in ((bi, 0), (bi, 1), (bi, 2), (bh, 2), (bh, 0), (bh, 1))]).T,
    )
    arrays = {k: np.ascontiguousarray(v) for k, v in arrays.items()}
    nc = bacc.Bacc("TRN2", target_bir_lowering=False, num_devices=1)
    aps = {k: nc.dram_tensor(k, v.shape, F32, kind="ExternalInput").ap() for k, v in arrays.items()}
    out = nc.dram_tensor("out", (N, P), F32, kind="ExternalOutput").ap()
    build(nc, **aps, out=out)
    return run_bass_kernel_spmd(nc, [arrays], core_ids=[0]).results[0]["out"]
```
